# Optimizing a Trainium2 kernel written in Bass

```python
import numpy as np
import jax
import jax.numpy as jnp

def _softmax(x, axis=-1):
    return jax.nn.softmax(x, axis=axis)

def _gelu(x):
    return jax.nn.gelu(x, approximate=True)

def _silu(x):
    return jax.nn.silu(x)

def _sigmoid(x):
    return jax.nn.sigmoid(x)

def _layernorm(x, axis=-1, eps=1e-05):
    m = jnp.mean(x, axis=axis, keepdims=True)
    v = jnp.var(x, axis=axis, keepdims=True)
    return (x - m) / jnp.sqrt(v + eps)

def _scatter_add(tgt, idx, src, axis=0):
    return tgt.at[idx].add(src)

def _segment_sum(src, seg, n):
    return jax.ops.segment_sum(src, seg, n)
kernel_name = 'mk_perceiver_d2_seqx_r4_981722'

def setup_inputs(seed: int=0):
    np.random.seed(seed)
    _w = jnp.asarray

    def _rec_inputs():
        import jax
        import jax.numpy as jnp
        _rk = jax.random.key(seed)
        x = 7.22e-05 + 1 * jax.random.normal(jax.random.fold_in(_rk, 1), (2, 256, 512), jnp.float32)
        _lenS = 256 - jax.random.randint(jax.random.fold_in(_rk, 7), (2,), 0, max(1, 256 // 4) + 1, jnp.int32)
        _lenS2 = 4096 - jax.random.randint(jax.random.fold_in(_rk, 8), (2,), 0, max(1, 4096 // 4) + 1, jnp.int32)
        _ctx_512P = jax.random.normal(jax.random.fold_in(_rk, 11), (2, 16, 128), jnp.float32)
        _ctx_512c = jax.random.dirichlet(jax.random.fold_in(_rk, 511), 0.3 * jnp.ones((16,), jnp.float32), (2, 4096))
        _ctx_512t = jnp.einsum('bsk,bkd->bsd', _ctx_512c, _ctx_512P)
        _ctx_512t = _ctx_512t * jax.lax.rsqrt(jnp.mean(jnp.square(_ctx_512t)) + 1e-12) * 0.953939
        ctx_512 = -0.000514642 + 1.00011 * (_ctx_512t + 0.3 * jax.random.normal(jax.random.fold_in(_rk, 611), (2, 4096, 128), jnp.float32))
        return (x, ctx_512)
    x, ctx_512 = _rec_inputs()

    def _L0_xattn_setup():
        import jax, jax.numpy as jnp
        import numpy as np
        B, S, H, NH, L = (2, 512, 512, 16, 128)
        HD = H // NH
        key = jax.random.key(seed)
        k1, k2, k3, k4, k5 = jax.random.split(key, 5)
        scale = 0.02
        return {'q': jax.random.normal(k1, (B, S, H), dtype=jnp.float32), 'latent_kv': jax.random.normal(k2, (B, S, L), dtype=jnp.float32), 'Wq': jax.random.normal(k3, (H, H), dtype=jnp.float32) * scale, 'Wkv_expand': jax.random.normal(k4, (2 * H, L), dtype=jnp.float32) * scale, 'Wout': jax.random.normal(k5, (H, H), dtype=jnp.float32) * scale}
    _L0_xattn_all = _L0_xattn_setup()
    _L0_xattn_in = {k: v for k, v in _L0_xattn_all.items() if k in ('Wq', 'Wkv_expand', 'Wout')}
    del _L0_xattn_all

    def _L0_attn_setup():
        import jax, jax.numpy as jnp
        import numpy as np
        B, S, D = (2, 1024, 512)
        HK, HV, DK, DV, KCONV = (16, 16, 128, 128, 4)
        KEY_DIM, VALUE_DIM = (HK * DK, HV * DV)
        CONV_DIM = 2 * KEY_DIM + VALUE_DIM
        EPS = 1e-06

        def _l2norm(x):
            return x * jax.lax.rsqrt(jnp.sum(x * x, axis=-1, keepdims=True) + EPS)
        key = jax.random.key(seed)
        ks = jax.random.split(key, 10)

        def lin(k, fan_in, fan_out):
            return jax.random.normal(k, (fan_in, fan_out), jnp.float32) * fan_in ** (-0.5)
        return {'hidden_states': jax.random.normal(ks[0], (B, S, D), jnp.float32), 'W_qkv': lin(ks[1], D, CONV_DIM), 'W_z': lin(ks[2], D, VALUE_DIM), 'W_b': lin(ks[3], D, HV), 'W_a': lin(ks[4], D, HV), 'conv_w': jax.random.normal(ks[5], (CONV_DIM, 1, KCONV), jnp.float32) * KCONV ** (-0.5), 'A_log': jnp.log(jax.random.uniform(ks[6], (HV,), jnp.float32, 0.001, 16.0)), 'dt_bias': jnp.ones((HV,), jnp.float32), 'norm_w': jnp.ones((DV,), jnp.float32), 'W_out': lin(ks[7], VALUE_DIM, D)}
    _L0_attn_all = _L0_attn_setup()
    _L0_attn_in = {k: v for k, v in _L0_attn_all.items() if k in ('W_qkv', 'W_z', 'W_b', 'W_a', 'conv_w', 'A_log', 'dt_bias', 'norm_w', 'W_out')}
    del _L0_attn_all

    def _L0_ffn_setup():
        import jax, jax.numpy as jnp
        import numpy as np
        B, S, H = (2, 256, 512)
        E, K, F = (64, 8, 192)
        CAP = 128
        key = jax.random.key(seed)
        k1, k2, k3, k4, k5 = jax.random.split(key, 5)
        scale_h = 1.0 / np.sqrt(H)
        scale_f = 1.0 / np.sqrt(F)
        return {'hidden_states': jax.random.normal(k1, (B, S, H), jnp.float32), 'router_w': jax.random.normal(k2, (E, H), jnp.float32) * scale_h, 'w_gate': jax.random.normal(k3, (E, H, F), jnp.float32) * scale_h, 'w_up': jax.random.normal(k4, (E, H, F), jnp.float32) * scale_h, 'w_down': jax.random.normal(k5, (E, F, H), jnp.float32) * scale_f}
    _L0_ffn_all = _L0_ffn_setup()
    _L0_ffn_in = {k: v for k, v in _L0_ffn_all.items() if k in ('router_w', 'w_gate', 'w_up', 'w_down')}
    del _L0_ffn_all

    def _L1_xattn_setup():
        import jax, jax.numpy as jnp
        import numpy as np
        B, S, L = (2, 256, 256)
        DIM_Q, H, K, D_C, D_CQ, R = (512, 16, 128, 128, 384, 64)

        def _rope_tables(length, dim):
            inv = 1.0 / 10000.0 ** (jnp.arange(0, dim, 2, dtype=jnp.float32) / dim)
            f = jnp.arange(length, dtype=jnp.float32)[:, None] * inv[None, :]
            sin = jnp.repeat(jnp.sin(f), 2, axis=-1)
            cos = jnp.repeat(jnp.cos(f), 2, axis=-1)
            return (sin, cos)

        def _rotate_half(x):
            half = x.shape[-1] // 2
            return jnp.concatenate([-x[..., half:], x[..., :half]], axis=-1)

        def _apply_rope(x, sin, cos):
            return x * cos + _rotate_half(x) * sin
        key = jax.random.key(seed)
        ks = jax.random.split(key, 8)
        return {'hidden_q': jax.random.normal(ks[0], (B, S, DIM_Q), jnp.float32), 'kv_c': jax.random.normal(ks[1], (B, L, D_C), jnp.float32), 'Wq': jax.random.normal(ks[2], (H * K, DIM_Q), jnp.float32) / np.sqrt(DIM_Q).astype(np.float32), 'w_kc_q': jax.random.normal(ks[3], (H, K, D_CQ), jnp.float32) / np.sqrt(K).astype(np.float32), 'w_kc_kv': jax.random.normal(ks[4], (H, K, D_C), jnp.float32) / np.sqrt(K).astype(np.float32), 'W_qr': jax.random.normal(ks[5], (H, D_CQ, R), jnp.float32) / np.float32(np.sqrt(D_CQ) * np.sqrt(R)), 'W_kr': jax.random.normal(ks[6], (H, D_C, R), jnp.float32) / np.sqrt(D_C).astype(np.float32), 'Wo': jax.random.normal(ks[7], (DIM_Q, H * K), jnp.float32) / np.sqrt(H * K).astype(np.float32)}
    _L1_xattn_all = _L1_xattn_setup()
    _L1_xattn_in = {k: v for k, v in _L1_xattn_all.items() if k in ('Wq', 'w_kc_q', 'w_kc_kv', 'W_qr', 'W_kr', 'Wo')}
    del _L1_xattn_all

    def _L1_attn_setup():
        import jax, jax.numpy as jnp
        import numpy as np
        import math
        HIDDEN = 512
        NUM_HEADS = 16
        HEAD_SIZE = HIDDEN // NUM_HEADS
        BATCH = 2
        SEQ = 512
        key = jax.random.key(seed)
        k_x, k_wq, k_bq, k_wo, k_bo = jax.random.split(key, 5)
        scale_in = 1.0 / math.sqrt(HIDDEN)
        return {'x': jax.random.normal(k_x, (BATCH, SEQ, HIDDEN), dtype=jnp.float32), 'Wqkv': jax.random.normal(k_wq, (HIDDEN, 3 * HIDDEN), dtype=jnp.float32) * scale_in, 'bqkv': jax.random.normal(k_bq, (3 * HIDDEN,), dtype=jnp.float32) * 0.01, 'Wo': jax.random.normal(k_wo, (HIDDEN, HIDDEN), dtype=jnp.float32) * scale_in, 'bo': jax.random.normal(k_bo, (HIDDEN,), dtype=jnp.float32) * 0.01}
    _L1_attn_all = _L1_attn_setup()
    _L1_attn_in = {k: v for k, v in _L1_attn_all.items() if k in ('Wqkv', 'bqkv', 'Wo', 'bo')}
    del _L1_attn_all

    def _L1_ffn_setup():
        import jax, jax.numpy as jnp
        import numpy as np
        EPS_NORM = 1e-06
        EPS_Q = 1e-08
        QB = 127.0

        def _ternary_quantize(w):
            scale = jnp.maximum(jnp.mean(jnp.abs(w)), EPS_Q)
            w_q = jnp.clip(jnp.round(w / scale), -1.0, 1.0)
            return (w_q, scale)

        def _activation_quant(x):
            gamma = jnp.maximum(jnp.max(jnp.abs(x), axis=-1, keepdims=True), EPS_Q)
            x_q = jnp.clip(jnp.round(x * QB / gamma), -QB, QB)
            return (x_q, gamma / QB)

        def _rmsnorm(x, weight):
            out = x * jax.lax.rsqrt(jnp.mean(x * x, axis=-1, keepdims=True) + EPS_NORM)
            return out * weight
        key = jax.random.key(seed)
        dim, expansion = (512, 4)
        hidden = dim * expansion
        B, S = (4, 1024)
        k1, k2, k3 = jax.random.split(key, 3)
        x = jax.random.normal(k1, (B, S, dim), dtype=jnp.float32)
        weight_up = jax.random.normal(k2, (hidden, dim), dtype=jnp.float32) * 0.02
        weight_down = jax.random.normal(k3, (dim, hidden), dtype=jnp.float32) * 0.02
        norm_weight = jnp.ones((dim,), dtype=jnp.float32)
        gamma = jnp.full((dim,), 1e-05, dtype=jnp.float32)
        return {'x': x, 'weight_up': weight_up, 'weight_down': weight_down, 'norm_weight': norm_weight, 'gamma': gamma}
    _L1_ffn_all = _L1_ffn_setup()
    _L1_ffn_in = {k: v for k, v in _L1_ffn_all.items() if k in ('weight_up', 'weight_down', 'norm_weight', 'gamma')}
    del _L1_ffn_all
    return {'x': x, 'ctx_512': ctx_512, 'L0_xattn_Wq': _L0_xattn_in['Wq'], 'L0_xattn_Wkv_expand': _L0_xattn_in['Wkv_expand'], 'L0_xattn_Wout': _L0_xattn_in['Wout'], 'L0_attn_W_qkv': _L0_attn_in['W_qkv'], 'L0_attn_W_z': _L0_attn_in['W_z'], 'L0_attn_W_b': _L0_attn_in['W_b'], 'L0_attn_W_a': _L0_attn_in['W_a'], 'L0_attn_conv_w': _L0_attn_in['conv_w'], 'L0_attn_A_log': _L0_attn_in['A_log'], 'L0_attn_dt_bias': _L0_attn_in['dt_bias'], 'L0_attn_norm_w': _L0_attn_in['norm_w'], 'L0_attn_W_out': _L0_attn_in['W_out'], 'L0_ffn_router_w': _L0_ffn_in['router_w'], 'L0_ffn_w_gate': _L0_ffn_in['w_gate'], 'L0_ffn_w_up': _L0_ffn_in['w_up'], 'L0_ffn_w_down': _L0_ffn_in['w_down'], 'L1_xattn_Wq': _L1_xattn_in['Wq'], 'L1_xattn_w_kc_q': _L1_xattn_in['w_kc_q'], 'L1_xattn_w_kc_kv': _L1_xattn_in['w_kc_kv'], 'L1_xattn_W_qr': _L1_xattn_in['W_qr'], 'L1_xattn_W_kr': _L1_xattn_in['W_kr'], 'L1_xattn_Wo': _L1_xattn_in['Wo'], 'L1_attn_Wqkv': _L1_attn_in['Wqkv'], 'L1_attn_bqkv': _L1_attn_in['bqkv'], 'L1_attn_Wo': _L1_attn_in['Wo'], 'L1_attn_bo': _L1_attn_in['bo'], 'L1_ffn_weight_up': _L1_ffn_in['weight_up'], 'L1_ffn_weight_down': _L1_ffn_in['weight_down'], 'L1_ffn_norm_weight': _L1_ffn_in['norm_weight'], 'L1_ffn_gamma': _L1_ffn_in['gamma']}

def reference(x, ctx_512, L0_xattn_Wq, L0_xattn_Wkv_expand, L0_xattn_Wout, L0_attn_W_qkv, L0_attn_W_z, L0_attn_W_b, L0_attn_W_a, L0_attn_conv_w, L0_attn_A_log, L0_attn_dt_bias, L0_attn_norm_w, L0_attn_W_out, L0_ffn_router_w, L0_ffn_w_gate, L0_ffn_w_up, L0_ffn_w_down, L1_xattn_Wq, L1_xattn_w_kc_q, L1_xattn_w_kc_kv, L1_xattn_W_qr, L1_xattn_W_kr, L1_xattn_Wo, L1_attn_Wqkv, L1_attn_bqkv, L1_attn_Wo, L1_attn_bo, L1_ffn_weight_up, L1_ffn_weight_down, L1_ffn_norm_weight, L1_ffn_gamma):
    import jax
    import jax.numpy as jnp

    def _L0_xattn_ref(q, latent_kv, Wq, Wkv_expand, Wout):
        import jax, jax.numpy as jnp
        import numpy as np
        B, S, H, NH, L = (2, 512, 512, 16, 128)
        HD = H // NH
        b, sq, _ = q.shape
        sk = latent_kv.shape[1]
        qp = q @ Wq.T
        kv = latent_kv @ Wkv_expand.T
        k, v = jnp.split(kv, 2, axis=-1)
        qh = qp.reshape(b, sq, NH, HD).transpose(0, 2, 1, 3)
        kh = k.reshape(b, sk, NH, HD).transpose(0, 2, 1, 3)
        vh = v.reshape(b, sk, NH, HD).transpose(0, 2, 1, 3)
        inv_sqrt_d = 1.0 / jnp.sqrt(jnp.float32(HD))
        scores = jnp.einsum('bhqd,bhkd->bhqk', qh, kh) * inv_sqrt_d
        causal = jnp.tril(jnp.ones((sq, sk), dtype=bool))
        scores = jnp.where(causal, scores, jnp.finfo(scores.dtype).min)
        attn = jax.nn.softmax(scores, axis=-1)
        out = jnp.einsum('bhqk,bhkd->bhqd', attn, vh)
        out = out.transpose(0, 2, 1, 3).reshape(b, sq, H)
        return out @ Wout.T

    def _L0_attn_ref(hidden_states, W_qkv, W_z, W_b, W_a, conv_w, A_log, dt_bias, norm_w, W_out):
        import jax, jax.numpy as jnp
        import numpy as np
        B, S, D = (2, 1024, 512)
        HK, HV, DK, DV, KCONV = (16, 16, 128, 128, 4)
        KEY_DIM, VALUE_DIM = (HK * DK, HV * DV)
        CONV_DIM = 2 * KEY_DIM + VALUE_DIM
        EPS = 1e-06

        def _l2norm(x):
            return x * jax.lax.rsqrt(jnp.sum(x * x, axis=-1, keepdims=True) + EPS)
        b, s, _ = hidden_states.shape
        mixed = hidden_states @ W_qkv
        z = (hidden_states @ W_z).reshape(b, s, HV, DV)
        beta = jax.nn.sigmoid(hidden_states @ W_b)
        g = -jnp.exp(A_log) * jax.nn.softplus(hidden_states @ W_a + dt_bias)
        x = mixed.transpose(0, 2, 1)
        x = jnp.pad(x, ((0, 0), (0, 0), (KCONV - 1, 0)))
        x = jax.lax.conv_general_dilated(x, conv_w, window_strides=(1,), padding='VALID', feature_group_count=CONV_DIM, dimension_numbers=('NCH', 'OIH', 'NCH'))
        qkv = jax.nn.silu(x).transpose(0, 2, 1)
        q = _l2norm(qkv[..., :KEY_DIM].reshape(b, s, HK, DK)) * DK ** (-0.5)
        k = _l2norm(qkv[..., KEY_DIM:2 * KEY_DIM].reshape(b, s, HK, DK))
        v = qkv[..., 2 * KEY_DIM:].reshape(b, s, HV, DV)

        def step(St, inp):
            qt, kt, vt, bt, gt = inp
            St = St * jnp.exp(gt)[..., None, None]
            pred = jnp.einsum('bhk,bhkv->bhv', kt, St)
            delta = (vt - pred) * bt[..., None]
            St = St + jnp.einsum('bhk,bhv->bhkv', kt, delta)
            ot = jnp.einsum('bhk,bhkv->bhv', qt, St)
            return (St, ot)
        S0 = jnp.zeros((b, HV, DK, DV), hidden_states.dtype)
        xs = (q.transpose(1, 0, 2, 3), k.transpose(1, 0, 2, 3), v.transpose(1, 0, 2, 3), beta.transpose(1, 0, 2), g.transpose(1, 0, 2))
        _, ys = jax.lax.scan(step, S0, xs)
        core = ys.transpose(1, 0, 2, 3)
        core = core * jax.lax.rsqrt(jnp.mean(core * core, axis=-1, keepdims=True) + EPS)
        core = core * norm_w * jax.nn.silu(z)
        return core.reshape(b, s, VALUE_DIM) @ W_out

    def _L0_ffn_ref(hidden_states, router_w, w_gate, w_up, w_down):
        import jax, jax.numpy as jnp
        import numpy as np
        B, S, H = (2, 256, 512)
        E, K, F = (64, 8, 192)
        CAP = 128
        b, s, h = hidden_states.shape
        T = b * s
        xf = hidden_states.reshape(T, h)
        logits = xf @ router_w.T
        scores = jax.nn.softmax(logits.astype(jnp.float32), axis=-1)
        topk_w, topk_idx = jax.lax.top_k(scores, K)
        topk_w = topk_w / (topk_w.sum(axis=-1, keepdims=True) + 1e-20)
        slot_expert = topk_idx.reshape(-1)
        slot_token = jnp.repeat(jnp.arange(T), K)
        onehot = jax.nn.one_hot(slot_expert, E, dtype=jnp.int32)
        pos = (jnp.cumsum(onehot, axis=0) * onehot).sum(-1) - 1
        valid = pos < CAP
        dest = jnp.where(valid, slot_expert * CAP + pos, E * CAP)
        buf = jnp.zeros((E * CAP + 1, h), xf.dtype).at[dest].set(xf[slot_token])
        xb = buf[:E * CAP].reshape(E, CAP, h)
        gate = jnp.einsum('ech,ehf->ecf', xb, w_gate)
        up = jnp.einsum('ech,ehf->ecf', xb, w_up)
        hmid = jax.nn.silu(gate) * up
        yb = jnp.einsum('ecf,efh->ech', hmid, w_down).reshape(E * CAP, h)
        yb = jnp.concatenate([yb, jnp.zeros((1, h), yb.dtype)], axis=0)
        slot_out = yb[dest] * topk_w.reshape(-1)[:, None].astype(yb.dtype)
        out = jnp.zeros((T, h), yb.dtype).at[slot_token].add(slot_out)
        return out.reshape(b, s, h)

    def _L1_xattn_ref(hidden_q, kv_c, Wq, w_kc_q, w_kc_kv, W_qr, W_kr, Wo):
        import jax, jax.numpy as jnp
        import numpy as np
        B, S, L = (2, 256, 256)
        DIM_Q, H, K, D_C, D_CQ, R = (512, 16, 128, 128, 384, 64)

        def _rope_tables(length, dim):
            inv = 1.0 / 10000.0 ** (jnp.arange(0, dim, 2, dtype=jnp.float32) / dim)
            f = jnp.arange(length, dtype=jnp.float32)[:, None] * inv[None, :]
            sin = jnp.repeat(jnp.sin(f), 2, axis=-1)
            cos = jnp.repeat(jnp.cos(f), 2, axis=-1)
            return (sin, cos)

        def _rotate_half(x):
            half = x.shape[-1] // 2
            return jnp.concatenate([-x[..., half:], x[..., :half]], axis=-1)

        def _apply_rope(x, sin, cos):
            return x * cos + _rotate_half(x) * sin
        Bv, Sv, _ = hidden_q.shape
        _, Lv, _ = kv_c.shape
        q_hk = (hidden_q @ Wq.T).reshape(Bv, Sv, H, K)
        q_big = jnp.einsum('bshk,hkq->bshq', q_hk, w_kc_q)
        sin_q, cos_q = _rope_tables(Sv, D_CQ)
        q_big = _apply_rope(q_big, sin_q[None, :, None, :], cos_q[None, :, None, :])
        sin_k, cos_k = _rope_tables(Lv, D_C)
        kv_r = _apply_rope(kv_c, sin_k[None], cos_k[None])
        q_r = jnp.einsum('bshq,hqr->bhsr', q_big, W_qr)
        k_r = jnp.einsum('bld,hdr->bhlr', kv_r, W_kr)
        scores = jnp.einsum('bhsr,bhlr->bhsl', q_r, k_r)
        attn = jax.nn.softmax(scores, axis=-1)
        ctx_c = jnp.einsum('bhsl,bld->bhsd', attn, kv_r)
        ctx_lat = jnp.einsum('bhsd,hkd->bhsk', ctx_c, w_kc_kv)
        ctx = ctx_lat.transpose(0, 2, 1, 3).reshape(Bv, Sv, H * K)
        return ctx @ Wo.T

    def _L1_attn_ref(x, Wqkv, bqkv, Wo, bo):
        import jax, jax.numpy as jnp
        import numpy as np
        import math
        HIDDEN = 512
        NUM_HEADS = 16
        HEAD_SIZE = HIDDEN // NUM_HEADS
        BATCH = 2
        SEQ = 512
        b, s, _ = x.shape
        kqv = x @ Wqkv + bqkv
        kqv = kqv.reshape(b, s, 3, NUM_HEADS, HEAD_SIZE)
        q = kqv[:, :, 0]
        k = kqv[:, :, 1]
        v = kqv[:, :, 2]
        scores = jnp.einsum('bsnh,btnh->bnst', k, q) / math.sqrt(HEAD_SIZE)
        ones = jnp.ones_like(scores)
        scores = jnp.triu(scores) + -10000.0 * jnp.tril(ones, k=-1)
        attn = jax.nn.softmax(scores, axis=2)
        out = jnp.einsum('bnkq,bknh->bqnh', attn, v)
        out = out.reshape(b, s, NUM_HEADS * HEAD_SIZE)
        return out @ Wo + bo

    def _L1_ffn_ref(x, weight_up, weight_down, norm_weight, gamma):
        import jax, jax.numpy as jnp
        import numpy as np
        EPS_NORM = 1e-06
        EPS_Q = 1e-08
        QB = 127.0

        def _ternary_quantize(w):
            scale = jnp.maximum(jnp.mean(jnp.abs(w)), EPS_Q)
            w_q = jnp.clip(jnp.round(w / scale), -1.0, 1.0)
            return (w_q, scale)

        def _activation_quant(x):
            gamma = jnp.maximum(jnp.max(jnp.abs(x), axis=-1, keepdims=True), EPS_Q)
            x_q = jnp.clip(jnp.round(x * QB / gamma), -QB, QB)
            return (x_q, gamma / QB)

        def _rmsnorm(x, weight):
            out = x * jax.lax.rsqrt(jnp.mean(x * x, axis=-1, keepdims=True) + EPS_NORM)
            return out * weight
        residual = x
        xn = _rmsnorm(x, norm_weight)
        w_up_q, s_up = _ternary_quantize(weight_up)
        w_down_q, s_down = _ternary_quantize(weight_down)
        x_q, s_x = _activation_quant(xn)
        h = jnp.einsum('bsd,hd->bsh', x_q * s_x, w_up_q * s_up)
        h = jax.nn.silu(h)
        out = jnp.einsum('bsh,dh->bsd', h, w_down_q * s_down)
        return residual + out * gamma
    x = x + _L0_xattn_ref(_layernorm(x, axis=-1), ctx_512, L0_xattn_Wq, L0_xattn_Wkv_expand, L0_xattn_Wout)
    x = x + _L0_attn_ref(_layernorm(x, axis=-1), L0_attn_W_qkv, L0_attn_W_z, L0_attn_W_b, L0_attn_W_a, L0_attn_conv_w, L0_attn_A_log, L0_attn_dt_bias, L0_attn_norm_w, L0_attn_W_out)
    x = x + _L0_ffn_ref(_layernorm(x, axis=-1), L0_ffn_router_w, L0_ffn_w_gate, L0_ffn_w_up, L0_ffn_w_down)
    x = x + _L1_xattn_ref(_layernorm(x, axis=-1), ctx_512, L1_xattn_Wq, L1_xattn_w_kc_q, L1_xattn_w_kc_kv, L1_xattn_W_qr, L1_xattn_W_kr, L1_xattn_Wo)
    x = x + _L1_attn_ref(_layernorm(x, axis=-1), L1_attn_Wqkv, L1_attn_bqkv, L1_attn_Wo, L1_attn_bo)
    x = x + _L1_ffn_ref(_layernorm(x, axis=-1), L1_ffn_weight_up, L1_ffn_weight_down, L1_ffn_norm_weight, L1_ffn_gamma)
    return x

_drawn_inputs = setup_inputs


def setup_inputs(seed=0):
    import zlib

    import numpy as np

    out = dict(_drawn_inputs(seed))
    spreads = {'L0_attn_dt_bias': (1.0, 0.6),
     'L0_attn_norm_w': (1.0, 0.2),
     'L1_ffn_norm_weight': (1.0, 0.6),
     'L1_ffn_gamma': (9.999999747378752e-06, 0.6)}
    factors = {'L0_xattn_Wq': 6.28,
     'L1_attn_bqkv': 6.895,
     'L1_attn_bo': 7.055,
     'L1_ffn_weight_up': 200.0,
     'L1_ffn_weight_down': 200.0}
    for name, (base, spread) in spreads.items():
        noise = np.random.default_rng([zlib.crc32(name.encode()), seed]).standard_normal(out[name].shape)
        drawn = base * np.exp(spread * noise) if base else spread * noise
        out[name] = jnp.asarray(drawn.astype(out[name].dtype))
    for name, factor in factors.items():
        out[name] = (out[name] * factor).astype(out[name].dtype)
    return out
```

```python
import numpy as np
import concourse.bass as bass
from concourse import mybir
from contextlib import ExitStack

F32 = mybir.dt.float32
BF16 = mybir.dt.bfloat16
I32 = mybir.dt.int32
U32 = mybir.dt.uint32
ALU = mybir.AluOpType
ACT = mybir.ActivationFunctionType
AX = mybir.AxisListType

P = 128
BATCH, SEQ, D = 2, 256, 512
TOK = BATCH * SEQ
NT = TOK // P
DC = D // P
FMIN = float(np.finfo(np.float32).min)


class Links:

    def __init__(self, eng, sem, base=0):
        self.eng, self.sem, self.base, self.n = eng, sem, base, 0

    def link(self, ins):
        ins.then_inc(self.sem, 1)
        self.n += 1
        self.eng.wait_ge(self.sem, self.base + self.n)


class Mem:

    def __init__(self, nc, ctx, tag):
        self.nc, self.ctx, self.tag = nc, ctx, tag
        self.sems = []
        ctx.callback(self.clear)

    def clear(self):
        if self.sems:
            with self.nc.Block() as block:

                @block.gpsimd
                def _(pool):
                    for s in self.sems:
                        pool.sem_clear(s)

    def sb(self, name, shape, dt=F32):
        return self.ctx.enter_context(self.nc.sbuf_tensor(f"{self.tag}_{name}", shape, dt))

    def sem(self, name):
        s = self.ctx.enter_context(self.nc.semaphore(f"{self.tag}_{name}"))
        self.sems.append(s)
        return s


def constants_stage(nc, g):
    with ExitStack() as ctx:
        m = Mem(nc, ctx, "const")
        made = m.sem("made")
        loaded = m.sem("loaded")
        block = ctx.enter_context(nc.Block())

        @block.sync
        def _(sp):
            sp.dma_start(g.x[:, :, :], g.x_dram.rearrange("(t p) d -> p t d", p=P)).then_inc(loaded, 16)
            sp.wait_ge(loaded, 16)

        @block.gpsimd
        def _(pool):
            pool.memset(g.ident[:, :], 0.0).then_inc(made, 1)
            pool.memset(g.ones[:, :], 1.0).then_inc(made, 1)
            pool.memset(g.triu[:, :], 1.0).then_inc(made, 1)
            pool.memset(g.half[:, :], -0.5).then_inc(made, 1)
            pool.wait_ge(made, 4)
            pool.affine_select(out=g.ident[:, :], in_=g.ident[:, :], compare_op=ALU.not_equal, fill=1.0,
                               base=0, pattern=[[-1, P]], channel_multiplier=1).then_inc(made, 1)
            pool.affine_select(out=g.triu[:, :], in_=g.triu[:, :], compare_op=ALU.is_ge, fill=0.0,
                               base=0, pattern=[[1, P]], channel_multiplier=-1).then_inc(made, 1)
            pool.wait_ge(made, 6)


def norm_stage(nc, g, tag, eps, transpose=True):
    with ExitStack() as ctx:
        m = Mem(nc, ctx, tag)
        stats = m.sb("stats", [P, NT, 6])
        mv = m.sb("mv", [P, NT, 2])
        var = m.sb("var", [P, NT])
        rstd = m.sb("rstd", [P, NT])
        tp = [g.bank[i][:, :].rearrange("p (c n) -> p c n", c=DC) for i in range(2)]
        own = m.sem("own")
        var_ready = m.sem("var_ready")
        rstd_ready = m.sem("rstd_ready")
        xn_ready = m.sem("xn_ready")
        tp_ready = m.sem("tp_ready")
        copied = m.sem("copied")
        block = ctx.enter_context(nc.Block())

        @block.vector
        def _(dve):
            c = Links(dve, own)
            for t in range(NT):
                nc.vector.bn_stats(stats[:, t, :], g.x[:, t, :]).then_inc(own, 1)
            dve.wait_ge(own, NT)
            for t in range(NT):
                nc.vector.bn_aggr(mv[:, t, :], stats[:, t, :]).then_inc(own, 1)
            dve.wait_ge(own, 2 * NT)
            nc.vector.tensor_scalar(var[:, :], mv[:, :, 1], eps, None, ALU.add).then_inc(var_ready, 1)
            dve.wait_ge(rstd_ready, 1)
            for t in range(NT):
                nc.vector.tensor_scalar(g.xn[:, t, :], g.x[:, t, :], mv[:, t, 0:1], rstd[:, t:t + 1],
                                        ALU.subtract, ALU.mult).then_inc(xn_ready, 1)

        @block.gpsimd
        def _(pool):
            pool.wait_ge(var_ready, 1)
            nc.gpsimd.tensor_tensor(rstd[:, :], var[:, :], g.half[:, 0:NT], ALU.pow).then_inc(rstd_ready, 1)

        @block.tensor
        def _(pe):
            for t in range(NT if transpose else 0):
                pe.wait_ge(xn_ready, t + 1)
                if t >= 2:
                    pe.wait_ge(copied, t - 1)
                for c in range(DC):
                    last = nc.tensor.transpose(tp[t % 2][:, c, :], g.xn[:, t, c * P:(c + 1) * P], g.ident[:, :])
                last.then_inc(tp_ready, 1)

        @block.scalar
        def _(act):
            for t in range(NT if transpose else 0):
                act.wait_ge(tp_ready, t + 1)
                nc.scalar.copy(g.xT[:, :, t * P:(t + 1) * P], tp[t % 2][:, :, :]).then_inc(copied, 1)


def attention_stage(nc, g, tag, wq, wk, wv, wo, kvT, kv_dram, bias, masked_score):
    H, HD = 16, 32
    SCALE = HD ** -0.5
    KC = kvT.shape[1]
    UNITS = 8
    KT = SEQ // P
    DEEP = 4
    T_LAG, AV_LAG, OUT_LAG = 2, 3, 4
    with ExitStack() as ctx:
        m = Mem(nc, ctx, tag)
        wq_sb, wo_sb = m.sb("wq", [P, DC, D]), m.sb("wo", [P, DC, D])
        wk_sb, wv_sb = m.sb("wk", [P, KC, D]), m.sb("wv", [P, KC, D])
        qT, kT = m.sb("qT", [P, DC, TOK]), m.sb("kT", [P, DC, TOK])
        v = m.sb("v", [P, NT, D])
        O, OT = m.sb("O", [P, NT, D]), m.sb("OT", [P, DC, TOK])
        qs, ks = m.sb("qs", [P, TOK]), m.sb("ks", [P, TOK])
        keep = m.sb("keep", [P, KT, SEQ])
        fill = m.sb("fill", [P, KT, SEQ])
        E = [m.sb(f"E{i}", [P, KT, SEQ]) for i in range(DEEP)]
        ET = [m.sb(f"ET{i}", [P, KT, KT, P]) for i in range(2)]
        nmax = m.sb("nmax", [P, UNITS, KT])
        total = m.sb("total", [P, UNITS, KT])
        rtotal = m.sb("rtotal", [P, UNITS, KT])
        if bias:
            bq, bk = m.sb("bq", [P, DC]), m.sb("bk", [P, DC])
            bv, bo = m.sb("bv", [P, D]), m.sb("bo", [P, D])
        bank = g.bank
        S = [bank[i][:, :].rearrange("p (t k) -> p t k", t=KT) for i in range(2)]
        ETp = [bank[2 + i][:, :].rearrange("p (k q n) -> p k q n", k=KT, q=KT) for i in range(2)]
        AV = [bank[4 + i][:, 0:KT * HD].rearrange("p (t n) -> p t n", t=KT) for i in range(DEEP)]
        loads = {n: m.sem(f"loaded_{n}") for n in ["kv", "wq", "wk", "wv", "wo", "bias"]}
        masks = m.sem("masks")
        proj, proj_out = m.sem("proj"), m.sem("proj_out")
        staged = m.sem("staged")
        s_ready, s_free = m.sem("s_ready"), m.sem("s_free")
        max_ready, e_ready = m.sem("max_ready"), m.sem("e_ready")
        et_ready, et_copied = m.sem("et_ready"), m.sem("et_copied")
        av_ready, av_out = m.sem("av_ready"), m.sem("av_out")
        filled, inverted = m.sem("filled"), m.sem("inverted")
        ot_ready, ot_copied = m.sem("ot_ready"), m.sem("ot_copied")
        y_ready, y_added = m.sem("y_ready"), m.sem("y_added")
        block = ctx.enter_context(nc.Block())

        @block.sync
        def _(sp):
            if kv_dram is not None:
                for b in range(BATCH):
                    sp.dma_start(kvT[:, 0, b * SEQ:(b + 1) * SEQ], kv_dram[b, :, 0:SEQ]).then_inc(loads["kv"], 16)
            sp.dma_start(wk_sb[:, :, :], wk.rearrange("(c p) n -> p c n", p=P)).then_inc(loads["wk"], 16)
            sp.dma_start(wv_sb[:, :, :], wv.rearrange("(c p) n -> p c n", p=P)).then_inc(loads["wv"], 16)
            sp.dma_start(wq_sb[:, :, :], wq.rearrange("(c p) n -> p c n", p=P)).then_inc(loads["wq"], 16)
            if bias:
                bqkv, bqk_cols, bout = bias
                sp.dma_start(bq[:, :], bqk_cols[:, 0:DC]).then_inc(loads["bias"], 16)
                sp.dma_start(bk[:, :], bqk_cols[:, DC:2 * DC]).then_inc(loads["bias"], 16)
                sp.dma_start(bv[:, :], bqkv[2 * D:3 * D].partition_broadcast(P)).then_inc(loads["bias"], 16)
                sp.dma_start(bo[:, :], bout.partition_broadcast(P)).then_inc(loads["bias"], 16)
            sp.dma_start(wo_sb[:, :, :], wo.rearrange("(c p) n -> p c n", p=P)).then_inc(loads["wo"], 16)
            for s in loads.values():
                if s is loads["kv"]:
                    if kv_dram is not None:
                        sp.wait_ge(s, 16 * BATCH)
                elif s is loads["bias"]:
                    if bias:
                        sp.wait_ge(s, 64)
                else:
                    sp.wait_ge(s, 16)

        @block.gpsimd
        def _(pool):
            pool.memset(keep[:, :, :], 1.0).then_inc(masks, 1)
            pool.memset(fill[:, :, :], 0.0).then_inc(masks, 1)
            pool.wait_ge(masks, 2)
            for buf, value in ((keep, 0.0), (fill, masked_score)):
                pool.affine_select(out=buf[:, :, :], in_=buf[:, :, :], compare_op=ALU.is_ge, fill=value, base=0,
                                   pattern=[[P, KT], [-1, SEQ]], channel_multiplier=1).then_inc(masks, 1)

        @block.tensor
        def _(pe):
            n = 0

            def bank_free():
                if n >= 4:
                    pe.wait_ge(proj_out, n - 3)

            if kv_dram is not None:
                pe.wait_ge(loads["kv"], 16 * BATCH)
            pe.wait_ge(loads["wk"], 16)
            for o in range(DC):
                bank_free()
                for c in range(KC):
                    last = nc.tensor.matmul(bank[n % 4][:, :], wk_sb[:, c, o * P:(o + 1) * P], kvT[:, c, :],
                                            start=(c == 0), stop=(c == KC - 1))
                last.then_inc(proj, 1)
                n += 1
            pe.wait_ge(loads["wv"], 16)
            for t in range(NT):
                bank_free()
                for c in range(KC):
                    last = nc.tensor.matmul(bank[n % 4][:, :], kvT[:, c, t * P:(t + 1) * P], wv_sb[:, c, :],
                                            start=(c == 0), stop=(c == KC - 1))
                last.then_inc(proj, 1)
                n += 1
            pe.wait_ge(loads["wq"], 16)
            for o in range(DC):
                bank_free()
                for c in range(DC):
                    last = nc.tensor.matmul(bank[n % 4][:, :], wq_sb[:, c, o * P:(o + 1) * P], g.xT[:, c, :],
                                            start=(c == 0), stop=(c == DC - 1))
                last.then_inc(proj, 1)
                n += 1
            pe.wait_ge(proj_out, n)

            with pe.Fori(0, DC) as i:
                def scores(u):
                    j, b = u // 2, u % 2
                    if u == 0:
                        pe.wait_ge(staged, 2 * i + 2)
                    pe.wait_ge(s_free, UNITS * i + u + 1)
                    r = slice(j * HD, (j + 1) * HD)
                    for t in range(KT):
                        q0 = b * SEQ + t * P
                        last = nc.tensor.matmul(S[u % 2][:, t, :], qs[r, q0:q0 + P], ks[r, b * SEQ:(b + 1) * SEQ],
                                                start=True, stop=True)
                    last.then_inc(s_ready, 1)

                def transposes(u):
                    pe.wait_ge(e_ready, UNITS * i + u + 1)
                    for k in range(KT):
                        for t in range(KT):
                            last = nc.tensor.transpose(ETp[u % 2][:, k, t, :], E[u % DEEP][:, t, k * P:(k + 1) * P],
                                                       g.ident[:, :])
                    last.then_inc(et_ready, 1)

                def weighted(u):
                    j, b = u // 2, u % 2
                    pe.wait_ge(av_out, UNITS * i + u + 1)
                    pe.wait_ge(et_copied, UNITS * i + u + 1)
                    for t in range(KT):
                        for k in range(KT):
                            last = nc.tensor.matmul(AV[u % DEEP][:, t, :], ET[u % 2][:, k, t, :],
                                                    v[:, b * KT + k, bass.ds(i * P + j * HD, HD)],
                                                    start=(k == 0), stop=(k == KT - 1))
                    last.then_inc(av_ready, 1)

                for s in range(UNITS + AV_LAG):
                    if s < UNITS:
                        scores(s)
                    if 0 <= s - T_LAG < UNITS:
                        transposes(s - T_LAG)
                    if s >= AV_LAG:
                        weighted(s - AV_LAG)

            pe.wait_ge(av_out, DC * UNITS + DEEP)
            for t in range(NT):
                if t >= 2:
                    pe.wait_ge(ot_copied, t - 1)
                for c in range(DC):
                    last = nc.tensor.transpose(bank[t % 2][:, c * P:(c + 1) * P], O[:, t, c * P:(c + 1) * P],
                                               g.ident[:, :])
                last.then_inc(ot_ready, 1)
            pe.wait_ge(ot_copied, NT)
            pe.wait_ge(loads["wo"], 16)
            for t in range(NT):
                for c in range(DC):
                    last = nc.tensor.matmul(bank[4 + t][:, :], OT[:, c, t * P:(t + 1) * P], wo_sb[:, c, :],
                                            start=(c == 0), stop=(c == DC - 1))
                last.then_inc(y_ready, 1)

        @block.scalar
        def _(act):
            if bias:
                act.wait_ge(loads["bias"], 64)
            for n in range(3 * DC):
                kind, o = n // DC, n % DC
                act.wait_ge(proj, n + 1)
                if n:
                    act.wait_ge(proj_out, n)
                if kind == 1:
                    if bias:
                        continue
                    nc.scalar.copy(v[:, o, :], bank[n % 4][:, :]).then_inc(proj_out, 1)
                else:
                    dst, b = ((kT, "bk"), None, (qT, "bq"))[kind]
                    if bias:
                        bb = bk if b == "bk" else bq
                        nc.scalar.activation(dst[:, o, :], bank[n % 4][:, :], ACT.Identity,
                                             bias=bb[:, o:o + 1]).then_inc(proj_out, 1)
                    else:
                        nc.scalar.copy(dst[:, o, :], bank[n % 4][:, :]).then_inc(proj_out, 1)
            act.wait_ge(proj_out, 3 * DC)

            with act.Fori(0, DC) as i:
                act.wait_ge(s_free, UNITS * i + 2)
                nc.scalar.copy(qs[:, :], qT[:, :, :].rearrange("p c n -> p (c n)")[:, bass.ds(i * TOK, TOK)])\
                  .then_inc(staged, 1)
                nc.scalar.copy(ks[:, :], kT[:, :, :].rearrange("p c n -> p (c n)")[:, bass.ds(i * TOK, TOK)])\
                  .then_inc(staged, 1)

                def exps(u):
                    act.wait_ge(max_ready, UNITS * i + u + 1)
                    for t in range(KT):
                        e = E[u % DEEP][:, t, :]
                        last = nc.scalar.activation(e, e, ACT.Exp, bias=nmax[:, u, t:t + 1],
                                                    accum_out=total[:, u, t:t + 1])
                    last.then_inc(e_ready, 1)

                def copies(u):
                    act.wait_ge(et_ready, UNITS * i + u + 1)
                    if u >= 2:
                        act.wait_ge(av_ready, UNITS * i + u - 1)
                    nc.scalar.copy(ET[u % 2][:, :, :, :], ETp[u % 2]).then_inc(et_copied, 1)

                for s in range(UNITS + 1):
                    if s < UNITS:
                        exps(s)
                    if s >= 1:
                        copies(s - 1)

            for t in range(NT):
                act.wait_ge(ot_ready, t + 1)
                nc.scalar.copy(OT[:, :, t * P:(t + 1) * P],
                               bank[t % 2][:, :].rearrange("p (c n) -> p c n", c=DC)).then_inc(ot_copied, 1)

        @block.vector
        def _(dve):
            if bias:
                dve.wait_ge(loads["bias"], 64)
                for t in range(NT):
                    n = DC + t
                    dve.wait_ge(proj, n + 1)
                    dve.wait_ge(proj_out, n)
                    nc.vector.tensor_tensor(v[:, t, :], bank[n % 4][:, :], bv[:, :], ALU.add).then_inc(proj_out, 1)
            dve.wait_ge(masks, 4)
            dve.sem_inc(s_free, 2)
            dve.sem_inc(av_out, DEEP)
            with dve.Fori(0, DC) as i:

                def mask_and_max(u):
                    dve.wait_ge(s_ready, UNITS * i + u + 1)
                    if u >= DEEP:
                        dve.wait_ge(et_ready, UNITS * i + u - DEEP + 1)
                    e = E[u % DEEP]
                    nc.vector.scalar_tensor_tensor(out=e[:, :, :], in0=S[u % 2], scalar=SCALE, in1=keep[:, :, :],
                                                   op0=ALU.mult, op1=ALU.mult).then_inc(s_free, 1)
                    dve.wait_ge(s_free, UNITS * i + u + 3)
                    nc.vector.tensor_tensor(e[:, :, :], e[:, :, :], fill[:, :, :], ALU.add).then_inc(filled, 1)
                    dve.wait_ge(filled, UNITS * i + u + 1)
                    nc.vector.tensor_reduce(nmax[:, u, :], e[:, :, :], AX.X, ALU.max, negate=True)\
                      .then_inc(max_ready, 1)

                def normalise(u):
                    j, b = u // 2, u % 2
                    dve.wait_ge(av_ready, UNITS * i + u + 1)
                    nc.vector.reciprocal(rtotal[:, u, :], total[:, u, :]).then_inc(inverted, 1)
                    dve.wait_ge(inverted, UNITS * i + u + 1)
                    for t in range(KT):
                        last = nc.vector.tensor_scalar(O[:, b * KT + t, bass.ds(i * P + j * HD, HD)], AV[u % DEEP][:, t, :],
                                                       rtotal[:, u, t:t + 1], None, ALU.mult)
                    last.then_inc(av_out, 1)

                for s in range(UNITS + OUT_LAG):
                    if s < UNITS:
                        mask_and_max(s)
                    if s >= OUT_LAG:
                        normalise(s - OUT_LAG)
            for t in range(NT):
                dve.wait_ge(y_ready, t + 1)
                nc.vector.tensor_tensor(g.x[:, t, :], g.x[:, t, :], bank[4 + t][:, :], ALU.add).then_inc(y_added, 1)
                if bias:
                    dve.wait_ge(y_added, (t + 1) if not bias else 2 * t + 1)
                    nc.vector.tensor_tensor(g.x[:, t, :], g.x[:, t, :], bo[:, :], ALU.add).then_inc(y_added, 1)


def delta_stage(nc, g, dram):
    H, DK, DV, TAPS = 16, 128, 128, 4
    EPS = 1e-6
    LEVELS = 6
    HALF = P // 2
    BIG = 1e30
    CW, BETA, HBETA, CUM, NCUMX, CREST, NBX, GN, NS = 0, 12, 16, 20, 24, 28, 32, 36, 40
    NG = NT * H
    with ExitStack() as ctx:
        m = Mem(nc, ctx, "dn")
        w = [m.sb(f"w{i}", [P, DC, 4 * P]) for i in range(2)]
        wo = m.sb("wo", [P, H, D])
        scal = m.sb("scal", [P, H, NS])
        hs = [m.sb(f"hs{i}", [P, NS]) for i in range(2)]
        wab = m.sb("wab", [P, DC, 2 * H])
        dtb, alog, expa = m.sb("dtb", [P, H]), m.sb("alog", [P, H]), m.sb("expa", [P, H])
        ab = m.sb("ab", [P, NT, 2 * H])
        th, ga, gb, gneg = (m.sb(n, [P, NT, H]) for n in ("th", "ga", "gb", "gneg"))
        cum, last_cum = m.sb("cum", [P, NT, H]), m.sb("last_cum", [P, NT, H])
        normw = m.sb("normw", [P, DV])
        low = m.sb("low", [P, P])
        up = m.sb("up", [P, P])
        m0 = m.sb("m0", [P, P])
        pairm = m.sb("pairm", [P, LEVELS, HALF])
        yk, yv = m.sb("yk", [P, TOK]), m.sb("yv", [P, TOK])
        tn = [m.sb(f"tn{n}", [P, TOK]) for n in "kqv"]
        sq = [m.sb(f"sq{n}", [P, TOK]) for n in "kq"]
        ss = m.sb("ss", [P, 2, NT])
        zt = m.sb("zt", [P, NT, DV])
        dg = m.sb("dg", [P, NT, P])
        e1, e2 = m.sb("e1", [P, NT, P]), m.sb("e2", [P, NT, P])
        kh = m.sb("kh", [P, NT, DK])

        def two(name, shape):
            return [m.sb(f"{name}{i}", shape) for i in range(2)]

        yq, khT, kej = two("yq", [P, TOK]), two("khT", [P, NT, P]), two("kej", [P, NT, DK])
        bv, zs, rs = two("bv", [P, NT, DV]), two("zs", [P, NT, DV]), two("rs", [P, 2, NT])
        A, PT = two("A", [P, NT, P]), two("PT", [P, NT, P])
        X, Y = two("X", [P, NT, P]), two("Y", [P, NT, P])
        p1 = m.sb("p1", [P, NT, HALF])
        U, R = m.sb("U", [P, NT, DV]), m.sb("R", [P, BATCH, DV])
        St = m.sb("St", [P, BATCH, DV])
        o, osq = m.sb("o", [P, NT, DV]), m.sb("osq", [P, NT, DV])
        oss, rs2, f = m.sb("oss", [P, NT]), m.sb("rs2", [P, NT]), m.sb("f", [P, NT])
        core = m.sb("core", [P, NT, DV])
        coreT = m.sb("coreT", [P, H, NT, P])
        bank = g.bank

        def tiles(b):
            return b[:, :].rearrange("p (t n) -> p t n", t=NT)

        def half_tiles(b):
            return b[:, 0:NT * HALF].rearrange("p (t n) -> p t n", t=NT)

        def cols(p, name):
            return hs[p][:, name:name + NT].unsqueeze(2).broadcast_to((P, NT, P))

        loaded, wo_loaded = m.sem("loaded"), m.sem("wo_loaded")
        own, pool_own = m.sem("own"), m.sem("pool_own")
        w_loaded = [m.sem(f"w_loaded{i}") for i in range(2)]
        front_own, norm_own = m.sem("front_own"), m.sem("norm_own")
        names = """ab ab_out ab_exp ab_tanh g_exp g_ln gneg cums cums_out cum_exp scal_ready nw_ready
            hs_ready k_ps k_conv k_tanh k_silu k_square q_ps q_conv q_tanh q_silu q_square v_ps v_conv v_tanh v_silu
            z_ps z_tanh z_mul zs_ready dg_ready gb_ps e1_arg e2_arg e1_ready e2_ready ktok kh_ready
            sums ss_ready rs_ready vtok bv_ready khT_ps khT_ready kej_ready kk kq a_ready a_pairs x1 pt_ready
            y1_ps y1_ready p1_ps p1_ready yp_ps y_ready xt_ps x_ready u0_ps u0_ready s_ps s_ready
            ks_ps qs_ps r_ready u1_ps u1_ready o_ps o_copied o_ready f_arg f_pow f_ready core_ready
            coreT_ps coreT_ready out_ps out_added""".split()
        S = {n: m.sem(n) for n in names}

        def wait(eng, name, h, k=1, per=1):
            v = per * h + k
            if not isinstance(v, int) or v > 0:
                eng.wait_ge(S[name], v)

        block = ctx.enter_context(nc.Block())

        def w_heads(h):
            return dram["L0_attn_W_heads"][bass.ds(h * D, D), :].rearrange("(c p) n -> p c n", p=P)

        def pipeline(eng, turn):
            turn(0, None, None, 0)
            turn(1, 0, None, 1)
            with eng.Fori(1, H // 2) as pair:
                turn(2 * pair, 2 * pair - 1, 2 * pair - 2, 0)
                turn(2 * pair + 1, 2 * pair, 2 * pair - 1, 1)
            turn(None, H - 1, H - 2, 0)
            turn(None, None, H - 1, 1)

        @block.sync
        def _(sp):
            sp.dma_start(wab[:, :, :], dram["L0_attn_W_ab"].rearrange("(c p) n -> p c n", p=P)).then_inc(loaded, 16)
            sp.dma_start(dtb[:, :], dram["L0_attn_dt_bias"].partition_broadcast(P)).then_inc(loaded, 16)
            sp.dma_start(alog[:, :], dram["L0_attn_A_log"].partition_broadcast(P)).then_inc(loaded, 16)
            sp.dma_start(normw[:, :], dram["L0_attn_norm_w"].partition_broadcast(P)).then_inc(loaded, 16)
            sp.dma_start(scal[:, :, CW:CW + 3 * TAPS], dram["L0_attn_conv"].rearrange("p (h n) -> p h n", h=H))\
              .then_inc(loaded, 16)
            sp.wait_ge(loaded, 80)
            for h in range(2):
                sp.dma_start(w[h][:, :, :], w_heads(h)).then_inc(w_loaded[h], 16)
            sp.dma_start(wo[:, :, :], dram["L0_attn_W_out"].rearrange("(h p) n -> p h n", p=P)).then_inc(wo_loaded, 16)
            with sp.Fori(1, H // 2) as pair:
                for p in range(2):
                    sp.wait_ge(S["z_ps"], 2 * pair + (p - 1))
                    sp.dma_start(w[p][:, :, :], w_heads(2 * pair + p)).then_inc(w_loaded[p], 16)
            sp.wait_ge(wo_loaded, 16)

        @block.gpsimd
        def _(pool):
            n = 0
            for buf, v in ((low[:, :], 0.0), (up[:, :], 0.0), (m0[:, :], 0.0), (pairm[:, :, :], 0.0)):
                pool.memset(buf, v).then_inc(pool_own, 1)
                n += 1
            pool.wait_ge(pool_own, n)
            pool.affine_select(out=low[:, :], in_=low[:, :], compare_op=ALU.is_ge, fill=-BIG, base=0,
                               pattern=[[-1, P]], channel_multiplier=1).then_inc(pool_own, 1)
            pool.affine_select(out=up[:, :], in_=up[:, :], compare_op=ALU.is_ge, fill=BIG, base=0,
                               pattern=[[1, P]], channel_multiplier=-1).then_inc(pool_own, 1)
            mm = m0[:, :].rearrange("p (a two) -> p a two", two=2)[:, :, 0]
            pool.affine_select(out=mm, in_=mm, compare_op=ALU.not_equal, fill=1.0, base=-1,
                               pattern=[[-2, HALF]], channel_multiplier=1).then_inc(pool_own, 1)
            n += 3
            pool.wait_ge(pool_own, n)
            for l in range(LEVELS):
                s = 2 ** (l + 1)
                part = pairm[:, l, :].rearrange("p (q c) -> p q c", c=s)
                pool.memset(part, 1.0).then_inc(pool_own, 1)
                n += 1
                pool.wait_ge(pool_own, n)
                pool.affine_select(out=part, in_=part, compare_op=ALU.is_ge, fill=0.0, base=0,
                                   pattern=[[-2 * s, HALF // s], [0, s]], channel_multiplier=1).then_inc(pool_own, 1)
                n += 1
                pool.wait_ge(pool_own, n)
                pool.affine_select(out=part, in_=part, compare_op=ALU.is_ge, fill=0.0, base=s - 1,
                                   pattern=[[2 * s, HALF // s], [0, s]], channel_multiplier=-1).then_inc(pool_own, 1)
                n += 1
                pool.wait_ge(pool_own, n)

            def turn(front, middle, norm, p):
                if front is not None:
                    wait(pool, "hs_ready", front)
                    wait(pool, "gb_ps", front - 1)
                    nc.gpsimd.tensor_tensor(dg[:, :, :], g.triu[:, :].unsqueeze(1).broadcast_to((P, NT, P)),
                                            cols(p, GN), ALU.mult).then_inc(S["dg_ready"], 1)
                if norm is not None:
                    wait(pool, "f_arg", norm)
                    nc.gpsimd.tensor_tensor(f[:, :], oss[:, :], g.half[:, 0:NT], ALU.pow).then_inc(S["f_pow"], 1)
                if front is not None:
                    wait(pool, "ss_ready", front)
                    wait(pool, "core_ready", front - 2)
                    nc.gpsimd.tensor_tensor(rs[p][:, :, :], ss[:, :, :],
                                            g.half[:, 0:2 * NT].rearrange("p (a b) -> p a b", a=2),
                                            ALU.pow).then_inc(S["rs_ready"], 1)
                    wait(pool, "kh_ready", front)
                    wait(pool, "s_ps", front - 2)
                    nc.gpsimd.tensor_tensor(kej[p][:, :, :], kh[:, :, :], cols(p, CREST), ALU.mult)\
                      .then_inc(S["kej_ready"], 1)

            pipeline(pool, turn)

        @block.tensor
        def _(pe):
            pe.wait_ge(loaded, 80)
            for t in range(NT):
                for c in range(DC):
                    last = nc.tensor.matmul(bank[0][:, t * 2 * H:(t + 1) * 2 * H], g.xT[:, c, t * P:(t + 1) * P],
                                            wab[:, c, :], start=(c == 0), stop=(c == DC - 1))
            last.then_inc(S["ab"], 1)
            pe.wait_ge(S["gneg"], 1)
            gn = gneg[:, :, :].rearrange("p t h -> p (t h)")
            nc.tensor.matmul(bank[1][:, 0:NG], g.triu[:, :], gn, start=True, stop=True)
            nc.tensor.matmul(bank[2][:, 0:NG], g.ones[:, :], gn, start=True, stop=True).then_inc(S["cums"], 1)
            mm, tr = nc.tensor.matmul, nc.tensor.transpose

            def turn(front, middle, norm, p):
                q = 1 - p

                def project(kind, bk, chunks):
                    if front is None:
                        return
                    for c in chunks:
                        last = mm(bank[bk][:, :], w[p][:, c, kind * P:(kind + 1) * P], g.xT[:, c, :],
                                  start=(c == 0), stop=(c == DC - 1))
                    if chunks[-1] == DC - 1:
                        last.then_inc(S[("q_ps", "k_ps", "v_ps")[kind]], 1)

                def project_z(t):
                    if front is None:
                        return
                    if t == 0:
                        wait(pe, "q_conv", front)
                    for c in range(DC):
                        last = mm(bank[0][:, t * P:(t + 1) * P], g.xT[:, c, t * P:(t + 1) * P],
                                  w[p][:, c, 3 * P:4 * P], start=(c == 0), stop=(c == DC - 1))
                    if t == NT - 1:
                        last.then_inc(S["z_ps"], 1)

                def transposes(bk, src, signal):
                    for t in range(NT):
                        last = tr(bank[bk][:, t * P:(t + 1) * P], src(t), g.ident[:, :])
                    last.then_inc(S[signal], 1)

                def decays():
                    if front is None:
                        return
                    wait(pe, "dg_ready", front)
                    wait(pe, "y1_ready", front - 1)
                    mm(bank[3][:, :], g.ones[:, :], dg[:, :, :].rearrange("p t n -> p (t n)"), start=True, stop=True)\
                        .then_inc(S["gb_ps"], 1)

                def k_tokens():
                    if front is None:
                        return
                    wait(pe, "k_silu", front)
                    transposes(1, lambda t: yk[:, t * P:(t + 1) * P], "ktok")

                def square_sums():
                    if front is None:
                        return
                    wait(pe, "e2_arg", front)
                    wait(pe, "k_square", front)
                    wait(pe, "q_square", front)
                    for a in range(2):
                        for t in range(NT):
                            last = mm(bank[3][:, a * NT + t:a * NT + t + 1], sq[a][:, t * P:(t + 1) * P],
                                      g.ones[:, 0:1], start=True, stop=True)
                    last.then_inc(S["sums"], 1)

                def v_tokens():
                    if front is None:
                        return
                    wait(pe, "v_silu", front)
                    transposes(2, lambda t: yv[:, t * P:(t + 1) * P], "vtok")

                def k_features():
                    if front is None:
                        return
                    wait(pe, "kh_ready", front)
                    wait(pe, "ss_ready", front)
                    transposes(3, lambda t: kh[:, t, :], "khT_ps")

                def keys_keys():
                    if front is None:
                        return
                    wait(pe, "khT_ready", front)
                    for t in range(NT):
                        last = mm(bank[1][:, t * P:(t + 1) * P], khT[p][:, t, :], khT[p][:, t, :],
                                  start=True, stop=True)
                    last.then_inc(S["kk"], 1)

                def keys_queries():
                    if front is None:
                        return
                    wait(pe, "bv_ready", front)
                    for t in range(NT):
                        last = mm(bank[2][:, t * P:(t + 1) * P], khT[p][:, t, :], yq[p][:, t * P:(t + 1) * P],
                                  start=True, stop=True)
                    last.then_inc(S["kq"], 1)

                def first_inverse():
                    if front is None:
                        return
                    wait(pe, "x1", front)
                    transposes(3, lambda t: X[p][:, t, :], "y1_ps")

                def corner(l):
                    if middle is None:
                        return
                    s = 2 ** (l + 1)
                    if l == 0:
                        wait(pe, "y1_ready", middle)
                        wait(pe, "o_copied", middle - 1)
                    else:
                        wait(pe, "y_ready", middle, l, LEVELS)
                    for t in range(NT):
                        second = Y[q][:, t, :].rearrange("p (q two c) -> p q two c", two=2, c=s)[:, :, 1, :]
                        last = mm(half_tiles(bank[4])[:, t, :], A[q][:, t, :], second, start=True, stop=True)
                    last.then_inc(S["p1_ps"], 1)

                def turn_y(l):
                    if middle is None or l < 0:
                        return
                    transposes(6, lambda t: Y[q][:, t, :], "xt_ps")

                def joined(l):
                    if middle is None:
                        return
                    wait(pe, "p1_ready", middle, l + 1, LEVELS)
                    if l:
                        wait(pe, "x_ready", middle, l, LEVELS - 1)
                    for t in range(NT):
                        last = mm(half_tiles(bank[5])[:, t, :], X[q][:, t, :], p1[:, t, :], start=True, stop=True)
                    last.then_inc(S["yp_ps"], 1)

                def first_values():
                    if middle is None:
                        return
                    wait(pe, "y_ready", middle, LEVELS, LEVELS)
                    wait(pe, "coreT_ready", middle - 1)
                    wait(pe, "bv_ready", middle)
                    for b in range(BATCH):
                        last = mm(bank[7][:, b * P:(b + 1) * P], Y[q][:, 2 * b, :], bv[q][:, 2 * b, :],
                                  start=True, stop=True)
                    last.then_inc(S["u0_ps"], 1)

                def state():
                    if middle is None:
                        return
                    wait(pe, "u0_ready", middle)
                    wait(pe, "kej_ready", middle)
                    for b in range(BATCH):
                        last = mm(bank[4][:, b * P:(b + 1) * P], kej[q][:, 2 * b, :], U[:, 2 * b, :],
                                  start=True, stop=True)
                    last.then_inc(S["s_ps"], 1)

                def of_state():
                    if middle is None:
                        return
                    wait(pe, "s_ready", middle)
                    for b in range(BATCH):
                        last = mm(bank[5][:, b * P:(b + 1) * P], khT[q][:, 2 * b + 1, :], St[:, b, :],
                                  start=True, stop=True)
                    last.then_inc(S["ks_ps"], 1)
                    for b in range(BATCH):
                        last = mm(bank[6][:, b * P:(b + 1) * P], yq[q][:, (2 * b + 1) * P:(2 * b + 2) * P],
                                  St[:, b, :], start=True, stop=True)
                    last.then_inc(S["qs_ps"], 1)

                def second_values():
                    if middle is None:
                        return
                    wait(pe, "r_ready", middle)
                    for b in range(BATCH):
                        last = mm(bank[7][:, (2 + b) * P:(3 + b) * P], Y[q][:, 2 * b + 1, :], R[:, b, :],
                                  start=True, stop=True)
                    last.then_inc(S["u1_ps"], 1)

                def outputs():
                    if middle is None:
                        return
                    wait(pe, "u1_ready", middle)
                    wait(pe, "pt_ready", middle)
                    for t in range(NT):
                        last = mm(bank[4][:, t * P:(t + 1) * P], PT[q][:, t, :], U[:, t, :], start=True, stop=True)
                    last.then_inc(S["o_ps"], 1)

                def turn_core():
                    if norm is None:
                        return
                    wait(pe, "core_ready", norm)
                    transposes(7, lambda t: core[:, t, :], "coreT_ps")

                if front is not None:
                    pe.wait_ge(w_loaded[p], 8 * front + (16 - 8 * p))
                project(1, 1, range(DC))
                corner(0)
                project(0, 0, range(0, 1))
                joined(0)
                project(0, 0, range(1, 2))
                corner(1)
                turn_y(0)
                project(0, 0, range(2, 3))
                joined(1)
                project(0, 0, range(3, 4))
                corner(2)
                turn_y(1)
                if front is not None:
                    wait(pe, "pt_ready", front - 1)
                project(2, 2, range(0, 1))
                joined(2)
                project(2, 2, range(1, 2))
                turn_core()
                corner(3)
                turn_y(2)
                project(2, 2, range(2, 3))
                joined(3)
                project(2, 2, range(3, 4))
                corner(4)
                turn_y(3)
                decays()
                joined(4)
                k_tokens()
                corner(5)
                turn_y(4)
                project_z(0)
                joined(5)
                square_sums()
                project_z(1)
                first_values()
                project_z(2)
                state()
                project_z(3)
                of_state()
                k_features()
                second_values()
                v_tokens()
                keys_keys()
                outputs()
                keys_queries()
                first_inverse()

            pe.wait_ge(S["cums_out"], 2)
            pipeline(pe, turn)
            pe.wait_ge(wo_loaded, 16)
            wait(pe, "coreT_ready", H - 1)
            for t in range(NT):
                for h in range(H):
                    last = mm(bank[t][:, :], coreT[:, h, t, :], wo[:, h, :], start=(h == 0), stop=(h == H - 1))
                last.then_inc(S["out_ps"], 1)

        @block.scalar
        def _(act):
            A_ = nc.scalar.activation
            act.wait_ge(loaded, 80)
            A_(expa[:, :], alog[:, :], ACT.Exp).then_inc(S["ab_exp"], 1)
            act.wait_ge(S["ab_out"], 1)
            A_(th[:, :, :], ab[:, :, 0:H], ACT.Tanh, scale=0.5).then_inc(S["ab_tanh"], 1)
            act.wait_ge(S["ab_out"], 2)
            A_(gb[:, :, :], ga[:, :, :], ACT.Exp, scale=-1.0).then_inc(S["g_exp"], 1)
            act.wait_ge(S["g_exp"], 1)
            A_(gb[:, :, :], gb[:, :, :], ACT.Ln, bias=1.0).then_inc(S["g_ln"], 1)
            act.wait_ge(S["cums_out"], 2)
            act.wait_ge(S["cums_out"], 3)
            sc = scal[:, :, :].rearrange("p h n -> p n h")
            A_(sc[:, NCUMX:NCUMX + NT, :], cum[:, :, :], ACT.Exp, scale=-1.0).then_inc(S["cum_exp"], 1)
            A_(sc[:, CREST:CREST + NT, :], last_cum[:, :, :], ACT.Exp).then_inc(S["cum_exp"], 1)
            act.wait_ge(S["scal_ready"], 1)
            heads = scal[:, :, :].rearrange("p h n -> p (h n)")

            def turn(front, middle, norm, p):
                q = 1 - p

                def copy_x(l):
                    if middle is None:
                        return
                    wait(act, "xt_ps", middle, l + 1, LEVELS - 1)
                    nc.scalar.copy(X[q][:, :, :], tiles(bank[6])).then_inc(S["x_ready"], 1)

                def tanh(n, src):
                    if front is None:
                        return
                    wait(act, f"{n}_conv", front)
                    A_(tn["kqv".index(n)][:, :], src[:, :], ACT.Tanh, scale=0.5).then_inc(S[f"{n}_tanh"], 1)

                def square(n, src):
                    if front is None:
                        return
                    wait(act, f"{n}_silu", front)
                    A_(sq["kq".index(n)][:, :], src[:, :], ACT.Square).then_inc(S[f"{n}_square"], 1)

                if front is not None:
                    wait(act, "o_ready", front - 2)
                    nc.scalar.copy(hs[p][:, :], heads[:, bass.ds(front * NS, NS)]).then_inc(S["hs_ready"], 1)
                tanh("k", yk)
                copy_x(0)
                tanh("q", yq[p])
                copy_x(1)
                square("k", yk)
                if norm is not None:
                    wait(act, "coreT_ps", norm)
                    nc.scalar.copy(coreT[:, :, :, :].rearrange("p h t n -> p (h t n)")[:, bass.ds(norm * TOK, TOK)],
                                   bank[7][:, :]).then_inc(S["coreT_ready"], 1)
                copy_x(2)
                square("q", yq[p])
                copy_x(3)
                if front is not None:
                    wait(act, "e1_arg", front)
                    A_(e1[:, :, :], e1[:, :, :], ACT.Exp).then_inc(S["e1_ready"], 1)
                tanh("v", yv)
                copy_x(4)
                if front is not None:
                    wait(act, "e2_arg", front)
                    A_(e2[:, :, :], e2[:, :, :], ACT.Exp, scale=-1.0).then_inc(S["e2_ready"], 1)
                if middle is not None:
                    ev = U[:, :, :].rearrange("p (b two) n -> p b two n", two=2)
                    wait(act, "u0_ps", middle)
                    nc.scalar.copy(ev[:, :, 0, :], bank[7][:, 0:2 * P].rearrange("p (b n) -> p b n", b=BATCH))\
                      .then_inc(S["u0_ready"], 1)
                    wait(act, "s_ps", middle)
                    nc.scalar.copy(St[:, :, :], bank[4][:, 0:BATCH * P].rearrange("p (b n) -> p b n", b=BATCH))\
                      .then_inc(S["s_ready"], 1)
                if front is not None:
                    wait(act, "z_ps", front)
                    A_(zt[:, :, :], tiles(bank[0]), ACT.Tanh, scale=0.5).then_inc(S["z_tanh"], 1)
                    wait(act, "khT_ps", front)
                    nc.scalar.copy(khT[p][:, :, :], tiles(bank[3])).then_inc(S["khT_ready"], 1)
                if middle is not None:
                    wait(act, "u1_ps", middle)
                    nc.scalar.copy(ev[:, :, 1, :], bank[7][:, 2 * P:4 * P].rearrange("p (b n) -> p b n", b=BATCH))\
                      .then_inc(S["u1_ready"], 1)
                    wait(act, "o_ps", middle)
                    nc.scalar.copy(o[:, :, :], tiles(bank[4])).then_inc(S["o_copied"], 1)
                if front is not None:
                    wait(act, "y1_ps", front)
                    nc.scalar.copy(Y[p][:, :, :], tiles(bank[3])).then_inc(S["y1_ready"], 1)

            pipeline(act, turn)

        @block.vector
        def _(dve):
            V = nc.vector
            c = Links(dve, own)
            dve.wait_ge(loaded, 80)
            dve.wait_ge(S["ab"], 1)
            V.tensor_copy(ab[:, :, :], bank[0][:, 0:NT * 2 * H].rearrange("p (t n) -> p t n", t=NT))\
             .then_inc(S["ab_out"], 1)
            dve.wait_ge(S["ab_out"], 1)
            c.link(V.tensor_tensor(ab[:, :, H:2 * H], ab[:, :, H:2 * H],
                                   dtb[:, :].unsqueeze(1).broadcast_to((P, NT, H)), ALU.add))
            c.link(V.tensor_scalar(ga[:, :, :], ab[:, :, H:2 * H], -1.0, None, ALU.mult))
            V.tensor_tensor(ga[:, :, :], ga[:, :, :], ab[:, :, H:2 * H], ALU.max).then_inc(S["ab_out"], 1)
            dve.wait_ge(S["g_ln"], 1)
            c.link(V.scalar_tensor_tensor(out=gneg[:, :, :], in0=ab[:, :, H:2 * H], scalar=0.0, in1=gb[:, :, :],
                                          op0=ALU.max, op1=ALU.add))
            dve.wait_ge(S["ab_exp"], 1)
            V.tensor_tensor(gneg[:, :, :], gneg[:, :, :], expa[:, :].unsqueeze(1).broadcast_to((P, NT, H)),
                            ALU.mult).then_inc(S["gneg"], 1)
            dve.wait_ge(S["cums"], 1)
            V.tensor_copy(cum[:, :, :], bank[1][:, 0:NG].rearrange("p (t h) -> p t h", t=NT))\
             .then_inc(S["cums_out"], 1)
            dve.wait_ge(S["cums_out"], 1)
            V.scalar_tensor_tensor(out=last_cum[:, :, :], in0=bank[2][:, 0:NG].rearrange("p (t h) -> p t h", t=NT),
                                   scalar=-1.0, in1=cum[:, :, :], op0=ALU.mult, op1=ALU.add)\
             .then_inc(S["cums_out"], 1)
            sc = scal[:, :, :].rearrange("p h n -> p n h")
            V.tensor_copy(sc[:, CUM:CUM + NT, :], cum[:, :, :]).then_inc(S["cums_out"], 1)
            c.link(V.tensor_copy(sc[:, GN:GN + NT, :], gneg[:, :, :]))
            dve.wait_ge(S["ab_tanh"], 1)
            c.link(V.tensor_scalar(sc[:, BETA:BETA + NT, :], th[:, :, :], 1.0, 0.5, ALU.add, ALU.mult))
            c.link(V.tensor_scalar(sc[:, HBETA:HBETA + NT, :], th[:, :, :], 1.0, 0.25, ALU.add, ALU.mult))
            dve.wait_ge(S["cum_exp"], 2)
            c.link(V.scalar_tensor_tensor(out=sc[:, NBX:NBX + NT, :], in0=sc[:, NCUMX:NCUMX + NT, :], scalar=-1.0,
                                          in1=sc[:, BETA:BETA + NT, :], op0=ALU.mult, op1=ALU.mult))
            V.tensor_scalar(normw[:, :], normw[:, :], 0.5, None, ALU.mult).then_inc(S["scal_ready"], 1)
            dve.wait_ge(S["scal_ready"], 1)
            dve.wait_ge(pool_own, 7 + 3 * LEVELS)
            FRONT_OWN, NORM_OWN = 9, 4

            def turn(front, middle, norm, p):
                q = 1 - p
                cf = Links(dve, front_own, None if front is None else FRONT_OWN * front)
                cn = Links(dve, norm_own, None if norm is None else NORM_OWN * norm)

                def conv(n, dst_, bk, taps):
                    if front is None:
                        return
                    k0 = CW + TAPS * "qkv".index(n)
                    src = bank[bk][:, :].rearrange("p (b s) -> p b s", b=BATCH)
                    dst = dst_[:, :].rearrange("p (b s) -> p b s", b=BATCH)
                    for d in taps:
                        if d == 0:
                            wait(dve, f"{n}_ps", front)
                            ins = V.tensor_scalar(dst_[:, :], bank[bk][:, :], hs[p][:, k0 + 3:k0 + 4], None, ALU.mult)
                        else:
                            ins = V.scalar_tensor_tensor(out=dst[:, :, d:], in0=src[:, :, 0:SEQ - d],
                                                         scalar=hs[p][:, k0 + 3 - d:k0 + 4 - d], in1=dst[:, :, d:],
                                                         op0=ALU.mult, op1=ALU.add)
                        if d < 3:
                            cf.link(ins)
                        else:
                            ins.then_inc(S[f"{n}_conv"], 1)

                def silu(n, y):
                    if front is None:
                        return
                    wait(dve, f"{n}_tanh", front)
                    V.scalar_tensor_tensor(out=y[:, :], in0=tn["kqv".index(n)][:, :], scalar=1.0, in1=y[:, :],
                                           op0=ALU.add, op1=ALU.mult).then_inc(S[f"{n}_silu"], 1)

                def exponent(e, bound, op, signal):
                    if front is None:
                        return
                    wait(dve, "gb_ps", front)
                    for t in range(NT):
                        last = V.scalar_tensor_tensor(out=e[:, t, :], in0=tiles(bank[3])[:, t, :],
                                                      scalar=hs[p][:, CUM + t:CUM + t + 1], in1=bound[:, :],
                                                      op0=ALU.subtract, op1=op)
                    last.then_inc(S[signal], 1)

                def mask_corner(l):
                    if middle is None:
                        return
                    wait(dve, "p1_ps", middle, l + 1, LEVELS)
                    V.tensor_tensor(p1[:, :, :], half_tiles(bank[4]),
                                    pairm[:, l, :].unsqueeze(1).broadcast_to((P, NT, HALF)), ALU.mult)\
                     .then_inc(S["p1_ready"], 1)

                def join(l):
                    if middle is None:
                        return
                    wait(dve, "yp_ps", middle, l + 1, LEVELS)
                    s = 2 ** (l + 1)
                    sec = Y[q][:, :, :].rearrange("p t (q two c) -> p (t q) two c", two=2, c=s)[:, :, 1, :]
                    yp = bank[5][:, 0:NT * HALF].rearrange("p (q c) -> p q c", c=s)
                    V.tensor_tensor(sec, sec, yp, ALU.subtract).then_inc(S["y_ready"], 1)

                if front is not None:
                    wait(dve, "hs_ready", front)
                    wait(dve, "k_square", front - 1)
                conv("k", yk, 1, (0, 1))
                mask_corner(0)
                conv("k", yk, 1, (2, 3))
                join(0)
                if norm is not None:
                    wait(dve, "o_ready", norm)
                    wait(dve, "core_ready", norm - 1)
                    cn.link(V.tensor_tensor(osq[:, :, :], o[:, :, :], o[:, :, :], ALU.mult))
                    V.tensor_tensor(rs2[:, :], rs[p][:, 1, :], rs[p][:, 1, :], ALU.mult)
                    cn.link(V.tensor_reduce(oss[:, :], osq[:, :, :], AX.X, ALU.add))
                mask_corner(1)
                if norm is not None:
                    cn.link(V.tensor_tensor(oss[:, :], oss[:, :], rs2[:, :], ALU.mult))
                    V.tensor_scalar(oss[:, :], oss[:, :], 1.0 / (DV * DK), EPS, ALU.mult, ALU.add)\
                     .then_inc(S["f_arg"], 1)
                conv("q", yq[p], 0, (0,))
                join(1)
                silu("k", yk)
                conv("q", yq[p], 0, (1,))
                mask_corner(2)
                conv("q", yq[p], 0, (2, 3))
                join(2)
                if norm is not None:
                    wait(dve, "f_pow", norm)
                    cn.link(V.scalar_tensor_tensor(out=f[:, :], in0=f[:, :], scalar=DK ** -0.5, in1=rs[p][:, 1, :],
                                                   op0=ALU.mult, op1=ALU.mult))
                    wait(dve, "coreT_ps", norm - 1)
                    for t in range(NT):
                        last = V.scalar_tensor_tensor(out=core[:, t, :], in0=o[:, t, :], scalar=f[:, t:t + 1],
                                                      in1=zs[p][:, t, :], op0=ALU.mult, op1=ALU.mult)
                    last.then_inc(S["core_ready"], 1)
                mask_corner(3)
                silu("q", yq[p])
                conv("v", yv, 2, (0,))
                join(3)
                conv("v", yv, 2, (1, 2))
                mask_corner(4)
                conv("v", yv, 2, (3,))
                exponent(e1, low, ALU.min, "e1_arg")
                join(4)
                exponent(e2, up, ALU.max, "e2_arg")
                mask_corner(5)
                silu("v", yv)
                join(5)
                if front is not None:
                    wait(dve, "sums", front)
                    V.tensor_scalar(ss[:, :, :], bank[3][:, 0:2 * NT].rearrange("p (a t) -> p a t", a=2), 4 * EPS,
                                    None, ALU.add).then_inc(S["ss_ready"], 1)
                    wait(dve, "ktok", front)
                    wait(dve, "rs_ready", front)
                    V.tensor_tensor(kh[:, :, :], tiles(bank[1]), rs[p][:, 0, :].unsqueeze(2).broadcast_to((P, NT, DK)),
                                    ALU.mult).then_inc(S["kh_ready"], 1)
                if middle is not None:
                    wait(dve, "ks_ps", middle)
                    for b in range(BATCH):
                        t = 2 * b + 1
                        last = V.scalar_tensor_tensor(out=R[:, b, :], in0=bank[5][:, b * P:(b + 1) * P],
                                                      scalar=hs[q][:, NBX + t:NBX + t + 1], in1=bv[q][:, t, :],
                                                      op0=ALU.mult, op1=ALU.add)
                    last.then_inc(S["r_ready"], 1)
                if front is not None:
                    wait(dve, "vtok", front)
                    V.tensor_tensor(bv[p][:, :, :], tiles(bank[2]), cols(p, HBETA), ALU.mult)\
                     .then_inc(S["bv_ready"], 1)
                    wait(dve, "z_tanh", front)
                    V.scalar_tensor_tensor(out=zs[p][:, :, :], in0=zt[:, :, :], scalar=1.0, in1=tiles(bank[0]),
                                           op0=ALU.add, op1=ALU.mult).then_inc(S["z_mul"], 1)
                    wait(dve, "kk", front)
                    wait(dve, "e1_ready", front)
                    for t in range(NT):
                        last = V.scalar_tensor_tensor(out=A[p][:, t, :], in0=tiles(bank[1])[:, t, :],
                                                      scalar=hs[p][:, BETA + t:BETA + t + 1], in1=e1[:, t, :],
                                                      op0=ALU.mult, op1=ALU.mult)
                    last.then_inc(S["a_ready"], 1)
                    wait(dve, "a_ready", front)
                    V.tensor_tensor(X[p][:, :, :], A[p][:, :, :],
                                    m0[:, :].unsqueeze(1).broadcast_to((P, NT, P)), ALU.mult)\
                     .then_inc(S["a_pairs"], 1)
                    wait(dve, "a_pairs", front)
                    V.scalar_tensor_tensor(out=X[p][:, :, :], in0=X[p][:, :, :], scalar=-1.0,
                                           in1=g.ident[:, :].unsqueeze(1).broadcast_to((P, NT, P)),
                                           op0=ALU.mult, op1=ALU.add).then_inc(S["x1"], 1)
                if middle is not None:
                    wait(dve, "o_copied", middle)
                    wait(dve, "qs_ps", middle)
                    for b in range(BATCH):
                        t = 2 * b + 1
                        last = V.scalar_tensor_tensor(out=o[:, t, :], in0=bank[6][:, b * P:(b + 1) * P],
                                                      scalar=hs[q][:, NCUMX + t:NCUMX + t + 1], in1=o[:, t, :],
                                                      op0=ALU.mult, op1=ALU.add)
                    last.then_inc(S["o_ready"], 1)
                if front is not None:
                    wait(dve, "z_mul", front)
                    V.tensor_tensor(zs[p][:, :, :], zs[p][:, :, :],
                                    normw[:, :].unsqueeze(1).broadcast_to((P, NT, DV)), ALU.mult)\
                     .then_inc(S["zs_ready"], 1)
                    wait(dve, "kq", front)
                    wait(dve, "e2_ready", front)
                    V.tensor_tensor(PT[p][:, :, :], tiles(bank[2]), e2[:, :, :], ALU.mult).then_inc(S["pt_ready"], 1)
                assert front is None or cf.n == FRONT_OWN, cf.n
                assert norm is None or cn.n == NORM_OWN, cn.n

            pipeline(dve, turn)
            for t in range(NT):
                dve.wait_ge(S["out_ps"], t + 1)
                V.tensor_tensor(g.x[:, t, :], g.x[:, t, :], bank[t][:, :], ALU.add).then_inc(S["out_added"], 1)


def expert_stage(nc, g, dram):
    E, K, F, CAP = 64, 8, 192, 128
    FH = F // 2
    NONE = E * CAP
    DEEP = 4
    XT_LAG, H_LAG = 3, 4
    LAST = 4
    xn_rows, y_rows = dram["xn_rows"], dram["y_rows"]
    with ExitStack() as ctx:
        m = Mem(nc, ctx, "moe")
        rw = m.sb("rw", [P, DC, E])
        gu = [m.sb(f"gu{i}", [P, DC, 2 * F]) for i in range(DEEP)]
        wd = [m.sb(f"wd{i}", [FH, 2, D]) for i in range(DEEP)]
        logit, score, cut = m.sb("logit", [P, NT, E]), m.sb("score", [P, NT, E]), m.sb("cut", [P, NT, E])
        nmax, total, rtotal = m.sb("nmax", [P, NT]), m.sb("total", [P, NT]), m.sb("rtotal", [P, NT])
        top, wk = m.sb("top", [P, NT, K]), m.sb("wk", [P, NT, K])
        chosen_u, chosen = m.sb("chosen_u", [P, NT, K], U32), m.sb("chosen", [P, NT, K])
        mask, rank = m.sb("mask", [P, NT, E]), m.sb("rank", [P, NT, E])
        count = m.sb("count", [P, NT, E])
        rank_e = m.sb("rank_e", [P, E, NT])
        picked = m.sb("picked", [P, E])
        place, fits, dest = m.sb("place", [P, NT, K]), m.sb("fits", [P, NT, K]), m.sb("dest", [P, NT, K], I32)
        iota_e, iota_s = m.sb("iota_e", [P, E]), m.sb("iota_s", [P, CAP])
        tok = m.sb("tok", [P, 2, NT], BF16)
        onehot = [m.sb(f"onehot{i}", [P, NT, CAP], BF16) for i in range(2)]
        idx = [m.sb(f"idx{i}", [P, 1], I32) for i in range(DEEP)]
        xg = [m.sb(f"xg{i}", [P, D]) for i in range(DEEP)]
        xgT = [m.sb(f"xgT{i}", [P, DC, CAP]) for i in range(2)]
        th = [m.sb(f"th{i}", [P, F]) for i in range(2)]
        h = [m.sb(f"h{i}", [P, F]) for i in range(2)]
        hT = [m.sb(f"hT{i}", [FH, 2, CAP]) for i in range(2)]
        y = [m.sb(f"y{i}", [P, D]) for i in range(DEEP)]
        zero = m.sb("zero", [1, D])
        NG = 6
        yg = [m.sb(f"yg{i}", [P, D]) for i in range(NG)]
        IDX = g.bank[0]
        XT = [g.bank[1 + i][:, :].rearrange("p (c n) -> p c n", c=DC) for i in range(2)]
        GU = [g.bank[3 + i] for i in range(2)]
        HT = g.bank[5]
        HTv = HT[0:FH, 0:2 * CAP].rearrange("p (a n) -> p a n", a=2)
        Y = [g.bank[6 + i] for i in range(2)]
        rw_loaded, xn_stored, zero_stored = m.sem("rw_loaded"), m.sem("xn_stored"), m.sem("zero_stored")
        w_loaded = [m.sem(f"w_loaded{i}") for i in range(DEEP)]
        gathered = [m.sem(f"gathered{i}") for i in range(DEEP)]
        stored = [m.sem(f"stored{i}") for i in range(DEEP)]
        y_gathered = [m.sem(f"y_gathered{i}") for i in range(NG)]
        own, pool_own = m.sem("own"), m.sem("pool_own")
        names = """iotas logits exp_in exp_out mask_ready ranks dest_ready onehot_ready gather_begun idx_ps idx_ready xt_ps
            xgT_ready gu_ps th_ready h1_ready h_ready ht_ps hT_ready y_ps y_copied y_added""".split()
        S = {n: m.sem(n) for n in names}
        block = ctx.enter_context(nc.Block())

        def steps(eng, body, lo, hi):
            first, last = 8, 56
            for s in range(lo, first):
                body(s)
            with eng.Fori(first, last, DEEP) as r:
                for k in range(DEEP):
                    body(r, k)
            for s in range(last, hi):
                body(s)

        class At:

            def __init__(self, s, half, lag):
                if half is None:
                    self.e = s - lag
                    self.p, self.q = self.e % 2, self.e % DEEP
                    self.exists = 0 <= self.e < E
                    self.static = True
                else:
                    self.e = s + (half - lag)
                    self.p, self.q = (half - lag) % 2, (half - lag) % DEEP
                    self.exists = True
                    self.static = False

        def wait_own(eng, sem, at):
            eng.wait_ge(sem, at.e + 1)

        def wait_before(eng, sem, at, back):
            if not at.static or at.e >= back:
                eng.wait_ge(sem, at.e + (1 - back))

        def wait_dma(eng, sems, at, back=0, per=16):
            if not at.static or at.e >= back:
                eng.wait_ge(sems[at.q], at.e * (per // DEEP) + (per - (per // DEEP) * (at.q + back)))

        @block.sync
        def _(sp):
            sp.dma_start(rw[:, :, :], dram["L0_ffn_router"].rearrange("(c p) n -> p c n", p=P)).then_inc(rw_loaded, 16)
            sp.dma_start(xn_rows.rearrange("(t p) d -> p t d", p=P), g.xn[:, :, :]).then_inc(xn_stored, 16)

            def body(s, half=None):
                a = At(s, half, 0)
                if a.exists:
                    wait_before(sp, S["y_ps"], a, DEEP)
                    sp.dma_start(gu[a.q][:, :, :], dram["L0_ffn_gate_up"][bass.ds(a.e * P, P), :]
                                 .rearrange("p (c n) -> p c n", c=DC)).then_inc(w_loaded[a.q], 16)
                    sp.dma_start(wd[a.q][:, :, :], dram["L0_ffn_w_down"][bass.ds(a.e * FH, FH), :]
                                 .rearrange("p (a n) -> p a n", a=2)).then_inc(w_loaded[a.q], 16)
                a = At(s, half, LAST)
                if a.exists:
                    wait_own(sp, S["y_copied"], a)
                    sp.dma_start(y_rows[bass.ds(a.e * CAP, CAP), :], y[a.q][:, :]).then_inc(stored[a.q], 16)

            steps(sp, body, 0, E + LAST)
            sp.wait_ge(xn_stored, 16)
            for q in range(DEEP):
                sp.wait_ge(stored[q], 16 * E // DEEP)
            sp.wait_ge(zero_stored, 16)

        @block.gpsimd
        def _(pool):
            pool.iota(iota_e[:, :], pattern=[[1, E]], base=0, channel_multiplier=0,
                      allow_small_or_imprecise_dtypes=True).then_inc(S["iotas"], 1)
            pool.iota(iota_s[:, :], pattern=[[1, CAP]], base=1, channel_multiplier=0,
                      allow_small_or_imprecise_dtypes=True).then_inc(S["iotas"], 1)
            pool.iota(tok[:, 0, :], pattern=[[P, NT]], base=0, channel_multiplier=0,
                      allow_small_or_imprecise_dtypes=True).then_inc(S["iotas"], 1)
            pool.iota(tok[:, 1, :], pattern=[[0, NT]], base=0, channel_multiplier=1,
                      allow_small_or_imprecise_dtypes=True).then_inc(S["iotas"], 1)
            pool.memset(zero[:, :], 0.0).then_inc(pool_own, 1)
            pool.wait_ge(pool_own, 1)
            pool.dma_start(y_rows[NONE:NONE + 1, :], zero[:, :]).then_inc(zero_stored, 16)
            pool.wait_ge(xn_stored, 16)

            def body(s, half=None):
                a = At(s, half, 0)
                if a.exists:
                    wait_before(pool, S["xt_ps"], a, DEEP)
                    wait_own(pool, S["idx_ready"], a)
                    pool.sem_inc(S["gather_begun"], 1)
                    pool.indirect_dma_start(xg[a.q][:, :], None, xn_rows,
                                            bass.IndirectOffsetOnAxis(idx[a.q][:, 0:1], 0))\
                        .then_inc(gathered[a.q], 16)

            steps(pool, body, 0, E)
            pool.wait_ge(S["dest_ready"], 1)
            for q in range(DEEP):
                pool.wait_ge(stored[q], 16 * E // DEEP)
            pool.wait_ge(zero_stored, 16)
            for n in range(NT * K):
                if n >= NG:
                    pool.wait_ge(S["y_added"], n - NG + 1)
                pool.indirect_dma_start(yg[n % NG][:, :], None, y_rows,
                                        bass.IndirectOffsetOnAxis(dest[:, n // K, n % K:n % K + 1], 0))\
                    .then_inc(y_gathered[n % NG], 16)

        @block.tensor
        def _(pe):
            mm, tr = nc.tensor.matmul, nc.tensor.transpose
            pe.wait_ge(rw_loaded, 16)
            for t in range(NT):
                for c in range(DC):
                    last = mm(GU[0][:, t * E:(t + 1) * E], g.xT[:, c, t * P:(t + 1) * P], rw[:, c, :],
                              start=(c == 0), stop=(c == DC - 1))
            last.then_inc(S["logits"], 1)
            pe.wait_ge(S["mask_ready"], 1)
            flat = mask[:, :, :].rearrange("p t e -> p (t e)")
            mm(GU[0][:, 0:NT * E], g.triu[:, :], flat, start=True, stop=True)
            mm(GU[1][:, 0:NT * E], g.ones[:, :], flat, start=True, stop=True).then_inc(S["ranks"], 1)

            def body(s, half=None):
                a = At(s, half, 0)
                if a.exists:
                    wait_own(pe, S["onehot_ready"], a)
                    wait_before(pe, S["idx_ready"], a, 1)
                    for t in range(NT):
                        for part in range(2):
                            last = mm(IDX[:, 0:1], onehot[a.p][:, t, :], tok[:, part, t:t + 1],
                                      start=(t == 0 and part == 0), stop=(t == NT - 1 and part == 1))
                    last.then_inc(S["idx_ps"], 1)
                a = At(s, half, XT_LAG)
                if a.exists:
                    wait_dma(pe, gathered, a)
                    wait_before(pe, S["xgT_ready"], a, 2)
                    for c in range(DC):
                        last = tr(XT[a.p][:, c, :], xg[a.q][:, c * P:(c + 1) * P], g.ident[:, :])
                    last.then_inc(S["xt_ps"], 1)
                a = At(s, half, H_LAG)
                if a.exists:
                    wait_own(pe, S["h_ready"], a)
                    wait_before(pe, S["hT_ready"], a, 1)
                    for k in range(2):
                        last = tr(HTv[:, k, :], h[a.p][:, k * FH:(k + 1) * FH], g.ident[:, :])
                    last.then_inc(S["ht_ps"], 1)
                a = At(s, half, XT_LAG)
                if a.exists:
                    wait_dma(pe, w_loaded, a, per=32)
                    wait_own(pe, S["xgT_ready"], a)
                    wait_before(pe, S["h_ready"], a, 2)
                    for c in range(DC):
                        last = mm(GU[a.p][:, 0:2 * F], xgT[a.p][:, c, :], gu[a.q][:, c, :],
                                  start=(c == 0), stop=(c == DC - 1))
                    last.then_inc(S["gu_ps"], 1)
                a = At(s, half, H_LAG)
                if a.exists:
                    wait_own(pe, S["hT_ready"], a)
                    wait_before(pe, S["y_copied"], a, 2)
                    for k in range(2):
                        last = mm(Y[a.p][:, :], hT[a.p][:, k, :], wd[a.q][:, k, :], start=(k == 0), stop=(k == 1))
                    last.then_inc(S["y_ps"], 1)

            steps(pe, body, 0, E + LAST)

        @block.scalar
        def _(act):
            act.wait_ge(S["exp_in"], 1)
            nc.scalar.activation(score[:, :, :], logit[:, :, :], ACT.Exp).then_inc(S["exp_out"], 1)

            def body(s, half=None):
                a = At(s, half, XT_LAG)
                if a.exists:
                    wait_own(act, S["xt_ps"], a)
                    wait_before(act, S["gu_ps"], a, 2)
                    nc.scalar.copy(xgT[a.p][:, :, :], XT[a.p][:, :, :]).then_inc(S["xgT_ready"], 1)
                    wait_own(act, S["gu_ps"], a)
                    wait_before(act, S["h_ready"], a, 2)
                    nc.scalar.activation(th[a.p][:, :], GU[a.p][:, 0:F], ACT.Tanh, scale=0.5)\
                      .then_inc(S["th_ready"], 1)
                a = At(s, half, H_LAG)
                if a.exists:
                    wait_own(act, S["y_ps"], a)
                    wait_dma(act, stored, a, back=DEEP)
                    nc.scalar.copy(y[a.q][:, :], Y[a.p][:, :]).then_inc(S["y_copied"], 1)

            steps(act, body, 0, E + LAST)

        @block.vector
        def _(dve):
            V = nc.vector
            c = Links(dve, own)
            dve.wait_ge(S["logits"], 1)
            c.link(V.tensor_copy(logit[:, :, :], GU[0][:, 0:NT * E].rearrange("p (t e) -> p t e", t=NT)))
            c.link(V.tensor_reduce(nmax[:, :], logit[:, :, :], AX.X, ALU.max, negate=True))
            V.tensor_tensor(logit[:, :, :], logit[:, :, :], nmax[:, :].unsqueeze(2).broadcast_to((P, NT, E)), ALU.add)\
             .then_inc(S["exp_in"], 1)
            dve.wait_ge(S["exp_out"], 1)
            c.link(V.tensor_reduce(total[:, :], score[:, :, :], AX.X, ALU.add))
            c.link(V.reciprocal(rtotal[:, :], total[:, :]))
            c.link(V.tensor_tensor(score[:, :, :], score[:, :, :], rtotal[:, :].unsqueeze(2).broadcast_to((P, NT, E)),
                                   ALU.mult))
            for t in range(NT):
                c.link(V.max(top[:, t, :], score[:, t, :]))
                c.link(V.match_replace(cut[:, t, :], top[:, t, :], score[:, t, :], -1.0))
                c.link(V.max_index(chosen_u[:, t, :], top[:, t, :], score[:, t, :]))
            V.tensor_tensor(mask[:, :, :], score[:, :, :], cut[:, :, :], ALU.not_equal).then_inc(S["mask_ready"], 1)
            dve.wait_ge(S["iotas"], 4)
            c.link(V.tensor_reduce(total[:, :], top[:, :, :], AX.X, ALU.add))
            c.link(V.tensor_scalar(total[:, :], total[:, :], 1e-20, 2.0, ALU.add, ALU.mult))
            c.link(V.reciprocal(rtotal[:, :], total[:, :]))
            c.link(V.tensor_tensor(wk[:, :, :], top[:, :, :], rtotal[:, :].unsqueeze(2).broadcast_to((P, NT, K)),
                                   ALU.mult))
            c.link(V.tensor_copy(chosen[:, :, :], chosen_u[:, :, :]))
            dve.wait_ge(S["ranks"], 1)
            c.link(V.tensor_copy(rank[:, :, :], GU[0][:, 0:NT * E].rearrange("p (t e) -> p t e", t=NT)))
            c.link(V.tensor_copy(count[:, :, :], GU[1][:, 0:NT * E].rearrange("p (t e) -> p t e", t=NT)))
            for t in range(1, NT):
                for u in range(t):
                    c.link(V.tensor_tensor(rank[:, t, :], rank[:, t, :], count[:, u, :], ALU.add))
            c.link(V.tensor_tensor(rank[:, :, :], rank[:, :, :], mask[:, :, :], ALU.mult))
            c.link(V.tensor_copy(rank_e[:, :, :].rearrange("p e t -> p t e"), rank[:, :, :]))

            def places():
                for t in range(NT):
                    for k in range(K):
                        c.link(V.scalar_tensor_tensor(out=picked[:, :], in0=iota_e[:, :],
                                                      scalar=chosen[:, t, k:k + 1], in1=rank[:, t, :],
                                                      op0=ALU.is_equal, op1=ALU.mult,
                                                      accum_out=place[:, t, k:k + 1]))
                c.link(V.tensor_scalar(fits[:, :, :], place[:, :, :], float(CAP), None, ALU.is_le))
                c.link(V.scalar_tensor_tensor(out=place[:, :, :], in0=chosen[:, :, :], scalar=float(CAP),
                                              in1=place[:, :, :], op0=ALU.mult, op1=ALU.add))
                c.link(V.scalar_tensor_tensor(out=place[:, :, :], in0=place[:, :, :], scalar=-1.0 - NONE,
                                              in1=fits[:, :, :], op0=ALU.add, op1=ALU.mult))
                V.tensor_scalar(dest[:, :, :], place[:, :, :], float(NONE), None, ALU.add)\
                 .then_inc(S["dest_ready"], 1)

            def body(s, half=None):
                if half is None and s == 6:
                    places()
                a = At(s, half, -1)
                if a.exists:
                    wait_before(dve, S["idx_ps"], a, 2)
                    ranks = rank_e[:, :, :].rearrange("p e t -> p (e t)")[:, bass.ds(a.e * NT, NT)]
                    V.tensor_tensor(onehot[a.p][:, :, :], iota_s[:, :].unsqueeze(1).broadcast_to((P, NT, CAP)),
                                    ranks.unsqueeze(2).broadcast_to((P, NT, CAP)), ALU.is_equal)\
                     .then_inc(S["onehot_ready"], 1)
                a = At(s, half, 0)
                if a.exists:
                    wait_own(dve, S["idx_ps"], a)
                    wait_dma(dve, gathered, a, back=DEEP)
                    V.tensor_copy(idx[a.q][:, :], IDX[:, 0:1]).then_inc(S["idx_ready"], 1)
                a = At(s, half, H_LAG)
                if a.exists:
                    wait_own(dve, S["ht_ps"], a)
                    wait_before(dve, S["y_ps"], a, 2)
                    V.tensor_copy(hT[a.p][:, :, :], HTv).then_inc(S["hT_ready"], 1)
                a = At(s, half, XT_LAG)
                if a.exists:
                    wait_own(dve, S["th_ready"], a)
                    wait_before(dve, S["ht_ps"], a, 2)
                    V.scalar_tensor_tensor(out=th[a.p][:, :], in0=th[a.p][:, :], scalar=1.0, in1=GU[a.p][:, 0:F],
                                           op0=ALU.add, op1=ALU.mult).then_inc(S["h1_ready"], 1)
                    wait_own(dve, S["h1_ready"], a)
                    V.tensor_tensor(h[a.p][:, :], th[a.p][:, :], GU[a.p][:, F:2 * F], ALU.mult)\
                     .then_inc(S["h_ready"], 1)

            steps(dve, body, -1, E + LAST)
            for n in range(NT * K):
                t, k = n // K, n % K
                dve.wait_ge(y_gathered[n % NG], 16 * (n // NG + 1))
                if k:
                    dve.wait_ge(S["y_added"], n)
                V.scalar_tensor_tensor(out=g.x[:, t, :], in0=yg[n % NG][:, :], scalar=wk[:, t, k:k + 1],
                                       in1=g.x[:, t, :], op0=ALU.mult, op1=ALU.add).then_inc(S["y_added"], 1)


def ternary_stage(nc, g, dram):
    HID, QB = 2048, 127.0
    HC = HID // P
    ROUND = 1.5 * 2.0 ** 23
    with ExitStack() as ctx:
        m = Mem(nc, ctx, "ffn")
        up, down = m.sb("up", [P, DC * HID]), m.sb("down", [P, HC * D])
        above = m.sb("above", [P, DC * HID], BF16)
        upq = m.sb("upq", [P, DC, HID], BF16)
        hT = m.sb("hT", [P, HC, TOK])
        hm = [m.sb(f"hm{i}", [P, TOK]) for i in range(2)]
        ht = [m.sb(f"ht{i}", [P, TOK]) for i in range(2)]
        nw, gam = m.sb("nw", [P, D]), m.sb("gam", [P, D])
        sq = m.sb("sq", [P, NT, D])
        ss, r, big, rbig, sx = (m.sb(n, [P, NT]) for n in ("ss", "r", "big", "rbig", "sx"))
        dg, sxb = m.sb("dg", [P, NT, P]), m.sb("sxb", [P, TOK])
        xqT = m.sb("xqT", [P, DC, TOK], BF16)
        part, scale = m.sb("part", [P, 2]), m.sb("scale", [P, 2])
        thr, nthr = m.sb("thr", [P, 2]), m.sb("nthr", [P, 2])
        tscale, final = m.sb("tscale", [P, 1]), m.sb("final", [P, 1])
        bank = g.bank
        loaded = {n: m.sem(f"loaded_{n}") for n in ("up", "down", "rows")}
        own = m.sem("own")
        names = """square ss_ready r_ready xq_ready xqT_ps xqT_ready sx_dg sxb_ps abs_done sums scales up_q down_q
            h_ps hm_ready th_ready h_ready y_ps""".split()
        S = {n: m.sem(n) for n in names}
        block = ctx.enter_context(nc.Block())

        @block.sync
        def _(sp):
            sp.dma_start(nw[:, :], dram["L1_ffn_norm_weight"].partition_broadcast(P)).then_inc(loaded["rows"], 16)
            sp.dma_start(gam[:, :], dram["L1_ffn_gamma"].partition_broadcast(P)).then_inc(loaded["rows"], 16)
            sp.dma_start(up[:, :].rearrange("p (c n) -> p c n", c=DC),
                         dram["L1_ffn_up"].rearrange("(c p) n -> p c n", p=P)).then_inc(loaded["up"], 16)
            sp.dma_start(down[:, :].rearrange("p (c n) -> p c n", c=HC),
                         dram["L1_ffn_down"].rearrange("(c p) n -> p c n", p=P)).then_inc(loaded["down"], 16)

        @block.gpsimd
        def _(pool):
            pool.wait_ge(S["ss_ready"], 1)
            nc.gpsimd.tensor_tensor(r[:, :], ss[:, :], g.half[:, 0:NT], ALU.pow).then_inc(S["r_ready"], 1)

        @block.scalar
        def _(act):
            for t in range(NT):
                nc.scalar.activation(sq[:, t, :], g.xn[:, t, :], ACT.Square, accum_out=ss[:, t:t + 1])\
                  .then_inc(S["square"], 1)
            for t in range(NT):
                act.wait_ge(S["xqT_ps"], t + 1)
                nc.scalar.copy(xqT[:, :, t * P:(t + 1) * P],
                               bank[t % 2][:, :].rearrange("p (c n) -> p c n", c=DC)).then_inc(S["xqT_ready"], 1)
            act.wait_ge(S["scales"], 1)
            for j in range(HC):
                act.wait_ge(S["hm_ready"], j + 1)
                if j >= 2:
                    act.wait_ge(S["h_ready"], j - 1)
                nc.scalar.activation(ht[j % 2][:, :], hm[j % 2][:, :], ACT.Tanh, scale=tscale[:, 0:1])\
                  .then_inc(S["th_ready"], 1)

        @block.tensor
        def _(pe):
            mm, tr = nc.tensor.matmul, nc.tensor.transpose
            for t in range(NT):
                pe.wait_ge(S["xq_ready"], t + 1)
                if t >= 2:
                    pe.wait_ge(S["xqT_ready"], t - 1)
                for c in range(DC):
                    last = tr(bank[t % 2][:, c * P:(c + 1) * P], g.xn[:, t, c * P:(c + 1) * P], g.ident[:, :])
                last.then_inc(S["xqT_ps"], 1)
            pe.wait_ge(S["sx_dg"], 1)
            mm(bank[2][:, :], g.ones[:, :], dg[:, :, :].rearrange("p t n -> p (t n)"), start=True, stop=True)\
                .then_inc(S["sxb_ps"], 1)
            pe.wait_ge(S["abs_done"], 2)
            mm(bank[3][:, 0:2], g.ones[:, :], part[:, :], start=True, stop=True).then_inc(S["sums"], 1)
            pe.wait_ge(S["xqT_ready"], NT)
            pe.wait_ge(S["up_q"], 1)
            for j in range(HC):
                if j >= 2:
                    pe.wait_ge(S["hm_ready"], j - 1)
                for c in range(DC):
                    last = mm(bank[j % 2][:, :], upq[:, c, j * P:(j + 1) * P], xqT[:, c, :],
                              start=(c == 0), stop=(c == DC - 1))
                last.then_inc(S["h_ps"], 1)
            pe.wait_ge(S["down_q"], 1)
            pe.wait_ge(S["h_ready"], HC)
            for t in range(NT):
                for j in range(HC):
                    last = mm(bank[4 + t][:, :], hT[:, j, t * P:(t + 1) * P], down[:, j * D:(j + 1) * D],
                              start=(j == 0), stop=(j == HC - 1))
                last.then_inc(S["y_ps"], 1)

        @block.vector
        def _(dve):
            V = nc.vector
            c = Links(dve, own)
            c.link(V.tensor_tensor(g.x[:, :, :], g.x[:, :, :], g.xn[:, :, :], ALU.add))
            dve.wait_ge(S["square"], NT)
            V.tensor_scalar(ss[:, :], ss[:, :], 1.0 / D, 1e-6, ALU.mult, ALU.add).then_inc(S["ss_ready"], 1)
            dve.wait_ge(S["r_ready"], 1)
            dve.wait_ge(loaded["rows"], 32)
            for t in range(NT):
                last = V.scalar_tensor_tensor(out=g.xn[:, t, :], in0=g.xn[:, t, :], scalar=r[:, t:t + 1], in1=nw[:, :],
                                              op0=ALU.mult, op1=ALU.mult)
            c.link(last)
            c.link(V.tensor_reduce(big[:, :], g.xn[:, :, :], AX.X, ALU.max, apply_absolute_value=True))
            c.link(V.tensor_scalar(big[:, :], big[:, :], 1e-8, None, ALU.max))
            c.link(V.tensor_scalar(sx[:, :], big[:, :], 1.0 / QB, None, ALU.mult))
            c.link(V.reciprocal(rbig[:, :], big[:, :]))
            c.link(V.tensor_scalar(rbig[:, :], rbig[:, :], QB, None, ALU.mult))
            for t in range(NT):
                c.link(V.tensor_scalar(g.xn[:, t, :], g.xn[:, t, :], rbig[:, t:t + 1], ROUND, ALU.mult, ALU.add))
                V.tensor_scalar(g.xn[:, t, :], g.xn[:, t, :], ROUND, None, ALU.subtract).then_inc(S["xq_ready"], 1)
            V.tensor_tensor(dg[:, :, :], g.ident[:, :].unsqueeze(1).broadcast_to((P, NT, P)),
                            sx[:, :].unsqueeze(2).broadcast_to((P, NT, P)), ALU.mult).then_inc(S["sx_dg"], 1)
            for n, (buf, name) in enumerate(((up, "up"), (down, "down"))):
                dve.wait_ge(loaded[name], 16)
                V.tensor_reduce(part[:, n:n + 1], buf[:, :], AX.X, ALU.add, apply_absolute_value=True)\
                 .then_inc(S["abs_done"], 1)
            dve.wait_ge(S["sums"], 1)
            c.link(V.tensor_scalar(scale[:, :], bank[3][:, 0:2], 1.0 / (D * HID), 1e-8, ALU.mult, ALU.max))
            c.link(V.tensor_scalar(thr[:, :], scale[:, :], 0.5, None, ALU.mult))
            c.link(V.tensor_scalar(nthr[:, :], scale[:, :], -0.5, None, ALU.mult))
            V.tensor_scalar(tscale[:, :], scale[:, 0:1], -0.5, None, ALU.mult).then_inc(S["scales"], 1)
            c.link(V.tensor_tensor(final[:, :], scale[:, 0:1], scale[:, 1:2], ALU.mult))
            c.link(V.tensor_scalar(final[:, :], final[:, :], 0.5, None, ALU.mult))
            c.link(V.tensor_scalar(above[:, :], up[:, :], thr[:, 0:1], None, ALU.is_gt))
            V.scalar_tensor_tensor(out=upq[:, :, :].rearrange("p c n -> p (c n)"), in0=up[:, :],
                                   scalar=nthr[:, 0:1], in1=above[:, :], op0=ALU.is_lt, op1=ALU.subtract)\
             .then_inc(S["up_q"], 1)
            dve.wait_ge(S["up_q"], 1)
            c.link(V.tensor_scalar(above[:, :], down[:, :], thr[:, 1:2], None, ALU.is_gt))
            V.scalar_tensor_tensor(out=down[:, :], in0=down[:, :], scalar=nthr[:, 1:2], in1=above[:, :],
                                   op0=ALU.is_lt, op1=ALU.subtract).then_inc(S["down_q"], 1)
            dve.wait_ge(S["sxb_ps"], 1)
            c.link(V.tensor_copy(sxb[:, :], bank[2][:, :]))
            for j in range(HC + 1):
                if j < HC:
                    dve.wait_ge(S["h_ps"], j + 1)
                    if j >= 2:
                        dve.wait_ge(S["h_ready"], j - 1)
                    V.tensor_tensor(hm[j % 2][:, :], bank[j % 2][:, :], sxb[:, :], ALU.mult)\
                     .then_inc(S["hm_ready"], 1)
                if j >= 1:
                    dve.wait_ge(S["th_ready"], j)
                    V.scalar_tensor_tensor(out=hT[:, j - 1, :], in0=ht[(j - 1) % 2][:, :], scalar=1.0,
                                           in1=hm[(j - 1) % 2][:, :], op0=ALU.add, op1=ALU.mult)\
                     .then_inc(S["h_ready"], 1)
            for t in range(NT):
                dve.wait_ge(S["y_ps"], t + 1)
                c.link(V.scalar_tensor_tensor(out=sq[:, t, :], in0=bank[4 + t][:, :], scalar=final[:, 0:1],
                                              in1=gam[:, :], op0=ALU.mult, op1=ALU.mult))
                c.link(V.tensor_tensor(g.x[:, t, :], g.x[:, t, :], sq[:, t, :], ALU.add))


def latent_attention_stage(nc, g, dram):
    H, KEYS, DL, QB, R = 16, 4096, 128, 384, 64
    CH = 1024
    NC = KEYS // CH
    KT = CH // P
    STEPS = NT * NC
    QC = QB // P
    ROT = QB // 2
    F32R = mybir.dt.float32r
    kv_tiles = BATCH * KEYS // P
    with ExitStack() as outer:
        mo = Mem(nc, outer, "la")
        kvT_hi, kvT_lo = (mo.sb(n, [P, BATCH * KEYS], F32R) for n in ("kvT_hi", "kvT_lo"))
        kv_hl = mo.sb("kv_hl", [P, kv_tiles, 2 * DL], F32R)

        with ExitStack() as ctx:
            m = Mem(nc, ctx, "kv")
            G = 4
            NG = kv_tiles // G
            raw = [m.sb(f"raw{i}", [P, G, DL]) for i in range(2)]
            cs = [m.sb(f"cs{i}", [P, 2, G, DL]) for i in range(2)]
            turned = [m.sb(f"turned{i}", [P, G, DL]) for i in range(2)]
            roped = [m.sb(f"roped{i}", [P, G, DL]) for i in range(2)]
            tp = [[g.bank[2 * k + i] for i in range(2)] for k in range(2)]
            loaded = [m.sem(f"loaded{i}") for i in range(2)]
            S = {n: m.sem(n) for n in "cos_done sin_done roped_ready hi_ready lo_ready tp_ps copied".split()}
            block = ctx.enter_context(nc.Block())

            @block.sync
            def _(sp):
                for n in range(NG):
                    b, r0 = n * G * P // KEYS, n * G * P % KEYS
                    if n >= 2:
                        sp.wait_ge(S["roped_ready"], n - 1)
                        sp.wait_ge(S["cos_done"], n - 1)
                    sp.dma_start(raw[n % 2][:, :, :], dram["ctx"][b, r0:r0 + G * P, :]
                                 .rearrange("(t p) d -> p t d", p=P)).then_inc(loaded[n % 2], 16)
                    for k, name in enumerate(("cos_k", "sin_k")):
                        sp.dma_start(cs[n % 2][:, k, :, :], dram[name][r0:r0 + G * P, :]
                                     .rearrange("(t p) d -> p t d", p=P)).then_inc(loaded[n % 2], 16)

            @block.gpsimd
            def _(pool):
                for n in range(NG):
                    pool.wait_ge(loaded[n % 2], 48 * (n // 2 + 1))
                    if n >= 2:
                        pool.wait_ge(S["lo_ready"], n - 1)
                    nc.gpsimd.tensor_tensor(roped[n % 2][:, :, :], raw[n % 2][:, :, :], cs[n % 2][:, 0, :, :],
                                            ALU.mult).then_inc(S["cos_done"], 1)

            @block.vector
            def _(dve):
                V = nc.vector
                for n in range(NG):
                    i = n % 2
                    dve.wait_ge(loaded[i], 48 * (n // 2 + 1))
                    h = DL // 2
                    for a in range(2):
                        last = V.tensor_tensor(turned[i][:, :, a * h:(a + 1) * h], raw[i][:, :, (1 - a) * h:(2 - a) * h],
                                               cs[i][:, 1, :, a * h:(a + 1) * h], ALU.mult)
                    last.then_inc(S["sin_done"], 1)
                    dve.wait_ge(S["sin_done"], n + 1)
                    dve.wait_ge(S["cos_done"], n + 1)
                    V.tensor_tensor(roped[i][:, :, :], roped[i][:, :, :], turned[i][:, :, :], ALU.add)\
                     .then_inc(S["roped_ready"], 1)
                    dve.wait_ge(S["roped_ready"], n + 1)
                    hi = kv_hl[:, n * G:(n + 1) * G, 0:DL]
                    V.tensor_copy(hi, roped[i][:, :, :]).then_inc(S["hi_ready"], 1)
                    dve.wait_ge(S["hi_ready"], n + 1)
                    V.tensor_tensor(kv_hl[:, n * G:(n + 1) * G, DL:2 * DL], roped[i][:, :, :], hi.bitcast(F32),
                                    ALU.subtract).then_inc(S["lo_ready"], 1)

            @block.tensor
            def _(pe):
                for n in range(NG):
                    pe.wait_ge(S["lo_ready"], n + 1)
                    if n >= 2:
                        pe.wait_ge(S["copied"], 2 * (n - 1))
                    for k in range(2):
                        for t in range(G):
                            last = nc.tensor.transpose(tp[k][n % 2][:, t * P:(t + 1) * P],
                                                       kv_hl[:, n * G + t, k * DL:(k + 1) * DL].bitcast(F32),
                                                       g.ident[:, :])
                        last.then_inc(S["tp_ps"], 1)

            @block.scalar
            def _(act):
                for n in range(NG):
                    for k, dst in enumerate((kvT_hi, kvT_lo)):
                        act.wait_ge(S["tp_ps"], 2 * n + k + 1)
                        nc.scalar.copy(dst[:, n * G * P:(n + 1) * G * P], tp[k][n % 2][:, :]).then_inc(S["copied"], 1)

        with ExitStack() as ctx:
            m = Mem(nc, ctx, "lh")
            wq, wkc = m.sb("wq", [P, DC, P]), m.sb("wkc", [P, QB + ROT])
            wqr, wkr = m.sb("wqr", [P, QC, R]), m.sb("wkr", [R, DL])
            wkv, wo = m.sb("wkv", [DL, P]), m.sb("wo", [P, D])
            cosq, sinq = m.sb("cosq", [P, QC, SEQ]), m.sb("sinq", [P, QC, SEQ])
            qhk, turned, cxT, lat = (g.xn[:, n, :] for n in range(4))
            qr = m.sb("qr", [R, TOK])
            qb = [m.sb(f"qb{i}", [P, TOK]) for i in range(QC)]
            qh, ql = m.sb("qh", [DL, TOK], F32R), m.sb("ql", [DL, TOK], F32R)
            e = [m.sb(f"e{i}", [P, CH]) for i in range(2)]
            ph = [m.sb(f"ph{i}", [P, KT, P], F32R) for i in range(2)]
            pl = [m.sb(f"pl{i}", [P, KT, P], F32R) for i in range(2)]
            nmc, nm = m.sb("nmc", [P, STEPS]), m.sb("nm", [P, STEPS])
            alpha, part = m.sb("alpha", [P, STEPS]), m.sb("part", [P, STEPS])
            total, rtotal = m.sb("total", [P, STEPS]), m.sb("rtotal", [P, NT])
            acc = [m.sb(f"acc{i}", [P, DL]) for i in range(2)]
            cx = m.sb("cx", [P, NT, DL])
            SC = [g.psum[:, i * CH:(i + 1) * CH] for i in range(2)]
            T = [g.bank[4 + i][:, :].rearrange("p (k n) -> p k n", n=P) for i in range(2)]
            AV = g.bank[6]
            Gb = g.bank[7]
            tables = m.sem("tables")
            qw_loaded, ow_loaded = m.sem("qw_loaded"), m.sem("ow_loaded")
            names = """s_ps chunk_max nm_ready e_ready t_ps hi_ready lo_ready av_ps acc_scaled acc_done cx_ready
                total_ready inverted g_ps g_done turned_ready q_hi""".split()
            S = {n: m.sem(n) for n in names}
            block = ctx.enter_context(nc.Block())

            WHERE = {(1, 0): 0, (2, 0): 1, (3, 0): 2, (3, 1): 3, (4, 0): 4, (5, 0): 5, (6, 0): 6, (7, 0): 7,
                     (7, 1): 8, (8, 0): 9, (9, 0): 10, (10, 0): 11, (11, 0): 12, (12, 0): 13, (13, 0): 14}
            OUT, QSIDE = 6, 9

            def count(h, u):
                if isinstance(h, int) and h in (-1, H):
                    return u - OUT if h < 0 else QSIDE + H * (OUT + QSIDE) - (OUT + QSIDE) + u
                return h * (OUT + QSIDE) + (QSIDE - OUT + u)

            def heads(eng, first, step, last):
                first()
                for s in range(STEPS):
                    step(0, s, False, True)
                with eng.Fori(1, H - 1) as h:
                    for s in range(STEPS):
                        step(h, s, True, True)
                for s in range(STEPS):
                    step(H - 1, s, True, False)
                last()

            def scheduled(s, place, outs, qs):
                u = WHERE.get((s, place))
                return u if u is not None and (outs if u < OUT else qs) else None

            @block.sync
            def _(sp):
                sp.dma_start(cosq[:, :, :], dram["cos_q"].rearrange("(c p) s -> p c s", p=P)).then_inc(tables, 16)
                sp.dma_start(sinq[:, :, :], dram["sin_q"].rearrange("(c p) s -> p c s", p=P)).then_inc(tables, 16)

                def load_q(h):
                    sp.dma_start(wq[:, :, :], dram["L1_xattn_Wq"][bass.ds(h * P, P), :]
                                 .rearrange("p (c n) -> p c n", c=DC)).then_inc(qw_loaded, 16)
                    sp.dma_start(wkc[:, :], dram["L1_xattn_w_kc_q"][bass.ds(h * P, P), :]).then_inc(qw_loaded, 16)
                    sp.dma_start(wqr[:, :, :], dram["L1_xattn_W_qr"][bass.ds(h * P, P), :]
                                 .rearrange("p (c n) -> p c n", c=QC)).then_inc(qw_loaded, 16)
                    sp.dma_start(wkr[:, :], dram["L1_xattn_W_kr"][bass.ds(h * R, R), :]).then_inc(qw_loaded, 16)

                def load_o(h):
                    sp.dma_start(wkv[:, :], dram["L1_xattn_w_kc_kv"][bass.ds(h * P, P), :]).then_inc(ow_loaded, 16)
                    sp.dma_start(wo[:, :], dram["L1_xattn_Wo"][bass.ds(h * P, P), :]).then_inc(ow_loaded, 16)

                load_q(0)
                load_o(0)
                sp.wait_ge(S["g_ps"], count(-1, 14) + 1)
                load_q(1)
                with sp.Fori(1, H - 1) as h:
                    sp.wait_ge(S["g_ps"], count(h, 14) + (1 - OUT - QSIDE))
                    load_q(h + 1)
                    sp.wait_ge(S["g_ps"], count(h, 5) + 1)
                    load_o(h)
                sp.wait_ge(S["g_ps"], count(H - 1, 5) + 1)
                load_o(H - 1)

            @block.tensor
            def _(pe):
                mm, tr = nc.tensor.matmul, nc.tensor.transpose

                def scores(h, s):
                    n = h * STEPS + s
                    if s < 2 and isinstance(h, int) and h == 0:
                        pass
                    else:
                        pe.wait_ge(S["e_ready"], n + (-1))
                    t, c = s // NC, s % NC
                    b = t // 2
                    for k in range(CH // D):
                        k0 = b * KEYS + c * CH + k * D
                        out = SC[s % 2][:, k * D:(k + 1) * D]
                        q = slice(t * P, (t + 1) * P)
                        mm(out, qh[:, q], kvT_hi[:, k0:k0 + D], start=True, stop=False)
                        mm(out, qh[:, q], kvT_lo[:, k0:k0 + D], start=False, stop=False)
                        last = mm(out, ql[:, q], kvT_hi[:, k0:k0 + D], start=False, stop=True)
                    last.then_inc(S["s_ps"], 1)

                def transposes(h, s):
                    n = h * STEPS + s
                    pe.wait_ge(S["e_ready"], n + 1)
                    for j in range(2):
                        if not (isinstance(h, int) and h == 0 and s == 0):
                            pe.wait_ge(S["lo_ready"], 2 * n + (j - 1))
                        for k in range(KT // 2):
                            kk = j * (KT // 2) + k
                            last = tr(T[j][:, k, :], e[s % 2][:, kk * P:(kk + 1) * P], g.ident[:, :])
                        last.then_inc(S["t_ps"], 1)

                def weighted(h, s, n):
                    if not (isinstance(n, int) and n == 0):
                        pe.wait_ge(S["acc_done"], n)
                    t, c = s // NC, s % NC
                    for j in range(2):
                        pe.wait_ge(S["lo_ready"], 2 * n + (j + 1))
                        for k in range(KT // 2):
                            kk = j * (KT // 2) + k
                            tile = (t // 2) * (KEYS // P) + c * KT + kk
                            mm(AV[:, 0:2 * DL], ph[s % 2][:, kk, :], kv_hl[:, tile, :], start=(kk == 0),
                               stop=(kk == KT - 1), skip_group_check=True)
                            last = mm(AV[:, 0:DL], pl[s % 2][:, kk, :], kv_hl[:, tile, 0:DL], start=False,
                                      stop=(kk == KT - 1), skip_group_check=True)
                    last.then_inc(S["av_ps"], 1)

                def use(h, u, chain):
                    n = count(h, u)
                    if not (isinstance(h, int) and h < 0 and u == OUT):
                        pe.wait_ge(S["g_done"], n)
                    if u == 0:
                        pe.wait_ge(S["cx_ready"], NT * chain)
                        for t in range(NT):
                            last = tr(Gb[:, t * P:(t + 1) * P], cx[:, t, :], g.ident[:, :])
                    elif u == 1:
                        pe.wait_ge(ow_loaded, 32 * chain)
                        last = mm(Gb[:, :], wkv[:, :], cxT[:, :], start=True, stop=True)
                    elif u < OUT:
                        t = u - 2
                        last = mm(Gb[:, :], lat[:, t * P:(t + 1) * P], wo[:, :], start=True, stop=True)
                    elif u == 6:
                        pe.wait_ge(qw_loaded, 64 * chain + 64)
                        for c in range(DC):
                            last = mm(Gb[:, :], wq[:, c, :], g.xT[:, c, :], start=(c == 0), stop=(c == DC - 1))
                    elif u < 13:
                        c, rot = (u - 7) // 2, (u - 7) % 2
                        c0 = (c * P + ROT * rot) % QB
                        last = mm(Gb[:, :], wkc[:, c0:c0 + P], qhk[:, :], start=True, stop=True)
                    elif u == 13:
                        pe.wait_ge(S["turned_ready"], QC * chain + QC)
                        for c in range(QC):
                            last = mm(Gb[0:R, :], wqr[:, c, :], qb[c][:, :], start=(c == 0), stop=(c == QC - 1))
                    else:
                        last = mm(Gb[:, :], wkr[:, :], qr[:, :], start=True, stop=True)
                    last.then_inc(S["g_ps"], 1)

                def first():
                    for u in range(OUT, 15):
                        use(-1, u, 0)
                    pe.wait_ge(S["g_done"], count(-1, 14) + 1)
                    scores(0, 0)

                def step(h, s, outs, qs):
                    if s + 1 < STEPS:
                        scores(h, s + 1)
                    elif qs:
                        pe.wait_ge(S["g_done"], count(h, 14) + 1)
                        scores(h + 1, 0)
                    transposes(h, s)
                    chain = h
                    for place in range(2):
                        if place == 1:
                            n = h * STEPS + (s - 1)
                            if not (isinstance(h, int) and h == 0 and s == 0):
                                weighted(h, (s - 1) % STEPS, n)
                        u = scheduled(s, place, outs, qs)
                        if u is not None:
                            use(h, u, chain if u < OUT else chain + 1)

                def last():
                    weighted(H - 1, STEPS - 1, H * STEPS - 1)
                    for u in range(OUT):
                        use(H, u, H)

                pe.wait_ge(tables, 32)
                heads(pe, first, step, last)

            @block.scalar
            def _(act):
                A_ = nc.scalar.activation

                def evacuate(h, u):
                    if u not in (0, 1, 6, 13, 14):
                        return
                    act.wait_ge(S["g_ps"], count(h, u) + 1)
                    if u == 14:
                        nc.scalar.copy(qh[:, :], Gb[:, :]).then_inc(S["q_hi"], 1)
                        return
                    dst, src = {0: (cxT[:, :], Gb[:, :]), 1: (lat[:, :], Gb[:, :]), 6: (qhk[:, :], Gb[:, :]),
                                13: (qr[:, :], Gb[0:R, :])}[u]
                    nc.scalar.copy(dst, src).then_inc(S["g_done"], 1)

                def exps(n, s):
                    act.wait_ge(S["nm_ready"], n + 1)
                    if not isinstance(n, int) or n >= 2:
                        act.wait_ge(S["t_ps"], 2 * n + (-2))
                    if s % NC:
                        A_(alpha[:, s:s + 1], nm[:, s - 1:s], ACT.Exp, scale=-1.0, bias=nm[:, s:s + 1])
                    A_(e[s % 2][:, :], SC[s % 2][:, :], ACT.Exp, bias=nm[:, s:s + 1],
                       accum_out=part[:, s:s + 1]).then_inc(S["e_ready"], 1)

                def first():
                    for u in range(OUT, 15):
                        evacuate(-1, u)
                    exps(0, 0)

                def step(h, s, outs, qs):
                    n = h * STEPS + s
                    if not isinstance(n, int) or n >= 2:
                        act.wait_ge(S["av_ps"], n + (-1))
                    for j in range(2):
                        act.wait_ge(S["t_ps"], 2 * n + (j + 1))
                        nc.scalar.copy(ph[s % 2][:, j * (KT // 2):(j + 1) * (KT // 2), :], T[j][:, :, :])\
                          .then_inc(S["hi_ready"], 1)
                    if s + 1 < STEPS:
                        exps(h * STEPS + (s + 1), s + 1)
                    elif qs:
                        exps(h * STEPS + STEPS, 0)
                    for place in range(2):
                        u = scheduled(s, place, outs, qs)
                        if u is not None and u != 14:
                            evacuate(h, u)
                    if s == STEPS - 2 and qs:
                        act.wait_ge(S["s_ps"], h * STEPS + STEPS)
                        evacuate(h, 14)

                def last():
                    for u in range(OUT):
                        evacuate(H, u)

                heads(act, first, step, last)

            @block.vector
            def _(dve):
                V = nc.vector

                def evacuate(h, u, chain):
                    if u in (0, 1, 6, 13):
                        return
                    dve.wait_ge(S["g_ps"], count(h, u) + 1)
                    if u < OUT:
                        t = u - 2
                        V.tensor_tensor(g.x[:, t, :], g.x[:, t, :], Gb[:, :], ALU.add).then_inc(S["g_done"], 1)
                    elif u < 13:
                        c, rot = (u - 7) // 2, (u - 7) % 2
                        dst = turned if rot else qb[c]
                        tab = sinq if rot else cosq
                        V.tensor_tensor(dst[:, :].rearrange("p (b s) -> p b s", b=BATCH),
                                        Gb[:, :].rearrange("p (b s) -> p b s", b=BATCH),
                                        tab[:, c, :].unsqueeze(1).broadcast_to((P, BATCH, SEQ)), ALU.mult)\
                         .then_inc(S["g_done"], 1)
                        if rot:
                            dve.wait_ge(S["g_done"], count(h, u) + 1)
                            V.tensor_tensor(qb[c][:, :], qb[c][:, :], turned[:, :], ALU.add)\
                             .then_inc(S["turned_ready"], 1)
                            dve.wait_ge(S["turned_ready"], QC * chain + c + 1)
                    else:
                        dve.wait_ge(S["q_hi"], chain + 1)
                        V.tensor_tensor(ql[:, :], Gb[:, :], qh[:, :].bitcast(F32), ALU.subtract)\
                         .then_inc(S["g_done"], 1)

                def maxima(n, s):
                    dve.wait_ge(S["s_ps"], n + 1)
                    if s % NC:
                        V.tensor_reduce(nmc[:, s:s + 1], SC[s % 2][:, :], AX.X, ALU.max, negate=True)\
                         .then_inc(S["chunk_max"], 1)
                        dve.wait_ge(S["chunk_max"], n + 1)
                        V.tensor_tensor(nm[:, s:s + 1], nmc[:, s:s + 1], nm[:, s - 1:s], ALU.min)\
                         .then_inc(S["nm_ready"], 1)
                        dve.wait_ge(S["nm_ready"], n + 1)
                    else:
                        V.tensor_reduce(nm[:, s:s + 1], SC[s % 2][:, :], AX.X, ALU.max, negate=True)\
                         .then_inc(S["nm_ready"], 1)
                        dve.sem_inc(S["chunk_max"], 1)

                def accumulate(n, s):
                    dve.wait_ge(S["av_ps"], n + 1)
                    t, c = s // NC, s % NC
                    a = acc[t % 2]
                    if c:
                        V.scalar_tensor_tensor(out=a[:, :], in0=a[:, :], scalar=alpha[:, s:s + 1], in1=AV[:, 0:DL],
                                               op0=ALU.mult, op1=ALU.add).then_inc(S["acc_scaled"], 1)
                        V.scalar_tensor_tensor(out=total[:, s:s + 1], in0=total[:, s - 1:s],
                                               scalar=alpha[:, s:s + 1], in1=part[:, s:s + 1],
                                               op0=ALU.mult, op1=ALU.add).then_inc(S["total_ready"], 1)
                    else:
                        V.tensor_copy(a[:, :], AV[:, 0:DL]).then_inc(S["acc_scaled"], 1)
                        V.tensor_copy(total[:, s:s + 1], part[:, s:s + 1]).then_inc(S["total_ready"], 1)
                    dve.wait_ge(S["acc_scaled"], n + 1)
                    V.tensor_tensor(a[:, :], a[:, :], AV[:, DL:2 * DL], ALU.add).then_inc(S["acc_done"], 1)
                    dve.wait_ge(S["total_ready"], n + 1)
                    dve.wait_ge(S["acc_done"], n + 1)

                def finish(t, done):
                    s = t * NC + NC - 1
                    V.reciprocal(rtotal[:, t:t + 1], total[:, s:s + 1]).then_inc(S["inverted"], 1)
                    dve.wait_ge(S["inverted"], done + 1)
                    V.tensor_scalar(cx[:, t, :], acc[t % 2][:, :], rtotal[:, t:t + 1], None, ALU.mult)\
                     .then_inc(S["cx_ready"], 1)
                    dve.wait_ge(S["cx_ready"], done + 1)

                def first():
                    dve.wait_ge(tables, 32)
                    for u in range(OUT, 15):
                        evacuate(-1, u, 0)
                    maxima(0, 0)

                def step(h, s, outs, qs):
                    n = h * STEPS + s
                    if s + 1 < STEPS:
                        maxima(h * STEPS + (s + 1), s + 1)
                    elif qs:
                        maxima(h * STEPS + STEPS, 0)
                    if not isinstance(n, int) or n >= 2:
                        dve.wait_ge(S["av_ps"], n + (-1))
                    for j in range(2):
                        dve.wait_ge(S["hi_ready"], 2 * n + (j + 1))
                        half = slice(j * (KT // 2), (j + 1) * (KT // 2))
                        V.tensor_tensor(pl[s % 2][:, half, :], T[j][:, :, :], ph[s % 2][:, half, :].bitcast(F32),
                                        ALU.subtract).then_inc(S["lo_ready"], 1)
                    for place in range(2):
                        u = scheduled(s, place, outs, qs)
                        if place == 1 and not (isinstance(n, int) and n == 0):
                            accumulate(n + (-1), (s - 1) % STEPS)
                            if s % NC == 0 and s:
                                finish(s // NC - 1, h * NT + (s // NC - 1))
                            elif s == 0:
                                finish(NT - 1, h * NT + (-1))
                        if u is not None and u != 14:
                            evacuate(h, u, h + 1)
                    if s == STEPS - 2 and qs:
                        evacuate(h, 14, h + 1)

                def last():
                    accumulate(H * STEPS - 1, STEPS - 1)
                    finish(NT - 1, H * NT - 1)
                    for u in range(OUT):
                        evacuate(H, u, 0)

                heads(dve, first, step, last)


def out_stage(nc, g, src):
    with ExitStack() as ctx:
        m = Mem(nc, ctx, "out")
        stored = m.sem("stored")
        block = ctx.enter_context(nc.Block())

        @block.sync
        def _(sp):
            sp.dma_start(g.out_dram.rearrange("(t p) d -> p t d", p=P), src[:, :, :]).then_inc(stored, 16)
            sp.wait_ge(stored, 16)


class Globals:
    pass


def build(nc, dram, stages):
    g = Globals()
    g.x_dram = dram["x"]
    g.out_dram = dram["out"]
    with ExitStack() as ctx:
        m = Mem(nc, ctx, "g")
        g.x = m.sb("x", [P, NT, D])
        g.xn = m.sb("xn", [P, NT, D])
        g.xT = m.sb("xT", [P, DC, TOK])
        g.ident = m.sb("ident", [P, P])
        g.ones = m.sb("ones", [P, P])
        g.triu = m.sb("triu", [P, P])
        g.half = m.sb("half", [P, 16])
        g.psum = ctx.enter_context(nc.psum_tensor("psum", [P, 8 * D], F32))
        g.bank = [g.psum[:, i * D:(i + 1) * D] for i in range(8)]
        constants_stage(nc, g)
        if 1 in stages:
            norm_stage(nc, g, "n1", 1e-5)
            with ExitStack() as c2:
                kv = Mem(nc, c2, "kv0").sb("ctxT", [P, 1, TOK])
                attention_stage(nc, g, "l0x", dram["L0_xattn_Wq"], dram["L0_xattn_Wkv"][:, 0:D],
                                dram["L0_xattn_Wkv"][:, D:2 * D], dram["L0_xattn_Wout"], kv, dram["ctxT"], None, FMIN)
        if 2 in stages:
            norm_stage(nc, g, "n2", 1e-5)
            delta_stage(nc, g, dram)
        if 3 in stages:
            norm_stage(nc, g, "n3", 1e-5)
            expert_stage(nc, g, dram)
        if 4 in stages:
            norm_stage(nc, g, "n4", 1e-5)
            latent_attention_stage(nc, g, dram)
        if 5 in stages:
            norm_stage(nc, g, "n5", 1e-5)
            w = dram["L1_attn_Wqkv"]
            attention_stage(nc, g, "l1a", w[:, 0:D], w[:, D:2 * D], w[:, 2 * D:3 * D], dram["L1_attn_Wo"],
                            g.xT, None, (dram["L1_attn_bqkv"], dram["L1_attn_bqk_cols"], dram["L1_attn_bo"]), -10000.0)
        if 6 in stages:
            norm_stage(nc, g, "n6", 1e-5, transpose=False)
            ternary_stage(nc, g, dram)
        out_stage(nc, g, g.x)


def rope_tables(length, dim):
    f32 = np.float32
    inv = f32(1.0) / np.power(f32(10000.0), np.arange(0, dim, 2, dtype=f32) / f32(dim)).astype(f32)
    angle = np.arange(length, dtype=f32)[:, None] * inv[None, :].astype(f32)
    sin, cos = np.repeat(np.sin(angle), 2, axis=-1), np.repeat(np.cos(angle), 2, axis=-1)
    sin[:, 0:dim // 2] *= f32(-1.0)
    return sin, cos


def layouts(inputs):
    a = {k: np.asarray(v) for k, v in inputs.items()}
    o = {"x": a["x"].reshape(TOK, D)}
    o["ctxT"] = a["ctx_512"].transpose(0, 2, 1)
    o["L0_xattn_Wq"] = a["L0_xattn_Wq"].T
    o["L0_xattn_Wkv"] = a["L0_xattn_Wkv_expand"].T
    o["L0_xattn_Wout"] = a["L0_xattn_Wout"].T
    parts = [a["L0_attn_W_qkv"][:, n * 2048:(n + 1) * 2048] for n in range(3)] + [a["L0_attn_W_z"]]
    o["L0_attn_W_heads"] = np.stack([p.reshape(D, 16, P) for p in parts], 2).transpose(1, 0, 2, 3).reshape(16 * D, 4 * P)
    o["L0_attn_W_ab"] = np.concatenate([a["L0_attn_W_b"], a["L0_attn_W_a"]], 1)
    o["L0_attn_W_out"] = a["L0_attn_W_out"]
    o["L0_attn_conv"] = a["L0_attn_conv_w"].reshape(3, 16, P, 4).transpose(2, 1, 0, 3).reshape(P, 16 * 12)
    for n in ("A_log", "dt_bias", "norm_w"):
        o["L0_attn_" + n] = a["L0_attn_" + n]
    o["L0_ffn_router"] = a["L0_ffn_router_w"].T
    gu = np.concatenate([a["L0_ffn_w_gate"], a["L0_ffn_w_up"]], 2)
    o["L0_ffn_gate_up"] = gu.reshape(64, DC, P, 384).transpose(0, 2, 1, 3).reshape(64 * P, DC * 384)
    o["L0_ffn_w_down"] = a["L0_ffn_w_down"].reshape(64, 2, 96, D).transpose(0, 2, 1, 3).reshape(64 * 96, 2 * D)
    o["L1_ffn_up"] = a["L1_ffn_weight_up"].T
    o["L1_ffn_down"] = a["L1_ffn_weight_down"].T
    o["L1_ffn_norm_weight"] = a["L1_ffn_norm_weight"]
    o["L1_ffn_gamma"] = a["L1_ffn_gamma"]
    o["ctx"] = a["ctx_512"]
    o["L1_xattn_Wq"] = a["L1_xattn_Wq"].reshape(16, P, DC, P).transpose(0, 3, 2, 1).reshape(16 * P, DC * P)
    wkc = a["L1_xattn_w_kc_q"].reshape(16 * P, 384)
    o["L1_xattn_w_kc_q"] = np.concatenate([wkc, wkc[:, 0:192]], 1)
    o["L1_xattn_W_qr"] = a["L1_xattn_W_qr"].reshape(16, 3, P, 64).transpose(0, 2, 1, 3).reshape(16 * P, 3 * 64)
    o["L1_xattn_W_kr"] = a["L1_xattn_W_kr"].transpose(0, 2, 1).reshape(16 * 64, P)
    o["L1_xattn_w_kc_kv"] = a["L1_xattn_w_kc_kv"].transpose(0, 2, 1).reshape(16 * P, P)
    o["L1_xattn_Wo"] = a["L1_xattn_Wo"].T
    o["sin_k"], o["cos_k"] = rope_tables(4096, P)
    sin_q, cos_q = rope_tables(SEQ, 384)
    o["sin_q"], o["cos_q"] = sin_q.T, cos_q.T
    o["L1_attn_Wqkv"] = a["L1_attn_Wqkv"]
    o["L1_attn_bqkv"] = a["L1_attn_bqkv"]
    o["L1_attn_bqk_cols"] = a["L1_attn_bqkv"][0:2 * D].reshape(2 * DC, P).T
    o["L1_attn_Wo"] = a["L1_attn_Wo"]
    o["L1_attn_bo"] = a["L1_attn_bo"]
    return o


STAGES = (1, 2, 3, 4, 5, 6)


def kernel(**inputs):
    import concourse.bacc as bacc
    from concourse.bass_utils import run_bass_kernel_spmd

    nc = bacc.Bacc("TRN2", target_bir_lowering=False, num_devices=1)
    arrays, dram = {}, {}
    for name, a in layouts(inputs).items():
        a = np.ascontiguousarray(a)
        arrays[f"in_{name}"] = a
        dram[name] = nc.dram_tensor(f"in_{name}", a.shape, mybir.dt.from_np(a.dtype), kind="ExternalInput").ap()
    dram["out"] = nc.dram_tensor("out_0", (TOK, D), F32, kind="ExternalOutput").ap()
    dram["xn_rows"] = nc.dram_tensor("xn_rows", (TOK, D), F32, kind="Internal").ap()
    dram["y_rows"] = nc.dram_tensor("y_rows", (64 * 128 + 1, D), F32, kind="Internal").ap()
    build(nc, dram, STAGES)
    r = run_bass_kernel_spmd(nc, [arrays], core_ids=[0])
    return r.results[0]["out_0"].reshape(BATCH, SEQ, D)
```

```python
import numpy as np
import concourse.bass as bass
from concourse import mybir
from contextlib import ExitStack

F32 = mybir.dt.float32
BF16 = mybir.dt.bfloat16
I32 = mybir.dt.int32
U32 = mybir.dt.uint32
ALU = mybir.AluOpType
ACT = mybir.ActivationFunctionType
AX = mybir.AxisListType

P = 128
BATCH, SEQ, D = 2, 256, 512
TOK = BATCH * SEQ
NT = TOK // P
DC = D // P
FMIN = float(np.finfo(np.float32).min)


class Links:

    def __init__(self, eng, sem, base=0):
        self.eng, self.sem, self.base, self.n = eng, sem, base, 0

    def link(self, ins):
        ins.then_inc(self.sem, 1)
        self.n += 1
        self.eng.wait_ge(self.sem, self.base + self.n)


class Mem:

    def __init__(self, nc, ctx, tag):
        self.nc, self.ctx, self.tag = nc, ctx, tag
        self.sems = []
        ctx.callback(self.clear)

    def clear(self):
        if self.sems:
            with self.nc.Block() as block:

                @block.gpsimd
                def _(pool):
                    for s in self.sems[0::5]:
                        pool.sem_clear(s)

                @block.sync
                def _(sp):
                    for s in self.sems[1::5]:
                        sp.sem_clear(s)

                @block.vector
                def _(dve):
                    for s in self.sems[2::5]:
                        dve.sem_clear(s)

                @block.scalar
                def _(act):
                    for s in self.sems[3::5]:
                        act.sem_clear(s)

                @block.tensor
                def _(pe):
                    for s in self.sems[4::5]:
                        pe.sem_clear(s)

    def sb(self, name, shape, dt=F32):
        return self.ctx.enter_context(self.nc.sbuf_tensor(f"{self.tag}_{name}", shape, dt))

    def sem(self, name):
        s = self.ctx.enter_context(self.nc.semaphore(f"{self.tag}_{name}"))
        self.sems.append(s)
        return s


def constants_stage(nc, g):
    with ExitStack() as ctx:
        m = Mem(nc, ctx, "const")
        made = m.sem("made")
        loaded = m.sem("loaded")
        block = ctx.enter_context(nc.Block())

        @block.sync
        def _(sp):
            sp.dma_start(g.x[:, :, :], g.x_dram.rearrange("(t p) d -> p t d", p=P)).then_inc(loaded, 16)
            sp.wait_ge(loaded, 16)

        @block.gpsimd
        def _(pool):
            pool.memset(g.ident[:, :], 0.0).then_inc(made, 1)
            pool.memset(g.ones[:, :], 1.0).then_inc(made, 1)
            pool.memset(g.triu[:, :], 1.0).then_inc(made, 1)
            pool.memset(g.half[:, :], -0.5).then_inc(made, 1)
            pool.wait_ge(made, 4)
            pool.affine_select(out=g.ident[:, :], in_=g.ident[:, :], compare_op=ALU.not_equal, fill=1.0,
                               base=0, pattern=[[-1, P]], channel_multiplier=1).then_inc(made, 1)
            pool.affine_select(out=g.triu[:, :], in_=g.triu[:, :], compare_op=ALU.is_ge, fill=0.0,
                               base=0, pattern=[[1, P]], channel_multiplier=-1).then_inc(made, 1)
            pool.wait_ge(made, 6)


def norm_stage(nc, g, tag, eps, transpose=True):
    with ExitStack() as ctx:
        m = Mem(nc, ctx, tag)
        stats = m.sb("stats", [P, NT, 6])
        mv = m.sb("mv", [P, NT, 2])
        var = m.sb("var", [P, NT])
        rstd = m.sb("rstd", [P, NT])
        tp = [g.bank[i][:, :].rearrange("p (c n) -> p c n", c=DC) for i in range(2)]
        own = m.sem("own")
        var_ready = m.sem("var_ready")
        rstd_ready = m.sem("rstd_ready")
        xn_ready = m.sem("xn_ready")
        tp_ready = m.sem("tp_ready")
        copied = m.sem("copied")
        block = ctx.enter_context(nc.Block())

        @block.vector
        def _(dve):
            c = Links(dve, own)
            for t in range(NT):
                nc.vector.bn_stats(stats[:, t, :], g.x[:, t, :]).then_inc(own, 1)
            dve.wait_ge(own, NT)
            for t in range(NT):
                nc.vector.bn_aggr(mv[:, t, :], stats[:, t, :]).then_inc(own, 1)
            dve.wait_ge(own, 2 * NT)
            nc.vector.tensor_scalar(var[:, :], mv[:, :, 1], eps, None, ALU.add).then_inc(var_ready, 1)
            dve.wait_ge(rstd_ready, 1)
            for t in range(NT):
                nc.vector.tensor_scalar(g.xn[:, t, :], g.x[:, t, :], mv[:, t, 0:1], rstd[:, t:t + 1],
                                        ALU.subtract, ALU.mult).then_inc(xn_ready, 1)

        @block.gpsimd
        def _(pool):
            pool.wait_ge(var_ready, 1)
            nc.gpsimd.tensor_tensor(rstd[:, :], var[:, :], g.half[:, 0:NT], ALU.pow).then_inc(rstd_ready, 1)

        @block.tensor
        def _(pe):
            for t in range(NT if transpose else 0):
                pe.wait_ge(xn_ready, t + 1)
                if t >= 2:
                    pe.wait_ge(copied, t - 1)
                for c in range(DC):
                    last = nc.tensor.transpose(tp[t % 2][:, c, :], g.xn[:, t, c * P:(c + 1) * P], g.ident[:, :])
                last.then_inc(tp_ready, 1)

        @block.scalar
        def _(act):
            for t in range(NT if transpose else 0):
                act.wait_ge(tp_ready, t + 1)
                nc.scalar.copy(g.xT[:, :, t * P:(t + 1) * P], tp[t % 2][:, :, :]).then_inc(copied, 1)


def attention_stage(nc, g, tag, wq, wk, wv, wo, kvT, kv_dram, bias, masked_score, prefetch=None):
    H, HD = 16, 32
    SCALE = HD ** -0.5
    KC = kvT.shape[1]
    UNITS = 8
    KT = SEQ // P
    DEEP = 4
    T_LAG, AV_LAG, OUT_LAG = 2, 3, 4
    with ExitStack() as ctx:
        m = Mem(nc, ctx, tag)
        wq_sb, wo_sb = m.sb("wq", [P, DC, D]), m.sb("wo", [P, DC, D])
        wk_sb, wv_sb = m.sb("wk", [P, KC, D]), m.sb("wv", [P, KC, D])
        qT, kT = m.sb("qT", [P, DC, TOK]), m.sb("kT", [P, DC, TOK])
        v = m.sb("v", [P, NT, D])
        O, OT = m.sb("O", [P, NT, D]), m.sb("OT", [P, DC, TOK])
        qs, ks = m.sb("qs", [P, TOK]), m.sb("ks", [P, TOK])
        keep = m.sb("keep", [P, KT, SEQ])
        fill = m.sb("fill", [P, KT, SEQ])
        E = [m.sb(f"E{i}", [P, KT, SEQ]) for i in range(DEEP)]
        ET = [m.sb(f"ET{i}", [P, KT, KT, P]) for i in range(2)]
        nmax = m.sb("nmax", [P, UNITS, KT])
        total = m.sb("total", [P, UNITS, KT])
        rtotal = m.sb("rtotal", [P, UNITS, KT])
        if bias:
            bq, bk = m.sb("bq", [P, DC]), m.sb("bk", [P, DC])
            bv, bo = m.sb("bv", [P, D]), m.sb("bo", [P, D])
        bank = g.bank
        S = [bank[i][:, :].rearrange("p (t k) -> p t k", t=KT) for i in range(2)]
        ETp = [bank[2 + i][:, :].rearrange("p (k q n) -> p k q n", k=KT, q=KT) for i in range(2)]
        AV = [bank[4 + i][:, 0:KT * P].rearrange("p (t n) -> p t n", t=KT) for i in range(DEEP)]
        loads = {n: m.sem(f"loaded_{n}") for n in ["kv", "wq", "wk", "wv", "wo", "bias"]}
        masks = m.sem("masks")
        proj, proj_out = m.sem("proj"), m.sem("proj_out")
        staged = m.sem("staged")
        s_ready, s_free = m.sem("s_ready"), m.sem("s_free")
        max_ready, e_ready = m.sem("max_ready"), m.sem("e_ready")
        et_ready, et_copied = m.sem("et_ready"), m.sem("et_copied")
        av_ready, av_out = m.sem("av_ready"), m.sem("av_out")
        filled, inverted = m.sem("filled"), m.sem("inverted")
        ot_ready, ot_copied = m.sem("ot_ready"), m.sem("ot_copied")
        y_ready, y_added = m.sem("y_ready"), m.sem("y_added")
        block = ctx.enter_context(nc.Block())

        @block.sync
        def _(sp):
            if kv_dram is not None:
                for b in range(BATCH):
                    sp.dma_start(kvT[:, 0, b * SEQ:(b + 1) * SEQ], kv_dram[b, :, 0:SEQ]).then_inc(loads["kv"], 16)
            sp.dma_start(wk_sb[:, :, :], wk.rearrange("(c p) n -> p c n", p=P)).then_inc(loads["wk"], 16)
            sp.dma_start(wv_sb[:, :, :], wv.rearrange("(c p) n -> p c n", p=P)).then_inc(loads["wv"], 16)
            sp.dma_start(wq_sb[:, :, :], wq.rearrange("(c p) n -> p c n", p=P)).then_inc(loads["wq"], 16)
            if bias:
                bqkv, bqk_cols, bout = bias
                sp.dma_start(bq[:, :], bqk_cols[:, 0:DC]).then_inc(loads["bias"], 16)
                sp.dma_start(bk[:, :], bqk_cols[:, DC:2 * DC]).then_inc(loads["bias"], 16)
                sp.dma_start(bv[:, :], bqkv[2 * D:3 * D].partition_broadcast(P)).then_inc(loads["bias"], 16)
                sp.dma_start(bo[:, :], bout.partition_broadcast(P)).then_inc(loads["bias"], 16)
            sp.dma_start(wo_sb[:, :, :], wo.rearrange("(c p) n -> p c n", p=P)).then_inc(loads["wo"], 16)
            if prefetch is not None:
                prefetch(sp)
            for s in loads.values():
                if s is loads["kv"]:
                    if kv_dram is not None:
                        sp.wait_ge(s, 16 * BATCH)
                elif s is loads["bias"]:
                    if bias:
                        sp.wait_ge(s, 64)
                else:
                    sp.wait_ge(s, 16)

        @block.gpsimd
        def _(pool):
            pool.memset(keep[:, :, :], 1.0).then_inc(masks, 1)
            pool.memset(fill[:, :, :], 0.0).then_inc(masks, 1)
            pool.wait_ge(masks, 2)
            for buf, value in ((keep, 0.0), (fill, masked_score)):
                pool.affine_select(out=buf[:, :, :], in_=buf[:, :, :], compare_op=ALU.is_ge, fill=value, base=0,
                                   pattern=[[P, KT], [-1, SEQ]], channel_multiplier=1).then_inc(masks, 1)

        @block.tensor
        def _(pe):
            n = 0

            def bank_free():
                if n >= 4:
                    pe.wait_ge(proj_out, n - 3)

            if kv_dram is not None:
                pe.wait_ge(loads["kv"], 16 * BATCH)
            pe.wait_ge(loads["wk"], 16)
            for o in range(DC):
                bank_free()
                for c in range(KC):
                    last = nc.tensor.matmul(bank[n % 4][:, :], wk_sb[:, c, o * P:(o + 1) * P], kvT[:, c, :],
                                            start=(c == 0), stop=(c == KC - 1))
                last.then_inc(proj, 1)
                n += 1
            pe.wait_ge(loads["wv"], 16)
            for t in range(NT):
                bank_free()
                for c in range(KC):
                    last = nc.tensor.matmul(bank[n % 4][:, :], kvT[:, c, t * P:(t + 1) * P], wv_sb[:, c, :],
                                            start=(c == 0), stop=(c == KC - 1))
                last.then_inc(proj, 1)
                n += 1
            pe.wait_ge(loads["wq"], 16)
            for o in range(DC):
                bank_free()
                for c in range(DC):
                    last = nc.tensor.matmul(bank[n % 4][:, :], wq_sb[:, c, o * P:(o + 1) * P], g.xT[:, c, :],
                                            start=(c == 0), stop=(c == DC - 1))
                last.then_inc(proj, 1)
                n += 1
            pe.wait_ge(proj_out, n)

            with pe.Fori(0, DC) as i:
                def scores(u):
                    j, b = u // 2, u % 2
                    if u == 0:
                        pe.wait_ge(staged, 2 * i + 2)
                    pe.wait_ge(s_free, UNITS * i + u + 1)
                    r = slice(j * HD, (j + 1) * HD)
                    for t in range(KT):
                        q0 = b * SEQ + t * P
                        last = nc.tensor.matmul(S[u % 2][:, t, :], qs[r, q0:q0 + P], ks[r, b * SEQ:(b + 1) * SEQ],
                                                start=True, stop=True)
                    last.then_inc(s_ready, 1)

                def transposes(u):
                    pe.wait_ge(e_ready, UNITS * i + u + 1)
                    for k in range(KT):
                        for t in range(KT):
                            last = nc.tensor.transpose(ETp[u % 2][:, k, t, :], E[u % DEEP][:, t, k * P:(k + 1) * P],
                                                       g.ident[:, :])
                    last.then_inc(et_ready, 1)

                def weighted(u):
                    b = u % 2
                    pe.wait_ge(av_out, UNITS * i + u + 1)
                    pe.wait_ge(et_copied, UNITS * i + u + 1)
                    for t in range(KT):
                        for k in range(KT):
                            last = nc.tensor.matmul(AV[u % DEEP][:, t, :], ET[u % 2][:, k, t, :],
                                                    v[:, b * KT + k, bass.ds(i * P, P)],
                                                    start=(k == 0), stop=(k == KT - 1))
                    last.then_inc(av_ready, 1)

                for s in range(UNITS + AV_LAG):
                    if s < UNITS:
                        scores(s)
                    if 0 <= s - T_LAG < UNITS:
                        transposes(s - T_LAG)
                    if s >= AV_LAG:
                        weighted(s - AV_LAG)

            pe.wait_ge(av_out, DC * UNITS + DEEP)
            for t in range(NT):
                if t >= 2:
                    pe.wait_ge(ot_copied, t - 1)
                for c in range(DC):
                    last = nc.tensor.transpose(bank[t % 2][:, c * P:(c + 1) * P], O[:, t, c * P:(c + 1) * P],
                                               g.ident[:, :])
                last.then_inc(ot_ready, 1)
            pe.wait_ge(ot_copied, NT)
            pe.wait_ge(loads["wo"], 16)
            for t in range(NT):
                for c in range(DC):
                    last = nc.tensor.matmul(bank[4 + t][:, :], OT[:, c, t * P:(t + 1) * P], wo_sb[:, c, :],
                                            start=(c == 0), stop=(c == DC - 1))
                last.then_inc(y_ready, 1)

        @block.scalar
        def _(act):
            if bias:
                act.wait_ge(loads["bias"], 64)
            for n in range(3 * DC):
                kind, o = n // DC, n % DC
                act.wait_ge(proj, n + 1)
                if n:
                    act.wait_ge(proj_out, n)
                if kind == 1:
                    if bias:
                        continue
                    nc.scalar.copy(v[:, o, :], bank[n % 4][:, :]).then_inc(proj_out, 1)
                else:
                    dst, b = ((kT, "bk"), None, (qT, "bq"))[kind]
                    if bias:
                        bb = bk if b == "bk" else bq
                        nc.scalar.activation(dst[:, o, :], bank[n % 4][:, :], ACT.Identity,
                                             bias=bb[:, o:o + 1]).then_inc(proj_out, 1)
                    else:
                        nc.scalar.copy(dst[:, o, :], bank[n % 4][:, :]).then_inc(proj_out, 1)
            act.wait_ge(proj_out, 3 * DC)

            with act.Fori(0, DC) as i:
                act.wait_ge(s_free, UNITS * i + 2)
                nc.scalar.copy(qs[:, :], qT[:, :, :].rearrange("p c n -> p (c n)")[:, bass.ds(i * TOK, TOK)])\
                  .then_inc(staged, 1)
                nc.scalar.copy(ks[:, :], kT[:, :, :].rearrange("p c n -> p (c n)")[:, bass.ds(i * TOK, TOK)])\
                  .then_inc(staged, 1)

                def exps(u):
                    act.wait_ge(max_ready, UNITS * i + u + 1)
                    for t in range(KT):
                        e = E[u % DEEP][:, t, :]
                        last = nc.scalar.activation(e, e, ACT.Exp, bias=nmax[:, u, t:t + 1],
                                                    accum_out=total[:, u, t:t + 1])
                    last.then_inc(e_ready, 1)

                def copies(u):
                    act.wait_ge(et_ready, UNITS * i + u + 1)
                    if u >= 2:
                        act.wait_ge(av_ready, UNITS * i + u - 1)
                    nc.scalar.copy(ET[u % 2][:, :, :, :], ETp[u % 2]).then_inc(et_copied, 1)

                for s in range(UNITS + 1):
                    if s < UNITS:
                        exps(s)
                    if s >= 1:
                        copies(s - 1)

            for t in range(NT):
                act.wait_ge(ot_ready, t + 1)
                nc.scalar.copy(OT[:, :, t * P:(t + 1) * P],
                               bank[t % 2][:, :].rearrange("p (c n) -> p c n", c=DC)).then_inc(ot_copied, 1)

        @block.vector
        def _(dve):
            if bias:
                dve.wait_ge(loads["bias"], 64)
                for t in range(NT):
                    n = DC + t
                    dve.wait_ge(proj, n + 1)
                    dve.wait_ge(proj_out, n)
                    nc.vector.tensor_tensor(v[:, t, :], bank[n % 4][:, :], bv[:, :], ALU.add).then_inc(proj_out, 1)
            dve.wait_ge(masks, 4)
            dve.sem_inc(s_free, 2)
            dve.sem_inc(av_out, DEEP)
            with dve.Fori(0, DC) as i:

                def mask_and_max(u):
                    dve.wait_ge(s_ready, UNITS * i + u + 1)
                    if u >= DEEP:
                        dve.wait_ge(et_ready, UNITS * i + u - DEEP + 1)
                    e = E[u % DEEP]
                    nc.vector.scalar_tensor_tensor(out=e[:, :, :], in0=S[u % 2], scalar=SCALE, in1=keep[:, :, :],
                                                   op0=ALU.mult, op1=ALU.mult).then_inc(s_free, 1)
                    dve.wait_ge(s_free, UNITS * i + u + 3)
                    nc.vector.tensor_tensor(e[:, :, :], e[:, :, :], fill[:, :, :], ALU.add).then_inc(filled, 1)
                    dve.wait_ge(filled, UNITS * i + u + 1)
                    nc.vector.tensor_reduce(nmax[:, u, :], e[:, :, :], AX.X, ALU.max, negate=True)\
                      .then_inc(max_ready, 1)

                def normalise(u):
                    j, b = u // 2, u % 2
                    dve.wait_ge(av_ready, UNITS * i + u + 1)
                    nc.vector.reciprocal(rtotal[:, u, :], total[:, u, :]).then_inc(inverted, 1)
                    dve.wait_ge(inverted, UNITS * i + u + 1)
                    for t in range(KT):
                        last = nc.vector.tensor_scalar(O[:, b * KT + t, bass.ds(i * P + j * HD, HD)],
                                                       AV[u % DEEP][:, t, j * HD:(j + 1) * HD],
                                                       rtotal[:, u, t:t + 1], None, ALU.mult)
                    last.then_inc(av_out, 1)

                for s in range(UNITS + OUT_LAG):
                    if s < UNITS:
                        mask_and_max(s)
                    if s >= OUT_LAG:
                        normalise(s - OUT_LAG)
            for t in range(NT):
                dve.wait_ge(y_ready, t + 1)
                nc.vector.tensor_tensor(g.x[:, t, :], g.x[:, t, :], bank[4 + t][:, :], ALU.add).then_inc(y_added, 1)
                if bias:
                    dve.wait_ge(y_added, 2 * t + 1)
                    nc.vector.tensor_tensor(g.x[:, t, :], g.x[:, t, :], bo[:, :], ALU.add).then_inc(y_added, 1)


def delta_stage(nc, g, dram):
    H, DK, DV, TAPS = 16, 128, 128, 4
    EPS = 1e-6
    T2 = 2 * NT
    LEVELS = 6
    HALF = P // 2
    BIG = 1e30
    CW, BETA, HBETA, CUM, NCUMX, CREST, NBX, GN, NS = 0, 12, 16, 20, 24, 28, 32, 36, 40
    NG = NT * H
    with ExitStack() as ctx:
        m = Mem(nc, ctx, "dn")
        w = [m.sb(f"w{i}", [P, DC, 4 * P]) for i in range(2)]
        wo = m.sb("wo", [P, H // 2, D])
        scal = m.sb("scal", [P, H, NS])
        hs = [m.sb(f"hs{i}", [P, 2, NS]) for i in range(2)]
        wab = m.sb("wab", [P, DC, 2 * H])
        dtb, alog, expa = m.sb("dtb", [P, H]), m.sb("alog", [P, H]), m.sb("expa", [P, H])
        ab = m.sb("ab", [P, NT, 2 * H])
        th, ga, gb, gneg = (m.sb(n, [P, NT, H]) for n in ("th", "ga", "gb", "gneg"))
        cum, last_cum = m.sb("cum", [P, NT, H]), m.sb("last_cum", [P, NT, H])
        normw = m.sb("normw", [P, DV])
        low = m.sb("low", [P, P])
        up = m.sb("up", [P, P])
        m0 = m.sb("m0", [P, P])
        pairm = m.sb("pairm", [P, LEVELS, HALF])
        yk, yv = m.sb("yk", [P, TOK]), m.sb("yv", [P, TOK])
        tn = [m.sb(f"tn{n}", [P, TOK]) for n in "kqv"]
        sq = [m.sb(f"sq{n}", [P, TOK]) for n in "kq"]
        ss = m.sb("ss", [P, 2, NT])
        zt = m.sb("zt", [P, NT, DV])
        dg = m.sb("dg", [P, NT, P])
        e1, e2 = m.sb("e1", [P, NT, P]), m.sb("e2", [P, NT, P])
        kh = m.sb("kh", [P, NT, DK])

        def two(name, shape):
            return [m.sb(f"{name}{i}", shape) for i in range(2)]

        yq, khT, kej = two("yq", [P, T2, P]), two("khT", [P, T2, P]), two("kej", [P, T2, DK])
        bv, zs, rs = two("bv", [P, T2, DV]), two("zs", [P, T2, DV]), two("rs", [P, 2, 2, NT])
        A, PT = two("A", [P, T2, P]), two("PT", [P, T2, P])
        X, Y = two("X", [P, T2, P]), two("Y", [P, T2, P])
        p1 = m.sb("p1", [P, T2, HALF])
        R = m.sb("R", [P, 2 * BATCH, DV])
        St = m.sb("St", [P, 2 * BATCH, DV])
        U = m.sb("U", [P, T2, DV])
        o, osq = (g.xn[:, i * 2:(i + 1) * 2, :].rearrange("p a (t n) -> p (a t) n", n=DV) for i in range(2))
        core = osq
        oss, rs2, f = m.sb("oss", [P, T2]), m.sb("rs2", [P, T2]), m.sb("f", [P, T2])
        coreT = m.sb("coreT", [P, H, NT, P])
        bank = g.bank

        def tiles(b):
            return b[:, :].rearrange("p (t n) -> p t n", t=NT)

        def half_tiles(b):
            return b[:, :].rearrange("p (t n) -> p t n", t=T2)

        def cols(p, j, name):
            return hs[p][:, j, name:name + NT].unsqueeze(2).broadcast_to((P, NT, P))

        def two_banks(i):
            return g.psum[:, i * D:(i + 2) * D].rearrange("p (t n) -> p t n", t=T2)

        def bank_k(j):
            return 1 - j

        loaded, wo_loaded = m.sem("loaded"), m.sem("wo_loaded")
        own, pool_own = m.sem("own"), m.sem("pool_own")
        w_loaded = [m.sem(f"w_loaded{i}") for i in range(2)]
        front_own, norm_own = m.sem("front_own"), m.sem("norm_own")
        names = """ab ab_out ab_exp ab_tanh g_exp g_ln gneg cums cums_out cum_exp scal_ready
            hs_ready k_ps k_conv k_tanh k_silu k_square q_ps q_conv q_tanh q_silu q_square v_ps v_conv v_tanh v_silu
            z_ps z_tanh z_mul zs_ready dg_ready gb_ps e1_arg e2_arg e1_ready e2_ready ktok kh_ready
            sums ss_ready rs_ready vtok bv_ready khT_ps khT_ready kej_ready kk kq a_ready a_pairs x1 pt_ready
            y1_ps y1_ready p1_ps p1_ready yp_ps y_ready xt_ps x_ready u0_ps u0_ready s_ps s_ready
            ks_ps qs_ps r_ready u1_ps u1_ready o_ps o_copied o_ready f_arg f_pow core_ready
            coreT_ps coreT_ready out_ps out_added""".split()
        S = {n: m.sem(n) for n in names}

        def wait(eng, name, h, k=1, per=1):
            v = per * h + k
            if not isinstance(v, int) or v > 0:
                eng.wait_ge(S[name], v)

        block = ctx.enter_context(nc.Block())

        def w_heads(h):
            return dram["L0_attn_W_heads"][bass.ds(h * D, D), :].rearrange("(c p) n -> p c n", p=P)

        def pipeline(eng, turn):
            turn(0, None, None, 0)
            turn(1, 0, None, 1)
            with eng.Fori(1, H // 4) as r:
                turn(2 * r, 2 * r - 1, 2 * r - 2, 0)
                turn(2 * r + 1, 2 * r, 2 * r - 1, 1)
            turn(None, H // 2 - 1, H // 2 - 2, 0)
            turn(None, None, H // 2 - 1, 1)

        def tile(j, t):
            return j * NT + t

        @block.sync
        def _(sp):
            sp.dma_start(wab[:, :, :], dram["L0_attn_W_ab"].rearrange("(c p) n -> p c n", p=P)).then_inc(loaded, 16)
            sp.dma_start(dtb[:, :], dram["L0_attn_dt_bias"].partition_broadcast(P)).then_inc(loaded, 16)
            sp.dma_start(alog[:, :], dram["L0_attn_A_log"].partition_broadcast(P)).then_inc(loaded, 16)
            sp.dma_start(normw[:, :], dram["L0_attn_norm_w"].partition_broadcast(P)).then_inc(loaded, 16)
            sp.dma_start(scal[:, :, CW:CW + 3 * TAPS], dram["L0_attn_conv"].rearrange("p (h n) -> p h n", h=H))\
              .then_inc(loaded, 16)
            sp.wait_ge(loaded, 80)
            for h in range(2):
                sp.dma_start(w[h][:, :, :], w_heads(h)).then_inc(w_loaded[h], 16)
            w_out = dram["L0_attn_W_out"].rearrange("(h p) n -> p h n", p=P)
            sp.dma_start(wo[:, :, :], w_out[:, 0:H // 2, :]).then_inc(wo_loaded, 16)
            with sp.Fori(1, H // 2) as pair:
                for j in range(2):
                    sp.wait_ge(S["z_ps"], 2 * pair + (j - 1))
                    sp.dma_start(w[j][:, :, :], w_heads(2 * pair + j)).then_inc(w_loaded[j], 16)
            for j in range(2):
                sp.wait_ge(S["z_ps"], H - 1 + j)
                h0 = H // 2 + j * DC
                sp.dma_start(w[j][:, :, :], w_out[:, h0:h0 + DC, :]).then_inc(wo_loaded, 16)

        @block.gpsimd
        def _(pool):
            n = 0
            for buf, v in ((low[:, :], 0.0), (up[:, :], 0.0), (m0[:, :], 0.0), (pairm[:, :, :], 0.0)):
                pool.memset(buf, v).then_inc(pool_own, 1)
                n += 1
            pool.wait_ge(pool_own, n)
            pool.affine_select(out=low[:, :], in_=low[:, :], compare_op=ALU.is_ge, fill=-BIG, base=0,
                               pattern=[[-1, P]], channel_multiplier=1).then_inc(pool_own, 1)
            pool.affine_select(out=up[:, :], in_=up[:, :], compare_op=ALU.is_ge, fill=BIG, base=0,
                               pattern=[[1, P]], channel_multiplier=-1).then_inc(pool_own, 1)
            mm = m0[:, :].rearrange("p (a two) -> p a two", two=2)[:, :, 0]
            pool.affine_select(out=mm, in_=mm, compare_op=ALU.not_equal, fill=1.0, base=-1,
                               pattern=[[-2, HALF]], channel_multiplier=1).then_inc(pool_own, 1)
            n += 3
            pool.wait_ge(pool_own, n)
            for l in range(LEVELS):
                s = 2 ** (l + 1)
                part = pairm[:, l, :].rearrange("p (q c) -> p q c", c=s)
                pool.memset(part, 1.0).then_inc(pool_own, 1)
                n += 1
                pool.wait_ge(pool_own, n)
                pool.affine_select(out=part, in_=part, compare_op=ALU.is_ge, fill=0.0, base=0,
                                   pattern=[[-2 * s, HALF // s], [0, s]], channel_multiplier=1).then_inc(pool_own, 1)
                n += 1
                pool.wait_ge(pool_own, n)
                pool.affine_select(out=part, in_=part, compare_op=ALU.is_ge, fill=0.0, base=s - 1,
                                   pattern=[[2 * s, HALF // s], [0, s]], channel_multiplier=-1).then_inc(pool_own, 1)
                n += 1
                pool.wait_ge(pool_own, n)

            def turn(fronts, middle, norm, p):
                q = 1 - p

                def inverse_norms(n, j, par):
                    if n is None:
                        return
                    wait(pool, "ss_ready", 2 * n + j)
                    wait(pool, "core_ready", n - 2)
                    nc.gpsimd.tensor_tensor(rs[par][:, j, :, :], ss[:, :, :],
                                            g.half[:, 0:2 * NT].rearrange("p (a b) -> p a b", a=2),
                                            ALU.pow).then_inc(S["rs_ready"], 1)
                    wait(pool, "kh_ready", 2 * n + j)
                    wait(pool, "s_ps", n - 2)
                    nc.gpsimd.tensor_tensor(kej[par][:, j * NT:(j + 1) * NT, :], kh[:, :, :], cols(par, j, CREST),
                                            ALU.mult).then_inc(S["kej_ready"], 1)

                def decay_sources(j):
                    if fronts is None:
                        return
                    wait(pool, "hs_ready", fronts)
                    wait(pool, "gb_ps", 2 * fronts + j - 1)
                    nc.gpsimd.tensor_tensor(dg[:, :, :], g.triu[:, :].unsqueeze(1).broadcast_to((P, NT, P)),
                                            cols(p, j, GN), ALU.mult).then_inc(S["dg_ready"], 1)

                inverse_norms(middle, 1, q)
                decay_sources(0)
                if norm is not None:
                    wait(pool, "f_arg", norm)
                    nc.gpsimd.tensor_tensor(f[:, :], oss[:, :], g.half[:, 0:T2], ALU.pow).then_inc(S["f_pow"], 1)
                inverse_norms(fronts, 0, p)
                decay_sources(1)

            pipeline(pool, turn)

        @block.tensor
        def _(pe):
            pe.wait_ge(loaded, 80)
            for t in range(NT):
                for c in range(DC):
                    last = nc.tensor.matmul(bank[0][:, t * 2 * H:(t + 1) * 2 * H], g.xT[:, c, t * P:(t + 1) * P],
                                            wab[:, c, :], start=(c == 0), stop=(c == DC - 1))
            last.then_inc(S["ab"], 1)
            pe.wait_ge(S["gneg"], 1)
            gn = gneg[:, :, :].rearrange("p t h -> p (t h)")
            nc.tensor.matmul(bank[1][:, 0:NG], g.triu[:, :], gn, start=True, stop=True)
            nc.tensor.matmul(bank[2][:, 0:NG], g.ones[:, :], gn, start=True, stop=True).then_inc(S["cums"], 1)
            mm, tr = nc.tensor.matmul, nc.tensor.transpose

            def turn(fronts, middle, norm, p):
                q = 1 - p

                def owner(j):
                    return (fronts, p) if j == 0 else (middle, q)

                def project(n, j, chunks):
                    if fronts is None:
                        return
                    h = 2 * fronts + j
                    bk = {"k": bank_k(j), "q": 1 - bank_k(j), "v": 2}[n]
                    if chunks[0] == 0:
                        if n == "k":
                            pe.wait_ge(w_loaded[j], 16 * fronts + 16)
                            wait(pe, "z_mul", h - 1)
                        elif n == "q":
                            wait(pe, "a_ready", h - 1)
                        else:
                            wait(pe, "pt_ready", h - 1)
                    kind = "qkv".index(n)
                    for c in chunks:
                        last = mm(bank[bk][:, :], w[j][:, c, kind * P:(kind + 1) * P], g.xT[:, c, :],
                                  start=(c == 0), stop=(c == DC - 1))
                    if chunks[-1] == DC - 1:
                        last.then_inc(S[f"{n}_ps"], 1)

                def project_z(j, t):
                    if fronts is None:
                        return
                    if t == 0:
                        wait(pe, "q_conv", 2 * fronts + j)
                    for c in range(DC):
                        last = mm(bank[1 - bank_k(j)][:, t * P:(t + 1) * P], g.xT[:, c, t * P:(t + 1) * P],
                                  w[j][:, c, 3 * P:4 * P], start=(c == 0), stop=(c == DC - 1))
                    if t == NT - 1:
                        last.then_inc(S["z_ps"], 1)

                def transposes(bk, src, signal, tiles_=NT):
                    for t in range(tiles_):
                        last = tr(g.psum[:, bk * D + t * P:bk * D + (t + 1) * P], src(t), g.ident[:, :])
                    last.then_inc(S[signal], 1)

                def decays(j):
                    if fronts is None:
                        return
                    wait(pe, "dg_ready", 2 * fronts + j)
                    wait(pe, "y1_ready", 2 * fronts + j - 1)
                    mm(bank[3][:, :], g.ones[:, :], dg[:, :, :].rearrange("p t n -> p (t n)"), start=True, stop=True)\
                        .then_inc(S["gb_ps"], 1)

                def k_tokens(j):
                    if fronts is None:
                        return
                    wait(pe, "k_silu", 2 * fronts + j)
                    transposes(bank_k(j), lambda t: yk[:, t * P:(t + 1) * P], "ktok")

                def square_sums(j):
                    if fronts is None:
                        return
                    h = 2 * fronts + j
                    wait(pe, "e2_arg", h)
                    wait(pe, "k_square", h)
                    wait(pe, "q_square", h)
                    for a in range(2):
                        for t in range(NT):
                            last = mm(bank[3][:, a * NT + t:a * NT + t + 1], sq[a][:, t * P:(t + 1) * P],
                                      g.ones[:, 0:1], start=True, stop=True)
                    last.then_inc(S["sums"], 1)

                def v_tokens(j):
                    if fronts is None:
                        return
                    wait(pe, "v_silu", 2 * fronts + j)
                    transposes(2, lambda t: yv[:, t * P:(t + 1) * P], "vtok")

                def k_features(j):
                    n, par = owner(j)
                    if n is None:
                        return
                    wait(pe, "kh_ready", 2 * n + j)
                    wait(pe, "ss_ready", 2 * n + j)
                    transposes(3, lambda t: kh[:, t, :], "khT_ps")

                def keys_keys(j):
                    n, par = owner(j)
                    if n is None:
                        return
                    wait(pe, "khT_ready", 2 * n + j)
                    for t in range(NT):
                        k = khT[par][:, tile(j, t), :]
                        last = mm(bank[bank_k(j)][:, t * P:(t + 1) * P], k, k, start=True, stop=True)
                    last.then_inc(S["kk"], 1)

                def keys_queries(j):
                    n, par = owner(j)
                    if n is None:
                        return
                    wait(pe, "bv_ready", 2 * n + j)
                    for t in range(NT):
                        last = mm(bank[2][:, t * P:(t + 1) * P], khT[par][:, tile(j, t), :], yq[par][:, tile(j, t), :],
                                  start=True, stop=True)
                    last.then_inc(S["kq"], 1)

                def first_inverse(j):
                    n, par = owner(j)
                    if n is None:
                        return
                    wait(pe, "x1", 2 * n + j)
                    transposes(3, lambda t: X[par][:, tile(j, t), :], "y1_ps")

                def corner(l):
                    if middle is None:
                        return
                    s = 2 ** (l + 1)
                    if l == 0:
                        wait(pe, "y1_ready", 2 * middle + 1)
                        wait(pe, "o_copied", middle - 1)
                    else:
                        wait(pe, "y_ready", middle, l, LEVELS)
                    for t in range(T2):
                        second = Y[q][:, t, :].rearrange("p (q two c) -> p q two c", two=2, c=s)[:, :, 1, :]
                        last = mm(half_tiles(bank[4])[:, t, :], A[q][:, t, :], second, start=True, stop=True)
                    last.then_inc(S["p1_ps"], 1)

                def turn_y(l):
                    if middle is None:
                        return
                    if l == 0:
                        wait(pe, "o_ready", middle - 1)
                    if l == 3:
                        wait(pe, "coreT_ready", middle - 1)
                    transposes(6, lambda t: Y[q][:, t, :], "xt_ps", T2)

                def joined(l):
                    if middle is None:
                        return
                    wait(pe, "p1_ready", middle, l + 1, LEVELS)
                    if l:
                        wait(pe, "x_ready", middle, l, LEVELS - 1)
                    for t in range(T2):
                        last = mm(half_tiles(bank[5])[:, t, :], X[q][:, t, :], p1[:, t, :], start=True, stop=True)
                    last.then_inc(S["yp_ps"], 1)

                def first_values():
                    if middle is None:
                        return
                    wait(pe, "y_ready", middle, LEVELS, LEVELS)
                    for n in range(2 * BATCH):
                        last = mm(bank[7][:, n * P:(n + 1) * P], Y[q][:, 2 * n, :], bv[q][:, 2 * n, :],
                                  start=True, stop=True)
                    last.then_inc(S["u0_ps"], 1)

                def state():
                    if middle is None:
                        return
                    wait(pe, "u0_ready", middle)
                    wait(pe, "kej_ready", 2 * middle + 1)
                    for n in range(2 * BATCH):
                        last = mm(bank[4][:, n * P:(n + 1) * P], kej[q][:, 2 * n, :], U[:, 2 * n, :],
                                  start=True, stop=True)
                    last.then_inc(S["s_ps"], 1)

                def of_state():
                    if middle is None:
                        return
                    wait(pe, "s_ready", middle)
                    for n in range(2 * BATCH):
                        last = mm(bank[5][:, n * P:(n + 1) * P], khT[q][:, 2 * n + 1, :], St[:, n, :],
                                  start=True, stop=True)
                    last.then_inc(S["ks_ps"], 1)
                    for n in range(2 * BATCH):
                        last = mm(bank[6][:, n * P:(n + 1) * P], yq[q][:, 2 * n + 1, :], St[:, n, :],
                                  start=True, stop=True)
                    last.then_inc(S["qs_ps"], 1)

                def second_values():
                    if middle is None:
                        return
                    wait(pe, "r_ready", middle)
                    for n in range(2 * BATCH):
                        last = mm(bank[7][:, n * P:(n + 1) * P], Y[q][:, 2 * n + 1, :], R[:, n, :],
                                  start=True, stop=True)
                    last.then_inc(S["u1_ps"], 1)

                def outputs():
                    if middle is None:
                        return
                    wait(pe, "u1_ready", middle)
                    for t in range(T2):
                        last = mm(g.psum[:, 4 * D + t * P:4 * D + (t + 1) * P], PT[q][:, t, :], U[:, t, :],
                                  start=True, stop=True)
                    last.then_inc(S["o_ps"], 1)

                def turn_core():
                    if norm is None:
                        return
                    wait(pe, "core_ready", norm)
                    transposes(6, lambda t: core[:, t, :], "coreT_ps", T2)

                project("k", 0, range(0, 2))
                k_features(1)
                project("k", 0, range(2, 4))
                keys_keys(1)
                keys_queries(1)
                project("q", 0, range(0, 2))
                first_inverse(1)
                project("q", 0, range(2, 4))
                corner(0)
                project("v", 0, range(0, 2))
                joined(0)
                project("v", 0, range(2, 4))
                decays(0)
                corner(1)
                turn_y(0)
                k_tokens(0)
                project_z(0, 0)
                joined(1)
                project_z(0, 1)
                project_z(0, 2)
                corner(2)
                turn_y(1)
                project_z(0, 3)
                joined(2)
                corner(3)
                turn_y(2)
                square_sums(0)
                project("k", 1, range(0, 2))
                joined(3)
                v_tokens(0)
                project("k", 1, range(2, 4))
                turn_core()
                k_features(0)
                corner(4)
                turn_y(3)
                keys_keys(0)
                joined(4)
                keys_queries(0)
                project("q", 1, range(0, 2))
                corner(5)
                turn_y(4)
                project("q", 1, range(2, 4))
                joined(5)
                first_inverse(0)
                project("v", 1, range(0, 2))
                first_values()
                project("v", 1, range(2, 4))
                state()
                decays(1)
                k_tokens(1)
                of_state()
                project_z(1, 0)
                project_z(1, 1)
                second_values()
                project_z(1, 2)
                project_z(1, 3)
                outputs()
                v_tokens(1)
                square_sums(1)

            pe.wait_ge(S["cums_out"], 2)
            pipeline(pe, turn)
            pe.wait_ge(wo_loaded, 48)
            wait(pe, "coreT_ready", H // 2 - 1)
            wait(pe, "z_mul", H - 1)
            wait(pe, "pt_ready", H - 1)
            wait(pe, "y1_ready", H - 1)
            for t in range(NT):
                for h in range(H):
                    k = h - H // 2
                    w_h = wo[:, h, :] if k < 0 else w[k // DC][:, k % DC, :]
                    last = mm(bank[t][:, :], coreT[:, h, t, :], w_h, start=(h == 0), stop=(h == H - 1))
                last.then_inc(S["out_ps"], 1)

        @block.scalar
        def _(act):
            A_ = nc.scalar.activation
            act.wait_ge(loaded, 80)
            A_(expa[:, :], alog[:, :], ACT.Exp).then_inc(S["ab_exp"], 1)
            act.wait_ge(S["ab_out"], 1)
            A_(th[:, :, :], ab[:, :, 0:H], ACT.Tanh, scale=0.5).then_inc(S["ab_tanh"], 1)
            act.wait_ge(S["ab_out"], 2)
            A_(gb[:, :, :], ga[:, :, :], ACT.Exp, scale=-1.0).then_inc(S["g_exp"], 1)
            act.wait_ge(S["g_exp"], 1)
            A_(gb[:, :, :], gb[:, :, :], ACT.Ln, bias=1.0).then_inc(S["g_ln"], 1)
            act.wait_ge(S["cums_out"], 2)
            act.wait_ge(S["cums_out"], 3)
            sc = scal[:, :, :].rearrange("p h n -> p n h")
            A_(sc[:, NCUMX:NCUMX + NT, :], cum[:, :, :], ACT.Exp, scale=-1.0).then_inc(S["cum_exp"], 1)
            A_(sc[:, CREST:CREST + NT, :], last_cum[:, :, :], ACT.Exp).then_inc(S["cum_exp"], 1)
            act.wait_ge(S["scal_ready"], 1)
            heads = scal[:, :, :].rearrange("p h n -> p (h n)")

            def turn(fronts, middle, norm, p):
                q = 1 - p

                def owner(j):
                    return (fronts, p) if j == 0 else (middle, q)

                def copy_x(l):
                    if middle is None:
                        return
                    wait(act, "xt_ps", middle, l + 1, LEVELS - 1)
                    nc.scalar.copy(X[q][:, :, :], two_banks(6)).then_inc(S["x_ready"], 1)

                def source(n, j):
                    if n == "q":
                        return yq[p][:, j * NT:(j + 1) * NT, :].rearrange("p t n -> p (t n)")
                    return {"k": yk, "v": yv}[n][:, :]

                def tanh(n, j):
                    if fronts is None:
                        return
                    wait(act, f"{n}_conv", 2 * fronts + j)
                    A_(tn["kqv".index(n)][:, :], source(n, j), ACT.Tanh, scale=0.5).then_inc(S[f"{n}_tanh"], 1)

                def square(n, j):
                    if fronts is None:
                        return
                    wait(act, f"{n}_silu", 2 * fronts + j)
                    A_(sq["kq".index(n)][:, :], source(n, j), ACT.Square).then_inc(S[f"{n}_square"], 1)

                def decay(e, n, j):
                    if fronts is None:
                        return
                    wait(act, f"e{n}_arg", 2 * fronts + j)
                    A_(e[:, :, :], e[:, :, :], ACT.Exp, scale=(1.0, -1.0)[n - 1]).then_inc(S[f"e{n}_ready"], 1)

                def z_tanh(j):
                    if fronts is None:
                        return
                    wait(act, "z_ps", 2 * fronts + j)
                    A_(zt[:, :, :], tiles(bank[1 - bank_k(j)]), ACT.Tanh, scale=0.5).then_inc(S["z_tanh"], 1)

                def from_bank_3(dst, j, ps, signal):
                    n, par = owner(j)
                    if n is None:
                        return
                    wait(act, ps, 2 * n + j)
                    nc.scalar.copy(dst[par][:, j * NT:(j + 1) * NT, :], tiles(bank[3])).then_inc(S[signal], 1)

                if fronts is not None:
                    wait(act, "o_ready", fronts - 2)
                    nc.scalar.copy(hs[p][:, :, :].rearrange("p h n -> p (h n)"),
                                   heads[:, bass.ds(fronts * (2 * NS), 2 * NS)]).then_inc(S["hs_ready"], 1)
                from_bank_3(khT, 1, "khT_ps", "khT_ready")
                tanh("k", 0)
                from_bank_3(Y, 1, "y1_ps", "y1_ready")
                tanh("q", 0)
                copy_x(0)
                square("k", 0)
                tanh("v", 0)
                copy_x(1)
                square("q", 0)
                decay(e1, 1, 0)
                z_tanh(0)
                copy_x(2)
                decay(e2, 2, 0)
                if norm is not None:
                    wait(act, "coreT_ps", norm)
                    nc.scalar.copy(coreT[:, :, :, :].rearrange("p h t n -> p (h t n)")
                                   [:, bass.ds(norm * (2 * TOK), 2 * TOK)],
                                   g.psum[:, 6 * D:8 * D]).then_inc(S["coreT_ready"], 1)
                from_bank_3(khT, 0, "khT_ps", "khT_ready")
                copy_x(3)
                copy_x(4)
                tanh("k", 1)
                from_bank_3(Y, 0, "y1_ps", "y1_ready")
                ev = U[:, :, :].rearrange("p (b two) n -> p b two n", two=2)
                if middle is not None:
                    wait(act, "u0_ps", middle)
                    nc.scalar.copy(ev[:, :, 0, :], tiles(bank[7])).then_inc(S["u0_ready"], 1)
                tanh("q", 1)
                if middle is not None:
                    wait(act, "s_ps", middle)
                    nc.scalar.copy(St[:, :, :], tiles(bank[4])).then_inc(S["s_ready"], 1)
                square("k", 1)
                if middle is not None:
                    wait(act, "u1_ps", middle)
                    nc.scalar.copy(ev[:, :, 1, :], tiles(bank[7])).then_inc(S["u1_ready"], 1)
                tanh("v", 1)
                square("q", 1)
                decay(e1, 1, 1)
                z_tanh(1)
                if middle is not None:
                    wait(act, "o_ps", middle)
                    nc.scalar.copy(o, two_banks(4)).then_inc(S["o_copied"], 1)
                decay(e2, 2, 1)

            pipeline(act, turn)

        @block.vector
        def _(dve):
            V = nc.vector
            c = Links(dve, own)
            dve.wait_ge(loaded, 80)
            dve.wait_ge(S["ab"], 1)
            V.tensor_copy(ab[:, :, :], bank[0][:, 0:NT * 2 * H].rearrange("p (t n) -> p t n", t=NT))\
             .then_inc(S["ab_out"], 1)
            dve.wait_ge(S["ab_out"], 1)
            c.link(V.tensor_tensor(ab[:, :, H:2 * H], ab[:, :, H:2 * H],
                                   dtb[:, :].unsqueeze(1).broadcast_to((P, NT, H)), ALU.add))
            c.link(V.tensor_scalar(ga[:, :, :], ab[:, :, H:2 * H], -1.0, None, ALU.mult))
            V.tensor_tensor(ga[:, :, :], ga[:, :, :], ab[:, :, H:2 * H], ALU.max).then_inc(S["ab_out"], 1)
            dve.wait_ge(S["g_ln"], 1)
            c.link(V.scalar_tensor_tensor(out=gneg[:, :, :], in0=ab[:, :, H:2 * H], scalar=0.0, in1=gb[:, :, :],
                                          op0=ALU.max, op1=ALU.add))
            dve.wait_ge(S["ab_exp"], 1)
            V.tensor_tensor(gneg[:, :, :], gneg[:, :, :], expa[:, :].unsqueeze(1).broadcast_to((P, NT, H)),
                            ALU.mult).then_inc(S["gneg"], 1)
            dve.wait_ge(S["cums"], 1)
            V.tensor_copy(cum[:, :, :], bank[1][:, 0:NG].rearrange("p (t h) -> p t h", t=NT))\
             .then_inc(S["cums_out"], 1)
            dve.wait_ge(S["cums_out"], 1)
            V.scalar_tensor_tensor(out=last_cum[:, :, :], in0=bank[2][:, 0:NG].rearrange("p (t h) -> p t h", t=NT),
                                   scalar=-1.0, in1=cum[:, :, :], op0=ALU.mult, op1=ALU.add)\
             .then_inc(S["cums_out"], 1)
            sc = scal[:, :, :].rearrange("p h n -> p n h")
            V.tensor_copy(sc[:, CUM:CUM + NT, :], cum[:, :, :]).then_inc(S["cums_out"], 1)
            c.link(V.tensor_copy(sc[:, GN:GN + NT, :], gneg[:, :, :]))
            dve.wait_ge(S["ab_tanh"], 1)
            c.link(V.tensor_scalar(sc[:, BETA:BETA + NT, :], th[:, :, :], 1.0, 0.5, ALU.add, ALU.mult))
            c.link(V.tensor_scalar(sc[:, HBETA:HBETA + NT, :], th[:, :, :], 1.0, 0.25, ALU.add, ALU.mult))
            dve.wait_ge(S["cum_exp"], 2)
            c.link(V.scalar_tensor_tensor(out=sc[:, NBX:NBX + NT, :], in0=sc[:, NCUMX:NCUMX + NT, :], scalar=-1.0,
                                          in1=sc[:, BETA:BETA + NT, :], op0=ALU.mult, op1=ALU.mult))
            V.tensor_scalar(normw[:, :], normw[:, :], 0.5, None, ALU.mult).then_inc(S["scal_ready"], 1)
            dve.wait_ge(S["scal_ready"], 1)
            dve.wait_ge(pool_own, 7 + 3 * LEVELS)
            FRONT_OWN, NORM_OWN = 9, 4

            def turn(fronts, middle, norm, p):
                q = 1 - p
                cf = Links(dve, front_own, None if fronts is None else 2 * FRONT_OWN * fronts)
                cn = Links(dve, norm_own, None if norm is None else NORM_OWN * norm)

                def owner(j):
                    return (fronts, p) if j == 0 else (middle, q)

                def feature_major(n, j):
                    if n == "q":
                        return yq[p][:, j * NT:(j + 1) * NT, :].rearrange("p t n -> p (t n)")
                    return {"k": yk, "v": yv}[n][:, :]

                def conv(n, j, taps):
                    if fronts is None:
                        return
                    h = 2 * fronts + j
                    bk = bank[{"k": bank_k(j), "q": 1 - bank_k(j), "v": 2}[n]]
                    k0 = CW + TAPS * "qkv".index(n)
                    y = feature_major(n, j)
                    src = bk[:, :].rearrange("p (b s) -> p b s", b=BATCH)
                    dst = y.rearrange("p (b s) -> p b s", b=BATCH)
                    for d in taps:
                        if d == 0:
                            wait(dve, f"{n}_ps", h)
                            if n == "k":
                                wait(dve, "k_square", h - 1)
                            ins = V.tensor_scalar(y, bk[:, :], hs[p][:, j, k0 + 3:k0 + 4], None, ALU.mult)
                        else:
                            ins = V.scalar_tensor_tensor(out=dst[:, :, d:], in0=src[:, :, 0:SEQ - d],
                                                         scalar=hs[p][:, j, k0 + 3 - d:k0 + 4 - d],
                                                         in1=dst[:, :, d:], op0=ALU.mult, op1=ALU.add)
                        if d < 3:
                            cf.link(ins)
                        else:
                            ins.then_inc(S[f"{n}_conv"], 1)

                def silu(n, j):
                    if fronts is None:
                        return
                    wait(dve, f"{n}_tanh", 2 * fronts + j)
                    y = feature_major(n, j)
                    V.scalar_tensor_tensor(out=y, in0=tn["kqv".index(n)][:, :], scalar=1.0, in1=y,
                                           op0=ALU.add, op1=ALU.mult).then_inc(S[f"{n}_silu"], 1)

                def exponent(e, bound, op, signal, j):
                    if fronts is None:
                        return
                    wait(dve, "gb_ps", 2 * fronts + j)
                    for t in range(NT):
                        last = V.scalar_tensor_tensor(out=e[:, t, :], in0=tiles(bank[3])[:, t, :],
                                                      scalar=hs[p][:, j, CUM + t:CUM + t + 1], in1=bound[:, :],
                                                      op0=ALU.subtract, op1=op)
                    last.then_inc(S[signal], 1)

                def mask_corner(l):
                    if middle is None:
                        return
                    wait(dve, "p1_ps", middle, l + 1, LEVELS)
                    V.tensor_tensor(p1[:, :, :], half_tiles(bank[4]),
                                    pairm[:, l, :].unsqueeze(1).broadcast_to((P, T2, HALF)), ALU.mult)\
                     .then_inc(S["p1_ready"], 1)

                def join(l):
                    if middle is None:
                        return
                    wait(dve, "yp_ps", middle, l + 1, LEVELS)
                    s = 2 ** (l + 1)
                    sec = Y[q][:, :, :].rearrange("p t (q two c) -> p (t q) two c", two=2, c=s)[:, :, 1, :]
                    yp = bank[5][:, :].rearrange("p (q c) -> p q c", c=s)
                    V.tensor_tensor(sec, sec, yp, ALU.subtract).then_inc(S["y_ready"], 1)

                def add_epsilon(j):
                    if fronts is None:
                        return
                    wait(dve, "sums", 2 * fronts + j)
                    V.tensor_scalar(ss[:, :, :], bank[3][:, 0:2 * NT].rearrange("p (a t) -> p a t", a=2), 4 * EPS,
                                    None, ALU.add).then_inc(S["ss_ready"], 1)

                def unit_keys(j):
                    n, par = owner(j)
                    if n is None:
                        return
                    h = 2 * n + j
                    wait(dve, "ktok", h)
                    wait(dve, "kej_ready", h - 1)
                    wait(dve, "rs_ready", h)
                    V.tensor_tensor(kh[:, :, :], tiles(bank[bank_k(j)]),
                                    rs[par][:, j, 0, :].unsqueeze(2).broadcast_to((P, NT, DK)),
                                    ALU.mult).then_inc(S["kh_ready"], 1)

                def beta_values(j):
                    n, par = owner(j)
                    if n is None:
                        return
                    wait(dve, "vtok", 2 * n + j)
                    V.tensor_tensor(bv[par][:, j * NT:(j + 1) * NT, :], tiles(bank[2]), cols(par, j, HBETA), ALU.mult)\
                     .then_inc(S["bv_ready"], 1)

                def z_silu(j):
                    if fronts is None:
                        return
                    wait(dve, "core_ready", fronts - 2)
                    wait(dve, "z_tanh", 2 * fronts + j)
                    V.scalar_tensor_tensor(out=zs[p][:, j * NT:(j + 1) * NT, :], in0=zt[:, :, :], scalar=1.0,
                                           in1=tiles(bank[1 - bank_k(j)]), op0=ALU.add, op1=ALU.mult)\
                     .then_inc(S["z_mul"], 1)

                def z_norm_w(j):
                    if fronts is None:
                        return
                    wait(dve, "z_mul", 2 * fronts + j)
                    z = zs[p][:, j * NT:(j + 1) * NT, :]
                    V.tensor_tensor(z, z, normw[:, :].unsqueeze(1).broadcast_to((P, NT, DV)), ALU.mult)\
                     .then_inc(S["zs_ready"], 1)

                def key_products(j):
                    n, par = owner(j)
                    if n is None:
                        return
                    h = 2 * n + j
                    wait(dve, "kk", h)
                    wait(dve, "e1_ready", h)
                    for t in range(NT):
                        last = V.scalar_tensor_tensor(out=A[par][:, tile(j, t), :], in0=tiles(bank[bank_k(j)])[:, t, :],
                                                      scalar=hs[par][:, j, BETA + t:BETA + t + 1], in1=e1[:, t, :],
                                                      op0=ALU.mult, op1=ALU.mult)
                    last.then_inc(S["a_ready"], 1)

                def pairs_inverse(j):
                    n, par = owner(j)
                    if n is None:
                        return
                    h = 2 * n + j
                    x = X[par][:, j * NT:(j + 1) * NT, :]
                    wait(dve, "a_ready", h)
                    V.tensor_tensor(x, A[par][:, j * NT:(j + 1) * NT, :],
                                    m0[:, :].unsqueeze(1).broadcast_to((P, NT, P)), ALU.mult)\
                     .then_inc(S["a_pairs"], 1)
                    wait(dve, "a_pairs", h)
                    V.scalar_tensor_tensor(out=x, in0=x, scalar=-1.0,
                                           in1=g.ident[:, :].unsqueeze(1).broadcast_to((P, NT, P)),
                                           op0=ALU.mult, op1=ALU.add).then_inc(S["x1"], 1)

                def query_products(j):
                    n, par = owner(j)
                    if n is None:
                        return
                    wait(dve, "kq", 2 * n + j)
                    wait(dve, "e2_ready", 2 * n + j)
                    V.tensor_tensor(PT[par][:, j * NT:(j + 1) * NT, :], tiles(bank[2]), e2[:, :, :], ALU.mult)\
                     .then_inc(S["pt_ready"], 1)

                if fronts is not None:
                    wait(dve, "hs_ready", fronts)
                unit_keys(1)
                beta_values(1)
                conv("k", 0, (0, 1))
                key_products(1)
                pairs_inverse(1)
                query_products(1)
                conv("k", 0, (2, 3))
                conv("q", 0, (0, 1))
                mask_corner(0)
                conv("q", 0, (2, 3))
                join(0)
                silu("k", 0)
                if norm is not None:
                    wait(dve, "o_ready", norm)
                    wait(dve, "coreT_ps", norm - 1)
                    cn.link(V.tensor_tensor(osq, o, o, ALU.mult))
                    V.tensor_tensor(rs2[:, :].rearrange("p (j t) -> p j t", j=2), rs[p][:, :, 1, :], rs[p][:, :, 1, :],
                                    ALU.mult)
                    cn.link(V.tensor_reduce(oss[:, :], osq, AX.X, ALU.add))
                    cn.link(V.tensor_tensor(oss[:, :], oss[:, :], rs2[:, :], ALU.mult))
                    V.tensor_scalar(oss[:, :], oss[:, :], 1.0 / (DV * DK), EPS, ALU.mult, ALU.add)\
                     .then_inc(S["f_arg"], 1)
                mask_corner(1)
                conv("v", 0, (0, 1))
                join(1)
                conv("v", 0, (2, 3))
                exponent(e1, low, ALU.min, "e1_arg", 0)
                silu("q", 0)
                mask_corner(2)
                if norm is not None:
                    wait(dve, "f_pow", norm)
                    cn.link(V.scalar_tensor_tensor(out=f[:, :].rearrange("p (j t) -> p j t", j=2),
                                                   in0=f[:, :].rearrange("p (j t) -> p j t", j=2), scalar=DK ** -0.5,
                                                   in1=rs[p][:, :, 1, :], op0=ALU.mult, op1=ALU.mult))
                    for t in range(T2):
                        last = V.scalar_tensor_tensor(out=core[:, t, :], in0=o[:, t, :], scalar=f[:, t:t + 1],
                                                      in1=zs[p][:, t, :], op0=ALU.mult, op1=ALU.mult)
                    last.then_inc(S["core_ready"], 1)
                join(2)
                exponent(e2, up, ALU.max, "e2_arg", 0)
                z_silu(0)
                mask_corner(3)
                add_epsilon(0)
                silu("v", 0)
                join(3)
                unit_keys(0)
                beta_values(0)
                mask_corner(4)
                conv("k", 1, (0, 1))
                join(4)
                key_products(0)
                pairs_inverse(0)
                mask_corner(5)
                conv("k", 1, (2, 3))
                query_products(0)
                join(5)
                silu("k", 1)
                conv("q", 1, (0, 1, 2, 3))
                z_norm_w(0)
                if middle is not None:
                    wait(dve, "ks_ps", middle)
                    for j in range(2):
                        for b in range(BATCH):
                            n, t = j * BATCH + b, 2 * b + 1
                            last = V.scalar_tensor_tensor(out=R[:, n, :], in0=bank[5][:, n * P:(n + 1) * P],
                                                          scalar=hs[q][:, j, NBX + t:NBX + t + 1],
                                                          in1=bv[q][:, tile(j, t), :], op0=ALU.mult, op1=ALU.add)
                    last.then_inc(S["r_ready"], 1)
                conv("v", 1, (0, 1, 2, 3))
                silu("q", 1)
                exponent(e1, low, ALU.min, "e1_arg", 1)
                exponent(e2, up, ALU.max, "e2_arg", 1)
                silu("v", 1)
                z_silu(1)
                if middle is not None:
                    wait(dve, "o_copied", middle)
                    wait(dve, "qs_ps", middle)
                    for j in range(2):
                        for b in range(BATCH):
                            n, t = j * BATCH + b, 2 * b + 1
                            last = V.scalar_tensor_tensor(out=o[:, tile(j, t), :], in0=bank[6][:, n * P:(n + 1) * P],
                                                          scalar=hs[q][:, j, NCUMX + t:NCUMX + t + 1],
                                                          in1=o[:, tile(j, t), :], op0=ALU.mult, op1=ALU.add)
                    last.then_inc(S["o_ready"], 1)
                add_epsilon(1)
                z_norm_w(1)
                assert fronts is None or cf.n == 2 * FRONT_OWN, cf.n
                assert norm is None or cn.n == NORM_OWN, cn.n

            pipeline(dve, turn)
            for t in range(NT):
                dve.wait_ge(S["out_ps"], t + 1)
                V.tensor_tensor(g.x[:, t, :], g.x[:, t, :], bank[t][:, :], ALU.add).then_inc(S["out_added"], 1)


def expert_stage(nc, g, dram):
    E, K, F, CAP = 64, 8, 192, 128
    FH = F // 2
    NONE = E * CAP
    DEEP = 4
    XT_LAG, H_LAG = 3, 4
    LAST = 4
    xn_rows, y_rows = dram["xn_rows"], dram["y_rows"]
    with ExitStack() as ctx:
        m = Mem(nc, ctx, "moe")
        rw = m.sb("rw", [P, DC, E])
        gu = [m.sb(f"gu{i}", [P, DC, 2 * F]) for i in range(DEEP)]
        wd = [m.sb(f"wd{i}", [FH, 2, D]) for i in range(DEEP)]
        logit, score, cut = m.sb("logit", [P, NT, E]), m.sb("score", [P, NT, E]), m.sb("cut", [P, NT, E])
        nmax, total, rtotal = m.sb("nmax", [P, NT]), m.sb("total", [P, NT]), m.sb("rtotal", [P, NT])
        top, wk = m.sb("top", [P, NT, K]), m.sb("wk", [P, NT, K])
        chosen_u, chosen = m.sb("chosen_u", [P, NT, K], U32), m.sb("chosen", [P, NT, K])
        mask, rank = m.sb("mask", [P, NT, E]), m.sb("rank", [P, NT, E])
        count = m.sb("count", [P, NT, E])
        rank_e = m.sb("rank_e", [P, E, NT])
        picked = m.sb("picked", [P, E])
        place, fits, dest = m.sb("place", [P, NT, K]), m.sb("fits", [P, NT, K]), m.sb("dest", [P, NT, K], I32)
        iota_e, iota_s = m.sb("iota_e", [P, E]), m.sb("iota_s", [P, CAP])
        tok = m.sb("tok", [P, 2, NT], BF16)
        onehot = [m.sb(f"onehot{i}", [P, NT, CAP], BF16) for i in range(2)]
        idx = [m.sb(f"idx{i}", [P, 1], I32) for i in range(DEEP)]
        xg = [m.sb(f"xg{i}", [P, D]) for i in range(DEEP)]
        xgT = [m.sb(f"xgT{i}", [P, DC, CAP]) for i in range(2)]
        th = [m.sb(f"th{i}", [P, F]) for i in range(2)]
        h = [m.sb(f"h{i}", [P, F]) for i in range(2)]
        hT = [m.sb(f"hT{i}", [FH, 2, CAP]) for i in range(2)]
        y = [m.sb(f"y{i}", [P, D]) for i in range(DEEP)]
        zero = m.sb("zero", [1, D])
        NG = 6
        yg = [m.sb(f"yg{i}", [P, D]) for i in range(NG)]
        IDX = g.bank[0]
        XT = [g.bank[1 + i][:, :].rearrange("p (c n) -> p c n", c=DC) for i in range(2)]
        GU = [g.bank[3 + i] for i in range(2)]
        HT = g.bank[5]
        HTv = HT[0:FH, 0:2 * CAP].rearrange("p (a n) -> p a n", a=2)
        Y = [g.bank[6 + i] for i in range(2)]
        rw_loaded, xn_stored, zero_stored = m.sem("rw_loaded"), m.sem("xn_stored"), m.sem("zero_stored")
        w_loaded = [m.sem(f"w_loaded{i}") for i in range(DEEP)]
        gathered = [m.sem(f"gathered{i}") for i in range(DEEP)]
        stored = [m.sem(f"stored{i}") for i in range(DEEP)]
        y_gathered = [m.sem(f"y_gathered{i}") for i in range(NG)]
        own, pool_own = m.sem("own"), m.sem("pool_own")
        names = """iotas logits exp_in exp_out mask_ready ranks dest_ready onehot_ready gather_begun idx_ps idx_ready xt_ps
            xgT_ready gu_ps th_ready h1_ready h_ready ht_ps hT_ready y_ps y_copied y_added""".split()
        S = {n: m.sem(n) for n in names}
        block = ctx.enter_context(nc.Block())

        def steps(eng, body, lo, hi):
            first, last = 8, 56
            for s in range(lo, first):
                body(s)
            with eng.Fori(first, last, DEEP) as r:
                for k in range(DEEP):
                    body(r, k)
            for s in range(last, hi):
                body(s)

        class At:

            def __init__(self, s, half, lag):
                if half is None:
                    self.e = s - lag
                    self.p, self.q = self.e % 2, self.e % DEEP
                    self.exists = 0 <= self.e < E
                    self.static = True
                else:
                    self.e = s + (half - lag)
                    self.p, self.q = (half - lag) % 2, (half - lag) % DEEP
                    self.exists = True
                    self.static = False

        def wait_own(eng, sem, at):
            eng.wait_ge(sem, at.e + 1)

        def wait_before(eng, sem, at, back):
            if not at.static or at.e >= back:
                eng.wait_ge(sem, at.e + (1 - back))

        def wait_dma(eng, sems, at, back=0, per=16):
            if not at.static or at.e >= back:
                eng.wait_ge(sems[at.q], at.e * (per // DEEP) + (per - (per // DEEP) * (at.q + back)))

        @block.sync
        def _(sp):
            sp.dma_start(rw[:, :, :], dram["L0_ffn_router"].rearrange("(c p) n -> p c n", p=P)).then_inc(rw_loaded, 16)
            sp.dma_start(xn_rows.rearrange("(t p) d -> p t d", p=P), g.xn[:, :, :]).then_inc(xn_stored, 16)

            def body(s, half=None):
                a = At(s, half, 0)
                if a.exists:
                    wait_before(sp, S["y_ps"], a, DEEP)
                    sp.dma_start(gu[a.q][:, :, :], dram["L0_ffn_gate_up"][bass.ds(a.e * P, P), :]
                                 .rearrange("p (c n) -> p c n", c=DC)).then_inc(w_loaded[a.q], 16)
                    sp.dma_start(wd[a.q][:, :, :], dram["L0_ffn_w_down"][bass.ds(a.e * FH, FH), :]
                                 .rearrange("p (a n) -> p a n", a=2)).then_inc(w_loaded[a.q], 16)
                a = At(s, half, LAST)
                if a.exists:
                    wait_own(sp, S["y_copied"], a)
                    sp.dma_start(y_rows[bass.ds(a.e * CAP, CAP), :], y[a.q][:, :]).then_inc(stored[a.q], 16)

            steps(sp, body, 0, E + LAST)
            sp.wait_ge(xn_stored, 16)
            for q in range(DEEP):
                sp.wait_ge(stored[q], 16 * E // DEEP)
            sp.wait_ge(zero_stored, 16)

        @block.gpsimd
        def _(pool):
            pool.iota(iota_e[:, :], pattern=[[1, E]], base=0, channel_multiplier=0,
                      allow_small_or_imprecise_dtypes=True).then_inc(S["iotas"], 1)
            pool.iota(iota_s[:, :], pattern=[[1, CAP]], base=1, channel_multiplier=0,
                      allow_small_or_imprecise_dtypes=True).then_inc(S["iotas"], 1)
            pool.iota(tok[:, 0, :], pattern=[[P, NT]], base=0, channel_multiplier=0,
                      allow_small_or_imprecise_dtypes=True).then_inc(S["iotas"], 1)
            pool.iota(tok[:, 1, :], pattern=[[0, NT]], base=0, channel_multiplier=1,
                      allow_small_or_imprecise_dtypes=True).then_inc(S["iotas"], 1)
            pool.memset(zero[:, :], 0.0).then_inc(pool_own, 1)
            pool.wait_ge(pool_own, 1)
            pool.dma_start(y_rows[NONE:NONE + 1, :], zero[:, :]).then_inc(zero_stored, 16)
            pool.wait_ge(xn_stored, 16)

            def body(s, half=None):
                a = At(s, half, 0)
                if a.exists:
                    wait_before(pool, S["xt_ps"], a, DEEP)
                    wait_own(pool, S["idx_ready"], a)
                    pool.sem_inc(S["gather_begun"], 1)
                    pool.indirect_dma_start(xg[a.q][:, :], None, xn_rows,
                                            bass.IndirectOffsetOnAxis(idx[a.q][:, 0:1], 0))\
                        .then_inc(gathered[a.q], 16)

            steps(pool, body, 0, E)
            pool.wait_ge(S["dest_ready"], 1)
            for q in range(DEEP):
                pool.wait_ge(stored[q], 16 * E // DEEP)
            pool.wait_ge(zero_stored, 16)
            for n in range(NT * K):
                if n >= NG:
                    pool.wait_ge(S["y_added"], n - NG + 1)
                pool.indirect_dma_start(yg[n % NG][:, :], None, y_rows,
                                        bass.IndirectOffsetOnAxis(dest[:, n // K, n % K:n % K + 1], 0))\
                    .then_inc(y_gathered[n % NG], 16)

        @block.tensor
        def _(pe):
            mm, tr = nc.tensor.matmul, nc.tensor.transpose
            pe.wait_ge(rw_loaded, 16)
            for t in range(NT):
                for c in range(DC):
                    last = mm(GU[0][:, t * E:(t + 1) * E], g.xT[:, c, t * P:(t + 1) * P], rw[:, c, :],
                              start=(c == 0), stop=(c == DC - 1))
            last.then_inc(S["logits"], 1)
            pe.wait_ge(S["mask_ready"], 1)
            flat = mask[:, :, :].rearrange("p t e -> p (t e)")
            mm(GU[0][:, 0:NT * E], g.triu[:, :], flat, start=True, stop=True)
            mm(GU[1][:, 0:NT * E], g.ones[:, :], flat, start=True, stop=True).then_inc(S["ranks"], 1)

            def body(s, half=None):
                a = At(s, half, 0)
                if a.exists:
                    wait_own(pe, S["onehot_ready"], a)
                    wait_before(pe, S["idx_ready"], a, 1)
                    for t in range(NT):
                        for part in range(2):
                            last = mm(IDX[:, 0:1], onehot[a.p][:, t, :], tok[:, part, t:t + 1],
                                      start=(t == 0 and part == 0), stop=(t == NT - 1 and part == 1))
                    last.then_inc(S["idx_ps"], 1)
                a = At(s, half, XT_LAG)
                if a.exists:
                    wait_dma(pe, gathered, a)
                    wait_before(pe, S["xgT_ready"], a, 2)
                    for c in range(DC):
                        last = tr(XT[a.p][:, c, :], xg[a.q][:, c * P:(c + 1) * P], g.ident[:, :])
                    last.then_inc(S["xt_ps"], 1)
                a = At(s, half, H_LAG)
                if a.exists:
                    wait_own(pe, S["h_ready"], a)
                    wait_before(pe, S["hT_ready"], a, 1)
                    for k in range(2):
                        last = tr(HTv[:, k, :], h[a.p][:, k * FH:(k + 1) * FH], g.ident[:, :])
                    last.then_inc(S["ht_ps"], 1)
                a = At(s, half, XT_LAG)
                if a.exists:
                    wait_dma(pe, w_loaded, a, per=32)
                    wait_own(pe, S["xgT_ready"], a)
                    wait_before(pe, S["h_ready"], a, 2)
                    for c in range(DC):
                        last = mm(GU[a.p][:, 0:2 * F], xgT[a.p][:, c, :], gu[a.q][:, c, :],
                                  start=(c == 0), stop=(c == DC - 1))
                    last.then_inc(S["gu_ps"], 1)
                a = At(s, half, H_LAG)
                if a.exists:
                    wait_own(pe, S["hT_ready"], a)
                    wait_before(pe, S["y_copied"], a, 2)
                    for k in range(2):
                        last = mm(Y[a.p][:, :], hT[a.p][:, k, :], wd[a.q][:, k, :], start=(k == 0), stop=(k == 1))
                    last.then_inc(S["y_ps"], 1)

            steps(pe, body, 0, E + LAST)

        @block.scalar
        def _(act):
            act.wait_ge(S["exp_in"], 1)
            nc.scalar.activation(score[:, :, :], logit[:, :, :], ACT.Exp).then_inc(S["exp_out"], 1)

            def body(s, half=None):
                a = At(s, half, XT_LAG)
                if a.exists:
                    wait_own(act, S["xt_ps"], a)
                    wait_before(act, S["gu_ps"], a, 2)
                    nc.scalar.copy(xgT[a.p][:, :, :], XT[a.p][:, :, :]).then_inc(S["xgT_ready"], 1)
                    wait_own(act, S["gu_ps"], a)
                    wait_before(act, S["h_ready"], a, 2)
                    nc.scalar.activation(th[a.p][:, :], GU[a.p][:, 0:F], ACT.Tanh, scale=0.5)\
                      .then_inc(S["th_ready"], 1)
                a = At(s, half, H_LAG)
                if a.exists:
                    wait_own(act, S["y_ps"], a)
                    wait_dma(act, stored, a, back=DEEP)
                    nc.scalar.copy(y[a.q][:, :], Y[a.p][:, :]).then_inc(S["y_copied"], 1)

            steps(act, body, 0, E + LAST)

        @block.vector
        def _(dve):
            V = nc.vector
            c = Links(dve, own)
            dve.wait_ge(S["logits"], 1)
            c.link(V.tensor_copy(logit[:, :, :], GU[0][:, 0:NT * E].rearrange("p (t e) -> p t e", t=NT)))
            c.link(V.tensor_reduce(nmax[:, :], logit[:, :, :], AX.X, ALU.max, negate=True))
            V.tensor_tensor(logit[:, :, :], logit[:, :, :], nmax[:, :].unsqueeze(2).broadcast_to((P, NT, E)), ALU.add)\
             .then_inc(S["exp_in"], 1)
            dve.wait_ge(S["exp_out"], 1)
            c.link(V.tensor_reduce(total[:, :], score[:, :, :], AX.X, ALU.add))
            c.link(V.reciprocal(rtotal[:, :], total[:, :]))
            c.link(V.tensor_tensor(score[:, :, :], score[:, :, :], rtotal[:, :].unsqueeze(2).broadcast_to((P, NT, E)),
                                   ALU.mult))
            for t in range(NT):
                c.link(V.max(top[:, t, :], score[:, t, :]))
                c.link(V.match_replace(cut[:, t, :], top[:, t, :], score[:, t, :], -1.0))
                c.link(V.max_index(chosen_u[:, t, :], top[:, t, :], score[:, t, :]))
            V.tensor_tensor(mask[:, :, :], score[:, :, :], cut[:, :, :], ALU.not_equal).then_inc(S["mask_ready"], 1)
            dve.wait_ge(S["iotas"], 4)
            c.link(V.tensor_reduce(total[:, :], top[:, :, :], AX.X, ALU.add))
            c.link(V.tensor_scalar(total[:, :], total[:, :], 1e-20, 2.0, ALU.add, ALU.mult))
            c.link(V.reciprocal(rtotal[:, :], total[:, :]))
            c.link(V.tensor_tensor(wk[:, :, :], top[:, :, :], rtotal[:, :].unsqueeze(2).broadcast_to((P, NT, K)),
                                   ALU.mult))
            c.link(V.tensor_copy(chosen[:, :, :], chosen_u[:, :, :]))
            dve.wait_ge(S["ranks"], 1)
            c.link(V.tensor_copy(rank[:, :, :], GU[0][:, 0:NT * E].rearrange("p (t e) -> p t e", t=NT)))
            c.link(V.tensor_copy(count[:, :, :], GU[1][:, 0:NT * E].rearrange("p (t e) -> p t e", t=NT)))
            for t in range(1, NT):
                for u in range(t):
                    c.link(V.tensor_tensor(rank[:, t, :], rank[:, t, :], count[:, u, :], ALU.add))
            c.link(V.tensor_tensor(rank[:, :, :], rank[:, :, :], mask[:, :, :], ALU.mult))
            c.link(V.tensor_copy(rank_e[:, :, :].rearrange("p e t -> p t e"), rank[:, :, :]))

            def places():
                for t in range(NT):
                    for k in range(K):
                        c.link(V.scalar_tensor_tensor(out=picked[:, :], in0=iota_e[:, :],
                                                      scalar=chosen[:, t, k:k + 1], in1=rank[:, t, :],
                                                      op0=ALU.is_equal, op1=ALU.mult,
                                                      accum_out=place[:, t, k:k + 1]))
                c.link(V.tensor_scalar(fits[:, :, :], place[:, :, :], float(CAP), None, ALU.is_le))
                c.link(V.scalar_tensor_tensor(out=place[:, :, :], in0=chosen[:, :, :], scalar=float(CAP),
                                              in1=place[:, :, :], op0=ALU.mult, op1=ALU.add))
                c.link(V.scalar_tensor_tensor(out=place[:, :, :], in0=place[:, :, :], scalar=-1.0 - NONE,
                                              in1=fits[:, :, :], op0=ALU.add, op1=ALU.mult))
                V.tensor_scalar(dest[:, :, :], place[:, :, :], float(NONE), None, ALU.add)\
                 .then_inc(S["dest_ready"], 1)

            def body(s, half=None):
                if half is None and s == 6:
                    places()
                a = At(s, half, -1)
                if a.exists:
                    wait_before(dve, S["idx_ps"], a, 2)
                    ranks = rank_e[:, :, :].rearrange("p e t -> p (e t)")[:, bass.ds(a.e * NT, NT)]
                    V.tensor_tensor(onehot[a.p][:, :, :], iota_s[:, :].unsqueeze(1).broadcast_to((P, NT, CAP)),
                                    ranks.unsqueeze(2).broadcast_to((P, NT, CAP)), ALU.is_equal)\
                     .then_inc(S["onehot_ready"], 1)
                a = At(s, half, 0)
                if a.exists:
                    wait_own(dve, S["idx_ps"], a)
                    wait_dma(dve, gathered, a, back=DEEP)
                    V.tensor_copy(idx[a.q][:, :], IDX[:, 0:1]).then_inc(S["idx_ready"], 1)
                a = At(s, half, H_LAG)
                if a.exists:
                    wait_own(dve, S["ht_ps"], a)
                    wait_before(dve, S["y_ps"], a, 2)
                    V.tensor_copy(hT[a.p][:, :, :], HTv).then_inc(S["hT_ready"], 1)
                a = At(s, half, XT_LAG)
                if a.exists:
                    wait_own(dve, S["th_ready"], a)
                    wait_before(dve, S["ht_ps"], a, 2)
                    V.scalar_tensor_tensor(out=th[a.p][:, :], in0=th[a.p][:, :], scalar=1.0, in1=GU[a.p][:, 0:F],
                                           op0=ALU.add, op1=ALU.mult).then_inc(S["h1_ready"], 1)
                    wait_own(dve, S["h1_ready"], a)
                    V.tensor_tensor(h[a.p][:, :], th[a.p][:, :], GU[a.p][:, F:2 * F], ALU.mult)\
                     .then_inc(S["h_ready"], 1)

            steps(dve, body, -1, E + LAST)
            for n in range(NT * K):
                t, k = n // K, n % K
                dve.wait_ge(y_gathered[n % NG], 16 * (n // NG + 1))
                if k:
                    dve.wait_ge(S["y_added"], n)
                V.scalar_tensor_tensor(out=g.x[:, t, :], in0=yg[n % NG][:, :], scalar=wk[:, t, k:k + 1],
                                       in1=g.x[:, t, :], op0=ALU.mult, op1=ALU.add).then_inc(S["y_added"], 1)


class FfnWeights:

    def __init__(self, m, dram):
        self.up = m.sb("up", [P, DC * 2048])
        self.down = m.sb("down", [P, 16 * D])
        self.loaded = {n: m.sem(f"loaded_{n}") for n in ("up", "down")}
        self.dram = dram

    def load(self, sp):
        sp.dma_start(self.up[:, :].rearrange("p (c n) -> p c n", c=DC),
                     self.dram["L1_ffn_up"].rearrange("(c p) n -> p c n", p=P)).then_inc(self.loaded["up"], 16)
        sp.dma_start(self.down[:, :].rearrange("p (c n) -> p c n", c=16),
                     self.dram["L1_ffn_down"].rearrange("(c p) n -> p c n", p=P)).then_inc(self.loaded["down"], 16)


def ternary_stage(nc, g, dram, weights):
    F32R = mybir.dt.float32r
    HID, QB = 2048, 127.0
    HC = HID // P
    RING = 4
    LAG = 3
    ROUND = 1.5 * 2.0 ** 23
    with ExitStack() as ctx:
        m = Mem(nc, ctx, "ffn")
        up, down = weights.up, weights.down
        above = m.sb("above", [P, DC * HID], BF16)
        upq = m.sb("upq", [P, DC, HID], BF16)
        downq = m.sb("downq", [P, HC * D], F32R)
        h_hi, h_lo = m.sb("h_hi", [P, RING, TOK], F32R), m.sb("h_lo", [P, RING, TOK], F32R)
        h = [m.sb(f"h{i}", [P, TOK]) for i in range(2)]
        hm = [m.sb(f"hm{i}", [P, TOK]) for i in range(2)]
        ht = [m.sb(f"ht{i}", [P, TOK]) for i in range(2)]
        nw, gam = m.sb("nw", [P, D]), m.sb("gam", [P, D])
        sq = g.xT
        ss, r, big, rbig, sx = (m.sb(n, [P, NT]) for n in ("ss", "r", "big", "rbig", "sx"))
        dg = m.sb("dg", [P, NT, P])
        sxb = dg[:, :, :].rearrange("p t n -> p (t n)")
        xqT = m.sb("xqT", [P, DC, TOK], BF16)
        small = m.sb("small", [P, 10])
        part, scale, thr, nthr = (small[:, 2 * n:2 * n + 2] for n in range(4))
        tscale, final = small[:, 8:9], small[:, 9:10]
        bank = g.bank
        loaded, rows_loaded = weights.loaded, m.sem("rows_loaded")
        own = m.sem("own")
        names = """square ss_ready r_ready xq_ready xqT_ps xqT_ready sx_dg sxb_ps up_abs down_abs sums scales up_q down_q
            h_ps hm_ready th_ready h_ready hi_ready lo_ready down_ps""".split()
        S = {n: m.sem(n) for n in names}
        block = ctx.enter_context(nc.Block())

        @block.sync
        def _(sp):
            sp.dma_start(nw[:, :], dram["L1_ffn_norm_weight"].partition_broadcast(P)).then_inc(rows_loaded, 16)
            sp.dma_start(gam[:, :], dram["L1_ffn_gamma"].partition_broadcast(P)).then_inc(rows_loaded, 16)

        @block.gpsimd
        def _(pool):
            pool.wait_ge(S["ss_ready"], 1)
            nc.gpsimd.tensor_tensor(r[:, :], ss[:, :], g.half[:, 0:NT], ALU.pow).then_inc(S["r_ready"], 1)
            for j in range(HC):
                pool.wait_ge(S["hi_ready"], j + 1)
                nc.gpsimd.tensor_tensor(h_lo[:, j % RING, :], h[j % 2][:, :], h_hi[:, j % RING, :].bitcast(F32), ALU.subtract)\
                  .then_inc(S["lo_ready"], 1)

        @block.scalar
        def _(act):
            for t in range(NT):
                nc.scalar.activation(sq[:, t, :], g.xn[:, t, :], ACT.Square, accum_out=ss[:, t:t + 1])\
                  .then_inc(S["square"], 1)
            for t in range(NT):
                act.wait_ge(S["xqT_ps"], t + 1)
                nc.scalar.copy(xqT[:, :, t * P:(t + 1) * P],
                               bank[t % 2][:, :].rearrange("p (c n) -> p c n", c=DC)).then_inc(S["xqT_ready"], 1)
            act.wait_ge(loaded["down"], 16)
            nc.scalar.activation(above[:, :], down[:, :], ACT.Abs, accum_out=part[:, 1:2]).then_inc(S["down_abs"], 1)
            act.wait_ge(S["scales"], 1)
            for j in range(HC):
                act.wait_ge(S["hm_ready"], j + 1)
                if j == 0:
                    act.wait_ge(S["down_abs"], 1)
                nc.scalar.activation(ht[j % 2][:, :], hm[j % 2][:, :], ACT.Tanh, scale=tscale[:, 0:1])\
                  .then_inc(S["th_ready"], 1)
                act.wait_ge(S["h_ready"], j + 1)
                if j >= RING:
                    act.wait_ge(S["down_ps"], j - RING + 1)
                nc.scalar.copy(h_hi[:, j % RING, :], h[j % 2][:, :]).then_inc(S["hi_ready"], 1)

        @block.tensor
        def _(pe):
            mm, tr = nc.tensor.matmul, nc.tensor.transpose
            for t in range(NT):
                pe.wait_ge(S["xq_ready"], t + 1)
                if t >= 2:
                    pe.wait_ge(S["xqT_ready"], t - 1)
                for c in range(DC):
                    last = tr(bank[t % 2][:, c * P:(c + 1) * P], g.xn[:, t, c * P:(c + 1) * P], g.ident[:, :])
                last.then_inc(S["xqT_ps"], 1)
            pe.wait_ge(S["sx_dg"], 1)
            mm(bank[2][:, :], g.ones[:, :], dg[:, :, :].rearrange("p t n -> p (t n)"), start=True, stop=True)\
                .then_inc(S["sxb_ps"], 1)
            pe.wait_ge(S["up_abs"], 1)
            pe.wait_ge(S["down_abs"], 1)
            mm(bank[3][:, 0:2], g.ones[:, :], part[:, :], start=True, stop=True).then_inc(S["sums"], 1)
            pe.wait_ge(S["xqT_ready"], NT)
            for s in range(HC + LAG):
                if s < HC:
                    if s % 4 == 0:
                        pe.wait_ge(S["up_q"], s // 4 + 1)
                    if s >= 2:
                        pe.wait_ge(S["hm_ready"], s - 1)
                    for c in range(DC):
                        last = mm(bank[s % 2][:, :], upq[:, c, s * P:(s + 1) * P], xqT[:, c, :],
                                  start=(c == 0), stop=(c == DC - 1))
                    last.then_inc(S["h_ps"], 1)
                if s >= LAG:
                    j = s - LAG
                    if j % 4 == 0:
                        pe.wait_ge(S["down_q"], j // 4 + 1)
                    pe.wait_ge(S["lo_ready"], j + 1)
                    for t in range(NT):
                        for half in (h_hi, h_lo):
                            last = mm(bank[4 + t][:, :], half[:, j % RING, t * P:(t + 1) * P], downq[:, j * D:(j + 1) * D],
                                      start=(j == 0 and half is h_hi), stop=(j == HC - 1 and half is h_lo))
                    last.then_inc(S["down_ps"], 1)

        @block.vector
        def _(dve):
            V = nc.vector
            c = Links(dve, own)
            c.link(V.tensor_tensor(g.x[:, :, :], g.x[:, :, :], g.xn[:, :, :], ALU.add))
            dve.wait_ge(S["square"], NT)
            V.tensor_scalar(ss[:, :], ss[:, :], 1.0 / D, 1e-6, ALU.mult, ALU.add).then_inc(S["ss_ready"], 1)
            dve.wait_ge(S["r_ready"], 1)
            dve.wait_ge(rows_loaded, 32)
            for t in range(NT):
                last = V.scalar_tensor_tensor(out=g.xn[:, t, :], in0=g.xn[:, t, :], scalar=r[:, t:t + 1], in1=nw[:, :],
                                              op0=ALU.mult, op1=ALU.mult)
            c.link(last)
            c.link(V.tensor_reduce(big[:, :], g.xn[:, :, :], AX.X, ALU.max, apply_absolute_value=True))
            c.link(V.tensor_scalar(big[:, :], big[:, :], 1e-8, None, ALU.max))
            c.link(V.tensor_scalar(sx[:, :], big[:, :], 1.0 / QB, None, ALU.mult))
            c.link(V.reciprocal(rbig[:, :], big[:, :]))
            c.link(V.tensor_scalar(rbig[:, :], rbig[:, :], QB, None, ALU.mult))
            for t in range(NT):
                c.link(V.tensor_scalar(g.xn[:, t, :], g.xn[:, t, :], rbig[:, t:t + 1], ROUND, ALU.mult, ALU.add))
                V.tensor_scalar(g.xn[:, t, :], g.xn[:, t, :], ROUND, None, ALU.subtract).then_inc(S["xq_ready"], 1)
            V.tensor_tensor(dg[:, :, :], g.ident[:, :].unsqueeze(1).broadcast_to((P, NT, P)),
                            sx[:, :].unsqueeze(2).broadcast_to((P, NT, P)), ALU.mult).then_inc(S["sx_dg"], 1)
            dve.wait_ge(loaded["up"], 16)
            V.tensor_reduce(part[:, 0:1], up[:, :], AX.X, ALU.add, apply_absolute_value=True)\
             .then_inc(S["up_abs"], 1)
            dve.wait_ge(S["sums"], 1)
            c.link(V.tensor_scalar(scale[:, :], bank[3][:, 0:2], 1.0 / (D * HID), 1e-8, ALU.mult, ALU.max))
            c.link(V.tensor_scalar(thr[:, :], scale[:, :], 0.5, None, ALU.mult))
            c.link(V.tensor_scalar(nthr[:, :], scale[:, :], -0.5, None, ALU.mult))
            V.tensor_scalar(tscale[:, :], scale[:, 0:1], -0.5, None, ALU.mult).then_inc(S["scales"], 1)
            c.link(V.tensor_tensor(final[:, :], scale[:, 0:1], scale[:, 1:2], ALU.mult))
            c.link(V.tensor_scalar(final[:, :], final[:, :], 0.5, None, ALU.mult))
            dve.wait_ge(S["down_abs"], 1)

            def quantise(n, name, q):
                if n == 0:
                    part_of = slice(q * HID // 4, (q + 1) * HID // 4)
                    src, tmp = (b[:, :].rearrange("p (c n) -> p c n", c=DC)[:, :, part_of] for b in (up, above))
                    dst = upq[:, :, part_of]
                else:
                    part_of = slice(q * HC * D // 4, (q + 1) * HC * D // 4)
                    src, tmp, dst = (b[:, part_of] for b in (down, above, downq))
                c.link(V.tensor_scalar(tmp, src, thr[:, n:n + 1], None, ALU.is_gt))
                V.scalar_tensor_tensor(out=dst, in0=src, scalar=nthr[:, n:n + 1], in1=tmp,
                                       op0=ALU.is_lt, op1=ALU.subtract).then_inc(S[name], 1)
                dve.wait_ge(S[name], q + 1)

            quantise(0, "up_q", 0)
            dve.wait_ge(S["sxb_ps"], 1)
            c.link(V.tensor_copy(sxb, bank[2][:, :]))
            quantise(1, "down_q", 0)
            for j in range(HC + 1):
                if j % 4 == 1 and j // 4 < 3:
                    quantise(0, "up_q", j // 4 + 1)
                if j % 4 == 3 and j // 4 < 3:
                    quantise(1, "down_q", j // 4 + 1)
                if j < HC:
                    dve.wait_ge(S["h_ps"], j + 1)
                    if j >= 2:
                        dve.wait_ge(S["h_ready"], j - 1)
                    V.tensor_tensor(hm[j % 2][:, :], bank[j % 2][:, :], sxb, ALU.mult)\
                     .then_inc(S["hm_ready"], 1)
                if j >= 1:
                    dve.wait_ge(S["th_ready"], j)
                    if j >= 3:
                        dve.wait_ge(S["lo_ready"], j - 2)
                    V.scalar_tensor_tensor(out=h[(j - 1) % 2][:, :], in0=ht[(j - 1) % 2][:, :], scalar=1.0,
                                           in1=hm[(j - 1) % 2][:, :], op0=ALU.add, op1=ALU.mult)\
                     .then_inc(S["h_ready"], 1)
            dve.wait_ge(S["down_ps"], HC)
            for t in range(NT):
                c.link(V.scalar_tensor_tensor(out=sq[:, t, :], in0=bank[4 + t][:, :], scalar=final[:, 0:1],
                                              in1=gam[:, :], op0=ALU.mult, op1=ALU.mult))
                c.link(V.tensor_tensor(g.x[:, t, :], g.x[:, t, :], sq[:, t, :], ALU.add))


def latent_attention_stage(nc, g, dram):
    H, KEYS, DL, QB, R = 16, 4096, 128, 384, 64
    CH = 1024
    NC = KEYS // CH
    KT = CH // P
    STEPS = NT * NC
    QC = QB // P
    ROT = QB // 2
    F32R = mybir.dt.float32r
    kv_tiles = BATCH * KEYS // P
    with ExitStack() as outer:
        mo = Mem(nc, outer, "la")
        kvT_hi, kvT_lo = (mo.sb(n, [P, BATCH * KEYS], F32R) for n in ("kvT_hi", "kvT_lo"))
        kv_hl = mo.sb("kv_hl", [P, kv_tiles, 2 * DL], F32R)

        with ExitStack() as ctx:
            m = Mem(nc, ctx, "kv")
            G = 4
            NG = kv_tiles // G
            raw = [m.sb(f"raw{i}", [P, G, DL]) for i in range(2)]
            cs = [m.sb(f"cs{i}", [P, 2, G, DL // 2]) for i in range(2)]
            turned = [m.sb(f"turned{i}", [P, G, DL]) for i in range(2)]
            roped = [m.sb(f"roped{i}", [P, G, DL]) for i in range(2)]
            tp = [[g.bank[2 * k + i] for i in range(2)] for k in range(2)]
            loaded = [m.sem(f"loaded{i}") for i in range(2)]
            S = {n: m.sem(n) for n in "cos_done sin_done roped_ready hi_ready lo_ready tp_ps copied".split()}

            def pairs(ap):
                return ap.rearrange("p t (d two) -> p t d two", two=2)

            def spread(ap):
                return ap.unsqueeze(3).broadcast_to((P, G, ap.shape[2], 2))

            block = ctx.enter_context(nc.Block())

            @block.sync
            def _(sp):
                for n in range(NG):
                    b, r0 = n * G * P // KEYS, n * G * P % KEYS
                    if n >= 2:
                        sp.wait_ge(S["roped_ready"], n - 1)
                        sp.wait_ge(S["cos_done"], n - 1)
                    sp.dma_start(raw[n % 2][:, :, :], dram["ctx"][b, r0:r0 + G * P, :]
                                 .rearrange("(t p) d -> p t d", p=P)).then_inc(loaded[n % 2], 16)
                    for k, name in enumerate(("cos_k", "sin_k")):
                        sp.dma_start(cs[n % 2][:, k, :, :], dram[name][r0:r0 + G * P, :]
                                     .rearrange("(t p) d -> p t d", p=P)).then_inc(loaded[n % 2], 16)

            @block.gpsimd
            def _(pool):
                for n in range(NG):
                    pool.wait_ge(loaded[n % 2], 48 * (n // 2 + 1))
                    if n >= 2:
                        pool.wait_ge(S["lo_ready"], n - 1)
                    nc.gpsimd.tensor_tensor(pairs(roped[n % 2][:, :, :]), pairs(raw[n % 2][:, :, :]),
                                            spread(cs[n % 2][:, 0, :, :]), ALU.mult).then_inc(S["cos_done"], 1)

            @block.vector
            def _(dve):
                V = nc.vector
                for n in range(NG):
                    i = n % 2
                    dve.wait_ge(loaded[i], 48 * (n // 2 + 1))
                    h = DL // 2
                    for a in range(2):
                        last = V.tensor_tensor(pairs(turned[i][:, :, a * h:(a + 1) * h]),
                                               pairs(raw[i][:, :, (1 - a) * h:(2 - a) * h]),
                                               spread(cs[i][:, 1, :, a * h // 2:(a + 1) * h // 2]), ALU.mult)
                    last.then_inc(S["sin_done"], 1)
                    dve.wait_ge(S["sin_done"], n + 1)
                    dve.wait_ge(S["cos_done"], n + 1)
                    V.tensor_tensor(roped[i][:, :, :], roped[i][:, :, :], turned[i][:, :, :], ALU.add)\
                     .then_inc(S["roped_ready"], 1)
                    dve.wait_ge(S["roped_ready"], n + 1)
                    hi = kv_hl[:, n * G:(n + 1) * G, 0:DL]
                    V.tensor_copy(hi, roped[i][:, :, :]).then_inc(S["hi_ready"], 1)
                    dve.wait_ge(S["hi_ready"], n + 1)
                    V.tensor_tensor(kv_hl[:, n * G:(n + 1) * G, DL:2 * DL], roped[i][:, :, :], hi.bitcast(F32),
                                    ALU.subtract).then_inc(S["lo_ready"], 1)

            @block.tensor
            def _(pe):
                for n in range(NG):
                    pe.wait_ge(S["lo_ready"], n + 1)
                    if n >= 2:
                        pe.wait_ge(S["copied"], 2 * (n - 1))
                    for k in range(2):
                        for t in range(G):
                            last = nc.tensor.transpose(tp[k][n % 2][:, t * P:(t + 1) * P],
                                                       kv_hl[:, n * G + t, k * DL:(k + 1) * DL].bitcast(F32),
                                                       g.ident[:, :])
                        last.then_inc(S["tp_ps"], 1)

            @block.scalar
            def _(act):
                for n in range(NG):
                    for k, dst in enumerate((kvT_hi, kvT_lo)):
                        act.wait_ge(S["tp_ps"], 2 * n + k + 1)
                        nc.scalar.copy(dst[:, n * G * P:(n + 1) * G * P], tp[k][n % 2][:, :]).then_inc(S["copied"], 1)

        with ExitStack() as ctx:
            m = Mem(nc, ctx, "lh")
            wq, wkc = m.sb("wq", [P, DC, P]), m.sb("wkc", [P, QB + ROT])
            wqr, wkr = m.sb("wqr", [P, QC, R]), m.sb("wkr", [R, DL])
            wkv, wo = m.sb("wkv", [DL, P]), m.sb("wo", [P, D])
            cosq, sinq = m.sb("cosq", [P, QC, SEQ]), m.sb("sinq", [P, QC, SEQ])
            qhk, turned, cxT, lat = (g.xn[:, n, :] for n in range(4))
            qr = m.sb("qr", [R, TOK])
            qb = [m.sb(f"qb{i}", [P, TOK]) for i in range(QC)]
            qh, ql = m.sb("qh", [DL, TOK], F32R), m.sb("ql", [DL, TOK], F32R)
            e = [m.sb(f"e{i}", [P, CH]) for i in range(2)]
            ph = [m.sb(f"ph{i}", [P, KT, P], F32R) for i in range(2)]
            pl = [m.sb(f"pl{i}", [P, KT, P], F32R) for i in range(2)]
            nmc, nm = m.sb("nmc", [P, STEPS]), m.sb("nm", [P, STEPS])
            alpha, part = m.sb("alpha", [P, STEPS]), m.sb("part", [P, STEPS])
            total, rtotal = m.sb("total", [P, STEPS]), m.sb("rtotal", [P, NT])
            acc = [m.sb(f"acc{i}", [P, DL]) for i in range(2)]
            cx = m.sb("cx", [P, NT, DL])
            SC = [g.psum[:, i * CH:(i + 1) * CH] for i in range(2)]
            T = [g.bank[4 + i][:, :].rearrange("p (k n) -> p k n", n=P) for i in range(2)]
            AV = g.bank[6]
            Gb = g.bank[7]
            tables = m.sem("tables")
            qw_loaded, ow_loaded = m.sem("qw_loaded"), m.sem("ow_loaded")
            names = """s_ps chunk_max nm_ready e_ready t_ps hi_ready lo_ready av_ps acc_scaled acc_done cx_ready
                total_ready inverted g_ps g_done turned_ready q_hi""".split()
            S = {n: m.sem(n) for n in names}
            block = ctx.enter_context(nc.Block())

            WHERE = {(1, 0): 0, (2, 0): 1, (3, 0): 2, (3, 1): 3, (4, 0): 4, (5, 0): 5, (6, 0): 6, (7, 0): 7,
                     (7, 1): 8, (8, 0): 9, (9, 0): 10, (10, 0): 11, (11, 0): 12, (12, 0): 13, (13, 0): 14}
            OUT, QSIDE = 6, 9

            def count(h, u):
                if isinstance(h, int) and h in (-1, H):
                    return u - OUT if h < 0 else QSIDE + H * (OUT + QSIDE) - (OUT + QSIDE) + u
                return h * (OUT + QSIDE) + (QSIDE - OUT + u)

            def heads(eng, first, step, last):
                first()
                for s in range(STEPS):
                    step(0, s, False, True)
                with eng.Fori(1, H - 1) as h:
                    for s in range(STEPS):
                        step(h, s, True, True)
                for s in range(STEPS):
                    step(H - 1, s, True, False)
                last()

            def scheduled(s, place, outs, qs):
                u = WHERE.get((s, place))
                return u if u is not None and (outs if u < OUT else qs) else None

            @block.sync
            def _(sp):
                sp.dma_start(cosq[:, :, :], dram["cos_q"].rearrange("(c p) s -> p c s", p=P)).then_inc(tables, 16)
                sp.dma_start(sinq[:, :, :], dram["sin_q"].rearrange("(c p) s -> p c s", p=P)).then_inc(tables, 16)

                def load_q(h):
                    sp.dma_start(wq[:, :, :], dram["L1_xattn_Wq"][bass.ds(h * P, P), :]
                                 .rearrange("p (c n) -> p c n", c=DC)).then_inc(qw_loaded, 16)
                    sp.dma_start(wkc[:, :], dram["L1_xattn_w_kc_q"][bass.ds(h * P, P), :]).then_inc(qw_loaded, 16)
                    sp.dma_start(wqr[:, :, :], dram["L1_xattn_W_qr"][bass.ds(h * P, P), :]
                                 .rearrange("p (c n) -> p c n", c=QC)).then_inc(qw_loaded, 16)
                    sp.dma_start(wkr[:, :], dram["L1_xattn_W_kr"][bass.ds(h * R, R), :]).then_inc(qw_loaded, 16)

                def load_o(h):
                    sp.dma_start(wkv[:, :], dram["L1_xattn_w_kc_kv"][bass.ds(h * P, P), :]).then_inc(ow_loaded, 16)
                    sp.dma_start(wo[:, :], dram["L1_xattn_Wo"][bass.ds(h * P, P), :]).then_inc(ow_loaded, 16)

                load_q(0)
                load_o(0)
                sp.wait_ge(S["g_ps"], count(-1, 14) + 1)
                load_q(1)
                with sp.Fori(1, H - 1) as h:
                    sp.wait_ge(S["g_ps"], count(h, 14) + (1 - OUT - QSIDE))
                    load_q(h + 1)
                    sp.wait_ge(S["g_ps"], count(h, 5) + 1)
                    load_o(h)
                sp.wait_ge(S["g_ps"], count(H - 1, 5) + 1)
                load_o(H - 1)

            @block.tensor
            def _(pe):
                mm, tr = nc.tensor.matmul, nc.tensor.transpose

                def scores(h, s):
                    n = h * STEPS + s
                    if s < 2 and isinstance(h, int) and h == 0:
                        pass
                    else:
                        pe.wait_ge(S["e_ready"], n + (-1))
                    t, c = s // NC, s % NC
                    b = t // 2
                    for k in range(CH // D):
                        k0 = b * KEYS + c * CH + k * D
                        out = SC[s % 2][:, k * D:(k + 1) * D]
                        q = slice(t * P, (t + 1) * P)
                        mm(out, qh[:, q], kvT_hi[:, k0:k0 + D], start=True, stop=False)
                        mm(out, qh[:, q], kvT_lo[:, k0:k0 + D], start=False, stop=False)
                        last = mm(out, ql[:, q], kvT_hi[:, k0:k0 + D], start=False, stop=True)
                    last.then_inc(S["s_ps"], 1)

                def transposes(h, s):
                    n = h * STEPS + s
                    pe.wait_ge(S["e_ready"], n + 1)
                    for j in range(2):
                        if not (isinstance(h, int) and h == 0 and s == 0):
                            pe.wait_ge(S["lo_ready"], 2 * n + (j - 1))
                        for k in range(KT // 2):
                            kk = j * (KT // 2) + k
                            last = tr(T[j][:, k, :], e[s % 2][:, kk * P:(kk + 1) * P], g.ident[:, :])
                        last.then_inc(S["t_ps"], 1)

                def weighted(h, s, n):
                    if not (isinstance(n, int) and n == 0):
                        pe.wait_ge(S["acc_done"], n)
                    t, c = s // NC, s % NC
                    for j in range(2):
                        pe.wait_ge(S["lo_ready"], 2 * n + (j + 1))
                        for k in range(KT // 2):
                            kk = j * (KT // 2) + k
                            tile = (t // 2) * (KEYS // P) + c * KT + kk
                            mm(AV[:, 0:2 * DL], ph[s % 2][:, kk, :], kv_hl[:, tile, :], start=(kk == 0),
                               stop=(kk == KT - 1), skip_group_check=True)
                            last = mm(AV[:, 0:DL], pl[s % 2][:, kk, :], kv_hl[:, tile, 0:DL], start=False,
                                      stop=(kk == KT - 1), skip_group_check=True)
                    last.then_inc(S["av_ps"], 1)

                def use(h, u, chain):
                    n = count(h, u)
                    if not (isinstance(h, int) and h < 0 and u == OUT):
                        pe.wait_ge(S["g_done"], n)
                    if u == 0:
                        pe.wait_ge(S["cx_ready"], NT * chain)
                        for t in range(NT):
                            last = tr(Gb[:, t * P:(t + 1) * P], cx[:, t, :], g.ident[:, :])
                    elif u == 1:
                        pe.wait_ge(ow_loaded, 32 * chain)
                        last = mm(Gb[:, :], wkv[:, :], cxT[:, :], start=True, stop=True)
                    elif u < OUT:
                        t = u - 2
                        last = mm(Gb[:, :], lat[:, t * P:(t + 1) * P], wo[:, :], start=True, stop=True)
                    elif u == 6:
                        pe.wait_ge(qw_loaded, 64 * chain + 64)
                        for c in range(DC):
                            last = mm(Gb[:, :], wq[:, c, :], g.xT[:, c, :], start=(c == 0), stop=(c == DC - 1))
                    elif u < 13:
                        c, rot = (u - 7) // 2, (u - 7) % 2
                        c0 = (c * P + ROT * rot) % QB
                        last = mm(Gb[:, :], wkc[:, c0:c0 + P], qhk[:, :], start=True, stop=True)
                    elif u == 13:
                        pe.wait_ge(S["turned_ready"], QC * chain + QC)
                        for c in range(QC):
                            last = mm(Gb[0:R, :], wqr[:, c, :], qb[c][:, :], start=(c == 0), stop=(c == QC - 1))
                    else:
                        last = mm(Gb[:, :], wkr[:, :], qr[:, :], start=True, stop=True)
                    last.then_inc(S["g_ps"], 1)

                def first():
                    for u in range(OUT, 15):
                        use(-1, u, 0)
                    pe.wait_ge(S["g_done"], count(-1, 14) + 1)
                    scores(0, 0)

                def step(h, s, outs, qs):
                    if s + 1 < STEPS:
                        scores(h, s + 1)
                    transposes(h, s)
                    chain = h
                    for place in range(2):
                        if place == 1:
                            n = h * STEPS + (s - 1)
                            if not (isinstance(h, int) and h == 0 and s == 0):
                                weighted(h, (s - 1) % STEPS, n)
                        u = scheduled(s, place, outs, qs)
                        if u is not None:
                            use(h, u, chain if u < OUT else chain + 1)
                    if s + 1 == STEPS and qs:
                        pe.wait_ge(S["g_done"], count(h, 14) + 1)
                        scores(h + 1, 0)

                def last():
                    weighted(H - 1, STEPS - 1, H * STEPS - 1)
                    for u in range(OUT):
                        use(H, u, H)

                pe.wait_ge(tables, 32)
                heads(pe, first, step, last)

            @block.scalar
            def _(act):
                A_ = nc.scalar.activation

                def evacuate(h, u):
                    if u not in (0, 1, 6, 13, 14):
                        return
                    act.wait_ge(S["g_ps"], count(h, u) + 1)
                    if u == 14:
                        nc.scalar.copy(qh[:, :], Gb[:, :]).then_inc(S["q_hi"], 1)
                        return
                    dst, src = {0: (cxT[:, :], Gb[:, :]), 1: (lat[:, :], Gb[:, :]), 6: (qhk[:, :], Gb[:, :]),
                                13: (qr[:, :], Gb[0:R, :])}[u]
                    nc.scalar.copy(dst, src).then_inc(S["g_done"], 1)

                def exps(n, s):
                    act.wait_ge(S["nm_ready"], n + 1)
                    if not isinstance(n, int) or n >= 2:
                        act.wait_ge(S["t_ps"], 2 * n + (-2))
                    if s % NC:
                        A_(alpha[:, s:s + 1], nm[:, s - 1:s], ACT.Exp, scale=-1.0, bias=nm[:, s:s + 1])
                    A_(e[s % 2][:, :], SC[s % 2][:, :], ACT.Exp, bias=nm[:, s:s + 1],
                       accum_out=part[:, s:s + 1]).then_inc(S["e_ready"], 1)

                def first():
                    for u in range(OUT, 15):
                        evacuate(-1, u)
                    exps(0, 0)

                def step(h, s, outs, qs):
                    n = h * STEPS + s
                    if not isinstance(n, int) or n >= 2:
                        act.wait_ge(S["av_ps"], n + (-1))
                    for j in range(2):
                        act.wait_ge(S["t_ps"], 2 * n + (j + 1))
                        nc.scalar.copy(ph[s % 2][:, j * (KT // 2):(j + 1) * (KT // 2), :], T[j][:, :, :])\
                          .then_inc(S["hi_ready"], 1)
                    if s + 1 < STEPS:
                        exps(h * STEPS + (s + 1), s + 1)
                    elif qs:
                        exps(h * STEPS + STEPS, 0)
                    for place in range(2):
                        u = scheduled(s, place, outs, qs)
                        if u is not None and u != 14:
                            evacuate(h, u)
                    if s == STEPS - 2 and qs:
                        act.wait_ge(S["s_ps"], h * STEPS + STEPS)
                        evacuate(h, 14)

                def last():
                    for u in range(OUT):
                        evacuate(H, u)

                heads(act, first, step, last)

            @block.vector
            def _(dve):
                V = nc.vector

                def evacuate(h, u, chain):
                    if u in (0, 1, 6, 13):
                        return
                    dve.wait_ge(S["g_ps"], count(h, u) + 1)
                    if u < OUT:
                        t = u - 2
                        V.tensor_tensor(g.x[:, t, :], g.x[:, t, :], Gb[:, :], ALU.add).then_inc(S["g_done"], 1)
                    elif u < 13:
                        c, rot = (u - 7) // 2, (u - 7) % 2
                        dst = turned if rot else qb[c]
                        tab = sinq if rot else cosq
                        V.tensor_tensor(dst[:, :].rearrange("p (b s) -> p b s", b=BATCH),
                                        Gb[:, :].rearrange("p (b s) -> p b s", b=BATCH),
                                        tab[:, c, :].unsqueeze(1).broadcast_to((P, BATCH, SEQ)), ALU.mult)\
                         .then_inc(S["g_done"], 1)
                        if rot:
                            dve.wait_ge(S["g_done"], count(h, u) + 1)
                            V.tensor_tensor(qb[c][:, :], qb[c][:, :], turned[:, :], ALU.add)\
                             .then_inc(S["turned_ready"], 1)
                            dve.wait_ge(S["turned_ready"], QC * chain + c + 1)
                    else:
                        dve.wait_ge(S["q_hi"], chain + 1)
                        V.tensor_tensor(ql[:, :], Gb[:, :], qh[:, :].bitcast(F32), ALU.subtract)\
                         .then_inc(S["g_done"], 1)

                def maxima(n, s):
                    dve.wait_ge(S["s_ps"], n + 1)
                    if s % NC:
                        V.tensor_reduce(nmc[:, s:s + 1], SC[s % 2][:, :], AX.X, ALU.max, negate=True)\
                         .then_inc(S["chunk_max"], 1)
                        dve.wait_ge(S["chunk_max"], n + 1)
                        V.tensor_tensor(nm[:, s:s + 1], nmc[:, s:s + 1], nm[:, s - 1:s], ALU.min)\
                         .then_inc(S["nm_ready"], 1)
                        dve.wait_ge(S["nm_ready"], n + 1)
                    else:
                        V.tensor_reduce(nm[:, s:s + 1], SC[s % 2][:, :], AX.X, ALU.max, negate=True)\
                         .then_inc(S["nm_ready"], 1)
                        dve.sem_inc(S["chunk_max"], 1)

                def accumulate(n, s):
                    dve.wait_ge(S["av_ps"], n + 1)
                    t, c = s // NC, s % NC
                    a = acc[t % 2]
                    if c:
                        V.scalar_tensor_tensor(out=a[:, :], in0=a[:, :], scalar=alpha[:, s:s + 1], in1=AV[:, 0:DL],
                                               op0=ALU.mult, op1=ALU.add).then_inc(S["acc_scaled"], 1)
                        V.scalar_tensor_tensor(out=total[:, s:s + 1], in0=total[:, s - 1:s],
                                               scalar=alpha[:, s:s + 1], in1=part[:, s:s + 1],
                                               op0=ALU.mult, op1=ALU.add).then_inc(S["total_ready"], 1)
                    else:
                        V.tensor_copy(a[:, :], AV[:, 0:DL]).then_inc(S["acc_scaled"], 1)
                        V.tensor_copy(total[:, s:s + 1], part[:, s:s + 1]).then_inc(S["total_ready"], 1)
                    dve.wait_ge(S["acc_scaled"], n + 1)
                    V.tensor_tensor(a[:, :], a[:, :], AV[:, DL:2 * DL], ALU.add).then_inc(S["acc_done"], 1)
                    dve.wait_ge(S["total_ready"], n + 1)
                    dve.wait_ge(S["acc_done"], n + 1)

                def finish(t, done):
                    s = t * NC + NC - 1
                    V.reciprocal(rtotal[:, t:t + 1], total[:, s:s + 1]).then_inc(S["inverted"], 1)
                    dve.wait_ge(S["inverted"], done + 1)
                    V.tensor_scalar(cx[:, t, :], acc[t % 2][:, :], rtotal[:, t:t + 1], None, ALU.mult)\
                     .then_inc(S["cx_ready"], 1)
                    dve.wait_ge(S["cx_ready"], done + 1)

                def first():
                    dve.wait_ge(tables, 32)
                    for u in range(OUT, 15):
                        evacuate(-1, u, 0)
                    maxima(0, 0)

                def step(h, s, outs, qs):
                    n = h * STEPS + s
                    if s + 1 < STEPS:
                        maxima(h * STEPS + (s + 1), s + 1)
                    elif qs:
                        maxima(h * STEPS + STEPS, 0)
                    if not isinstance(n, int) or n >= 2:
                        dve.wait_ge(S["av_ps"], n + (-1))
                    for j in range(2):
                        dve.wait_ge(S["hi_ready"], 2 * n + (j + 1))
                        half = slice(j * (KT // 2), (j + 1) * (KT // 2))
                        V.tensor_tensor(pl[s % 2][:, half, :], T[j][:, :, :], ph[s % 2][:, half, :].bitcast(F32),
                                        ALU.subtract).then_inc(S["lo_ready"], 1)
                    for place in range(2):
                        u = scheduled(s, place, outs, qs)
                        if place == 1 and not (isinstance(n, int) and n == 0):
                            accumulate(n + (-1), (s - 1) % STEPS)
                            if s % NC == 0 and s:
                                finish(s // NC - 1, h * NT + (s // NC - 1))
                            elif s == 0:
                                finish(NT - 1, h * NT + (-1))
                        if u is not None and u != 14:
                            evacuate(h, u, h + 1)
                    if s == STEPS - 2 and qs:
                        evacuate(h, 14, h + 1)

                def last():
                    accumulate(H * STEPS - 1, STEPS - 1)
                    finish(NT - 1, H * NT - 1)
                    for u in range(OUT):
                        evacuate(H, u, 0)

                heads(dve, first, step, last)


def out_stage(nc, g, src):
    with ExitStack() as ctx:
        m = Mem(nc, ctx, "out")
        stored = m.sem("stored")
        block = ctx.enter_context(nc.Block())

        @block.sync
        def _(sp):
            sp.dma_start(g.out_dram.rearrange("(t p) d -> p t d", p=P), src[:, :, :]).then_inc(stored, 16)
            sp.wait_ge(stored, 16)


class Globals:
    pass


def build(nc, dram):
    g = Globals()
    g.x_dram = dram["x"]
    g.out_dram = dram["out"]
    with ExitStack() as ctx:
        m = Mem(nc, ctx, "g")
        g.x = m.sb("x", [P, NT, D])
        g.xn = m.sb("xn", [P, NT, D])
        g.xT = m.sb("xT", [P, DC, TOK])
        g.ident = m.sb("ident", [P, P])
        g.ones = m.sb("ones", [P, P])
        g.triu = m.sb("triu", [P, P])
        g.half = m.sb("half", [P, 16])
        g.psum = ctx.enter_context(nc.psum_tensor("psum", [P, 8 * D], F32))
        g.bank = [g.psum[:, i * D:(i + 1) * D] for i in range(8)]
        constants_stage(nc, g)

        norm_stage(nc, g, "n1", 1e-5)
        with ExitStack() as c2:
            kv = Mem(nc, c2, "kv0").sb("ctxT", [P, 1, TOK])
            attention_stage(nc, g, "l0x", dram["L0_xattn_Wq"], dram["L0_xattn_Wkv"][:, 0:D],
                            dram["L0_xattn_Wkv"][:, D:2 * D], dram["L0_xattn_Wout"], kv, dram["ctxT"], None, FMIN)
        norm_stage(nc, g, "n2", 1e-5)
        delta_stage(nc, g, dram)
        norm_stage(nc, g, "n3", 1e-5)
        expert_stage(nc, g, dram)

        norm_stage(nc, g, "n4", 1e-5)
        latent_attention_stage(nc, g, dram)
        with ExitStack() as c2:
            ffn_weights = FfnWeights(Mem(nc, c2, "ffnw"), dram)
            norm_stage(nc, g, "n5", 1e-5)
            w = dram["L1_attn_Wqkv"]
            attention_stage(nc, g, "l1a", w[:, 0:D], w[:, D:2 * D], w[:, 2 * D:3 * D], dram["L1_attn_Wo"],
                            g.xT, None, (dram["L1_attn_bqkv"], dram["L1_attn_bqk_cols"], dram["L1_attn_bo"]), -10000.0,
                            ffn_weights.load)
            norm_stage(nc, g, "n6", 1e-5, transpose=False)
            ternary_stage(nc, g, dram, ffn_weights)
        out_stage(nc, g, g.x)


def rope_tables(length, dim):
    f32 = np.float32
    inv = f32(1.0) / np.power(f32(10000.0), np.arange(0, dim, 2, dtype=f32) / f32(dim)).astype(f32)
    angle = np.arange(length, dtype=f32)[:, None] * inv[None, :].astype(f32)
    sin, cos = np.repeat(np.sin(angle), 2, axis=-1), np.repeat(np.cos(angle), 2, axis=-1)
    sin[:, 0:dim // 2] *= f32(-1.0)
    return sin, cos


def layouts(inputs):
    a = {k: np.asarray(v) for k, v in inputs.items()}
    o = {"x": a["x"].reshape(TOK, D)}
    o["ctxT"] = a["ctx_512"].transpose(0, 2, 1)
    o["L0_xattn_Wq"] = a["L0_xattn_Wq"].T
    o["L0_xattn_Wkv"] = a["L0_xattn_Wkv_expand"].T
    o["L0_xattn_Wout"] = a["L0_xattn_Wout"].T
    parts = [a["L0_attn_W_qkv"][:, n * 2048:(n + 1) * 2048] for n in range(3)] + [a["L0_attn_W_z"]]
    o["L0_attn_W_heads"] = np.stack([p.reshape(D, 16, P) for p in parts], 2).transpose(1, 0, 2, 3).reshape(16 * D, 4 * P)
    o["L0_attn_W_ab"] = np.concatenate([a["L0_attn_W_b"], a["L0_attn_W_a"]], 1)
    o["L0_attn_W_out"] = a["L0_attn_W_out"]
    o["L0_attn_conv"] = a["L0_attn_conv_w"].reshape(3, 16, P, 4).transpose(2, 1, 0, 3).reshape(P, 16 * 12)
    for n in ("A_log", "dt_bias", "norm_w"):
        o["L0_attn_" + n] = a["L0_attn_" + n]
    o["L0_ffn_router"] = a["L0_ffn_router_w"].T
    gu = np.concatenate([a["L0_ffn_w_gate"], a["L0_ffn_w_up"]], 2)
    o["L0_ffn_gate_up"] = gu.reshape(64, DC, P, 384).transpose(0, 2, 1, 3).reshape(64 * P, DC * 384)
    o["L0_ffn_w_down"] = a["L0_ffn_w_down"].reshape(64, 2, 96, D).transpose(0, 2, 1, 3).reshape(64 * 96, 2 * D)
    o["L1_ffn_up"] = a["L1_ffn_weight_up"].T
    o["L1_ffn_down"] = a["L1_ffn_weight_down"].T
    o["L1_ffn_norm_weight"] = a["L1_ffn_norm_weight"]
    o["L1_ffn_gamma"] = a["L1_ffn_gamma"]
    o["ctx"] = a["ctx_512"]
    o["L1_xattn_Wq"] = a["L1_xattn_Wq"].reshape(16, P, DC, P).transpose(0, 3, 2, 1).reshape(16 * P, DC * P)
    wkc = a["L1_xattn_w_kc_q"].reshape(16 * P, 384)
    o["L1_xattn_w_kc_q"] = np.concatenate([wkc, wkc[:, 0:192]], 1)
    o["L1_xattn_W_qr"] = a["L1_xattn_W_qr"].reshape(16, 3, P, 64).transpose(0, 2, 1, 3).reshape(16 * P, 3 * 64)
    o["L1_xattn_W_kr"] = a["L1_xattn_W_kr"].transpose(0, 2, 1).reshape(16 * 64, P)
    o["L1_xattn_w_kc_kv"] = a["L1_xattn_w_kc_kv"].transpose(0, 2, 1).reshape(16 * P, P)
    o["L1_xattn_Wo"] = a["L1_xattn_Wo"].T
    o["sin_k"], o["cos_k"] = (np.ascontiguousarray(t[:, 0::2]) for t in rope_tables(4096, P))
    sin_q, cos_q = rope_tables(SEQ, 384)
    o["sin_q"], o["cos_q"] = sin_q.T, cos_q.T
    o["L1_attn_Wqkv"] = a["L1_attn_Wqkv"]
    o["L1_attn_bqkv"] = a["L1_attn_bqkv"]
    o["L1_attn_bqk_cols"] = a["L1_attn_bqkv"][0:2 * D].reshape(2 * DC, P).T
    o["L1_attn_Wo"] = a["L1_attn_Wo"]
    o["L1_attn_bo"] = a["L1_attn_bo"]
    return o


def kernel(**inputs):
    import concourse.bacc as bacc
    from concourse.bass_utils import run_bass_kernel_spmd

    nc = bacc.Bacc("TRN2", target_bir_lowering=False, num_devices=1)
    arrays, dram = {}, {}
    for name, a in layouts(inputs).items():
        a = np.ascontiguousarray(a)
        arrays[f"in_{name}"] = a
        dram[name] = nc.dram_tensor(f"in_{name}", a.shape, mybir.dt.from_np(a.dtype), kind="ExternalInput").ap()
    dram["out"] = nc.dram_tensor("out_0", (TOK, D), F32, kind="ExternalOutput").ap()
    dram["xn_rows"] = nc.dram_tensor("xn_rows", (TOK, D), F32, kind="Internal").ap()
    dram["y_rows"] = nc.dram_tensor("y_rows", (64 * 128 + 1, D), F32, kind="Internal").ap()
    build(nc, dram)
    r = run_bass_kernel_spmd(nc, [arrays], core_ids=[0])
    return r.results[0]["out_0"].reshape(BATCH, SEQ, D)
```
